# Optimizing a Trainium2 kernel written in Bass

```python
import numpy as np
import jax
import jax.numpy as jnp

def _softmax(x, axis=-1):
    return jax.nn.softmax(x, axis=axis)

def _gelu(x):
    return jax.nn.gelu(x, approximate=True)

def _silu(x):
    return jax.nn.silu(x)

def _sigmoid(x):
    return jax.nn.sigmoid(x)

def _layernorm(x, axis=-1, eps=1e-05):
    m = jnp.mean(x, axis=axis, keepdims=True)
    v = jnp.var(x, axis=axis, keepdims=True)
    return (x - m) / jnp.sqrt(v + eps)

def _scatter_add(tgt, idx, src, axis=0):
    return tgt.at[idx].add(src)

def _segment_sum(src, seg, n):
    return jax.ops.segment_sum(src, seg, n)
kernel_name = 'mk_decoder_preln_d1_seqx_r4_956c87'

def setup_inputs(seed: int=0):
    np.random.seed(seed)
    _w = jnp.asarray

    def _rec_inputs():
        import jax
        import jax.numpy as jnp
        _rk = jax.random.key(seed)
        x = -0.0002928 + 1 * jax.random.normal(jax.random.fold_in(_rk, 1), (32, 112, 256), jnp.float32)
        _lenS = 112 - jax.random.randint(jax.random.fold_in(_rk, 7), (32,), 0, max(1, 112 // 4) + 1, jnp.int32)
        _lenS2 = 375 - jax.random.randint(jax.random.fold_in(_rk, 8), (32,), 0, max(1, 375 // 4) + 1, jnp.int32)
        _ctx_1024P = jax.random.normal(jax.random.fold_in(_rk, 11), (32, 16, 256), jnp.float32)
        _ctx_1024c = jax.random.dirichlet(jax.random.fold_in(_rk, 511), 0.3 * jnp.ones((16,), jnp.float32), (32, 375))
        _ctx_1024t = jnp.einsum('bsk,bkd->bsd', _ctx_1024c, _ctx_1024P)
        _ctx_1024t = _ctx_1024t * jax.lax.rsqrt(jnp.mean(jnp.square(_ctx_1024t)) + 1e-12) * 0.953939
        ctx_1024 = 2.81802e-05 + 1.00001 * (_ctx_1024t + 0.3 * jax.random.normal(jax.random.fold_in(_rk, 611), (32, 375, 256), jnp.float32))
        _validS = jnp.arange(112)[None, :] < _lenS[:, None]
        _validS2 = jnp.arange(375)[None, :] < _lenS2[:, None]
        _causal = jnp.tril(jnp.ones((112, 112), dtype=bool))
        mask_BxS2_bk0 = jnp.logical_not(jnp.broadcast_to(_validS2[:, :], (32, 375)))
        return (x, ctx_1024, mask_BxS2_bk0)
    x, ctx_1024, mask_BxS2_bk0 = _rec_inputs()

    def _L0_attn_setup():
        import jax, jax.numpy as jnp
        import numpy as np
        NUM_HEADS = 16
        key = jax.random.key(seed)
        kx, kq, kk, kv = jax.random.split(key, 4)
        N, S, D = (2, 1024, 256)
        scale = 1.0 / np.sqrt(D)
        x = jax.random.normal(kx, (N, S, D), dtype=jnp.float32)
        Wq = jax.random.normal(kq, (D, D), dtype=jnp.float32) * scale
        Wk = jax.random.normal(kk, (D, D), dtype=jnp.float32) * scale
        Wv = jax.random.normal(kv, (D, D), dtype=jnp.float32) * scale
        return {'x': x, 'Wq': Wq, 'Wk': Wk, 'Wv': Wv}
    _L0_attn_all = _L0_attn_setup()
    _L0_attn_in = {k: v for k, v in _L0_attn_all.items() if k in ('Wq', 'Wk', 'Wv')}
    del _L0_attn_all

    def _L0_xattn_setup():
        import jax, jax.numpy as jnp
        import numpy as np
        NUM_HEADS, NUM_KV, HEAD_DIM, WIDTH = (4, 1, 64, 256)
        MASK_FILL = -2.3819763e+38

        def _apply_rope(x, positions, max_wavelength=10000.0):
            d = x.shape[-1]
            freq_exp = 2.0 / d * jnp.arange(d // 2, dtype=jnp.float32)
            timescale = max_wavelength ** freq_exp
            radians = positions[..., None].astype(jnp.float32) / timescale
            radians = radians[..., None, :]
            sin, cos = (jnp.sin(radians), jnp.cos(radians))
            x1, x2 = jnp.split(x, 2, axis=-1)
            out = jnp.concatenate([x1 * cos - x2 * sin, x2 * cos + x1 * sin], axis=-1)
            return out.astype(x.dtype)

        def _rmsnorm(x, scale):
            var = jnp.mean(jnp.square(x.astype(jnp.float32)), axis=-1, keepdims=True)
            normed = x * jax.lax.rsqrt(var + 1e-06)
            return (normed * (1 + scale)).astype(x.dtype)
        key = jax.random.key(seed)
        ks = jax.random.split(key, 7)
        B, T, S = (8, 128, 512)
        return {'x': jax.random.normal(ks[0], (B, T, WIDTH), jnp.float32), 'mem_seq': jax.random.normal(ks[1], (B, S, WIDTH), jnp.float32), 'mem_mask': jax.random.randint(ks[2], (B, S), 0, 2).astype(bool), 'rms_scale': jax.random.normal(ks[3], (WIDTH,), jnp.float32) * 0.02, 'q_w': jax.random.normal(ks[4], (NUM_HEADS, WIDTH, HEAD_DIM), jnp.float32) / np.sqrt(WIDTH), 'kv_w': jax.random.normal(ks[5], (2, NUM_KV, WIDTH, HEAD_DIM), jnp.float32) / np.sqrt(WIDTH), 'out_w': jax.random.normal(ks[6], (NUM_HEADS, HEAD_DIM, WIDTH), jnp.float32) / np.sqrt(NUM_HEADS * HEAD_DIM)}
    _L0_xattn_all = _L0_xattn_setup()
    _L0_xattn_in = {k: v for k, v in _L0_xattn_all.items() if k in ('rms_scale', 'q_w', 'kv_w', 'out_w')}
    del _L0_xattn_all

    def _L0_ffn_setup():
        import jax, jax.numpy as jnp
        import numpy as np
        E, D, F, GATE_DIM = (8, 256, 1024, 16)
        B, T = (2, 512)
        key = jax.random.key(seed)
        ks = jax.random.split(key, 7)
        s = 0.02
        return {'hidden_states': jax.random.normal(ks[0], (B, T, D), dtype=jnp.float32), 'w_red': jax.random.normal(ks[1], (D, GATE_DIM), dtype=jnp.float32) * s, 'wg': jax.random.normal(ks[2], (E, GATE_DIM), dtype=jnp.float32), 'w1': jax.random.normal(ks[3], (E, D, F), dtype=jnp.float32) * s, 'b1': jax.random.normal(ks[4], (E, F), dtype=jnp.float32) * s, 'w2': jax.random.normal(ks[5], (E, F, D), dtype=jnp.float32) * s, 'b2': jax.random.normal(ks[6], (E, D), dtype=jnp.float32) * s}
    _L0_ffn_all = _L0_ffn_setup()
    _L0_ffn_in = {k: v for k, v in _L0_ffn_all.items() if k in ('w_red', 'wg', 'w1', 'b1', 'w2', 'b2')}
    del _L0_ffn_all
    return {'x': x, 'ctx_1024': ctx_1024, 'mask_BxS2_bk0': mask_BxS2_bk0, 'L0_attn_Wq': _L0_attn_in['Wq'], 'L0_attn_Wk': _L0_attn_in['Wk'], 'L0_attn_Wv': _L0_attn_in['Wv'], 'L0_xattn_rms_scale': _L0_xattn_in['rms_scale'], 'L0_xattn_q_w': _L0_xattn_in['q_w'], 'L0_xattn_kv_w': _L0_xattn_in['kv_w'], 'L0_xattn_out_w': _L0_xattn_in['out_w'], 'L0_ffn_w_red': _L0_ffn_in['w_red'], 'L0_ffn_wg': _L0_ffn_in['wg'], 'L0_ffn_w1': _L0_ffn_in['w1'], 'L0_ffn_b1': _L0_ffn_in['b1'], 'L0_ffn_w2': _L0_ffn_in['w2'], 'L0_ffn_b2': _L0_ffn_in['b2']}

def reference(x, ctx_1024, mask_BxS2_bk0, L0_attn_Wq, L0_attn_Wk, L0_attn_Wv, L0_xattn_rms_scale, L0_xattn_q_w, L0_xattn_kv_w, L0_xattn_out_w, L0_ffn_w_red, L0_ffn_wg, L0_ffn_w1, L0_ffn_b1, L0_ffn_w2, L0_ffn_b2):
    import jax
    import jax.numpy as jnp

    def _L0_attn_ref(x, Wq, Wk, Wv):
        import jax, jax.numpy as jnp
        import numpy as np
        NUM_HEADS = 16
        N, S, D = x.shape
        H = NUM_HEADS
        hd = D // H
        q = (x @ Wq.T).reshape(N, S, H, hd).transpose(0, 2, 1, 3)
        k = (x @ Wk.T).reshape(N, S, H, hd).transpose(0, 2, 1, 3)
        v = (x @ Wv.T).reshape(N, S, H, hd).transpose(0, 2, 1, 3)
        energy = jnp.einsum('nhqd,nhkd->nhqk', q, k)
        attn = jax.nn.softmax(energy / jnp.sqrt(jnp.float32(hd)), axis=3)
        out = jnp.einsum('nhql,nhld->nhqd', attn, v)
        return out.transpose(0, 2, 1, 3).reshape(N, S, D)

    def _L0_xattn_ref(x, mem_seq, mem_mask, rms_scale, q_w, kv_w, out_w):
        import jax, jax.numpy as jnp
        import numpy as np
        NUM_HEADS, NUM_KV, HEAD_DIM, WIDTH = (4, 1, 64, 256)
        MASK_FILL = -2.3819763e+38

        def _apply_rope(x, positions, max_wavelength=10000.0):
            d = x.shape[-1]
            freq_exp = 2.0 / d * jnp.arange(d // 2, dtype=jnp.float32)
            timescale = max_wavelength ** freq_exp
            radians = positions[..., None].astype(jnp.float32) / timescale
            radians = radians[..., None, :]
            sin, cos = (jnp.sin(radians), jnp.cos(radians))
            x1, x2 = jnp.split(x, 2, axis=-1)
            out = jnp.concatenate([x1 * cos - x2 * sin, x2 * cos + x1 * sin], axis=-1)
            return out.astype(x.dtype)

        def _rmsnorm(x, scale):
            var = jnp.mean(jnp.square(x.astype(jnp.float32)), axis=-1, keepdims=True)
            normed = x * jax.lax.rsqrt(var + 1e-06)
            return (normed * (1 + scale)).astype(x.dtype)
        B, S, _ = mem_seq.shape
        T = x.shape[1]
        G = NUM_HEADS // NUM_KV
        xn = _rmsnorm(x, rms_scale)
        mn = _rmsnorm(mem_seq, rms_scale)
        q = jnp.einsum('BTD,NDH->BTNH', xn, q_w)
        kv = jnp.einsum('BSD,cKDH->cBSKH', mn, kv_w)
        k, v = (kv[0], kv[1])
        q_pos = jnp.broadcast_to(jnp.arange(S, T + S), (B, T))
        k_pos = jnp.broadcast_to(jnp.arange(S), (B, S))
        q = _apply_rope(q, q_pos) * HEAD_DIM ** (-0.5)
        k = _apply_rope(k, k_pos)
        q = q.reshape(B, T, NUM_KV, G, HEAD_DIM)
        logits = jnp.einsum('BTKGH,BSKH->BKGTS', q, k, preferred_element_type=jnp.float32)
        masked = jnp.where(mem_mask[:, None, None, None, :], logits, MASK_FILL)
        probs = jax.nn.softmax(masked, axis=-1).astype(x.dtype)
        enc = jnp.einsum('BKGTS,BSKH->BTKGH', probs, v).reshape(B, T, NUM_HEADS, HEAD_DIM)
        return jnp.einsum('BTNH,NHD->BTD', enc, out_w)

    def _L0_ffn_ref(hidden_states, w_red, wg, w1, b1, w2, b2):
        import jax, jax.numpy as jnp
        import numpy as np
        E, D, F, GATE_DIM = (8, 256, 1024, 16)
        B, T = (2, 512)
        b, t, c = hidden_states.shape
        x = hidden_states.reshape(-1, c)
        red = x @ w_red
        wg_n = wg / jnp.maximum(jnp.linalg.norm(wg, axis=1, keepdims=True), 0.0001)
        logits = red @ wg_n.T
        gates = jax.nn.softmax(logits, axis=1)
        idx = jnp.argmax(gates, axis=1)
        scores = jnp.take_along_axis(gates, idx[:, None], axis=1)
        h = jax.nn.gelu(jnp.einsum('td,edf->etf', x, w1) + b1[:, None, :], approximate=False)
        y = jnp.einsum('etf,efd->etd', h, w2) + b2[:, None, :]
        out = jnp.take_along_axis(y, idx[None, :, None], axis=0)[0]
        out = out * scores
        return out.reshape(b, t, c)
    x = x + _L0_attn_ref(_layernorm(x, axis=-1), L0_attn_Wq, L0_attn_Wk, L0_attn_Wv)
    x = x + _L0_xattn_ref(_layernorm(x, axis=-1), ctx_1024, mask_BxS2_bk0, L0_xattn_rms_scale, L0_xattn_q_w, L0_xattn_kv_w, L0_xattn_out_w)
    x = x + _L0_ffn_ref(_layernorm(x, axis=-1), L0_ffn_w_red, L0_ffn_wg, L0_ffn_w1, L0_ffn_b1, L0_ffn_w2, L0_ffn_b2)
    return x

_drawn_inputs = setup_inputs


def setup_inputs(seed=0):
    import zlib

    import numpy as np

    out = dict(_drawn_inputs(seed))
    spreads = {}
    factors = {'L0_xattn_rms_scale': 5.549,
     'L0_ffn_w_red': 3.253,
     'L0_ffn_wg': 3.26,
     'L0_ffn_w1': 3.178,
     'L0_ffn_b1': 8.0,
     'L0_ffn_w2': 3.086,
     'L0_ffn_b2': 8.0}
    for name, (base, spread) in spreads.items():
        noise = np.random.default_rng([zlib.crc32(name.encode()), seed]).standard_normal(out[name].shape)
        drawn = base * np.exp(spread * noise) if base else spread * noise
        out[name] = jnp.asarray(drawn.astype(out[name].dtype))
    for name, factor in factors.items():
        out[name] = (out[name] * factor).astype(out[name].dtype)
    return out
```

```python
from contextlib import ExitStack

import numpy as np

import concourse.bass as bass
from concourse import mybir

F32 = mybir.dt.float32
BF16 = mybir.dt.bfloat16
I32 = mybir.dt.int32
U8 = mybir.dt.uint8
ALU = mybir.AluOpType
ACT = mybir.ActivationFunctionType
AX = mybir.AxisListType

P = 128
B, T, D = 32, 112, 256
S = 375
KT, KP = 3, 125
KC = D // P
H, HD = 16, 16
HC = P // HD
G, GD = 4, 64
E, F = 8, 1024
FC = F // P
NB = 512
TILES = B * T // P + E - 1
BIG = 2.0 ** 100
ARENA = 9600
LATE = 3
R = GD + 1


def constants():
    half = GD // 2
    timescale = (np.float32(10000.0) ** (np.float32(2.0 / GD) * np.arange(half, dtype=np.float32))).astype(np.float32)
    def table(pos):
        rad = (pos.astype(np.float32)[:, None] / timescale[None, :]).astype(np.float32)
        s, c = np.sin(rad).astype(np.float32), np.cos(rad).astype(np.float32)
        return np.concatenate([c, c, -s, s], 1)
    ropeq = table(np.arange(S, S + T))
    ropek = table(np.arange(S)).reshape(KT, KP, 4 * half).transpose(1, 0, 2)
    p = np.arange(P)
    f = lambda a: np.ascontiguousarray(a, dtype=np.float32)
    misc = np.zeros((P, 8 + 8 + 28 + 256 + 8 + 36 + 112), np.float32)
    misc[:, 0:8] = p[:, None] // HD == np.arange(HC)[None]
    misc[:, 8:16] = np.arange(E)[None] - E
    misc[:, 16:44] = P * np.arange(28)[None]
    misc[:, 44:300] = (np.arange(256) % B != 0)[None]
    misc[:, 300:308] = (np.arange(E) != 0)[None]
    misc[:, 308:344] = np.arange(36)[None]
    misc[:T, 344:456] = (np.arange(T)[:, None] < np.arange(T)[None])
    pick = np.zeros((P, E, P), np.float32)
    for e in range(E):
        pick[3 * e:3 * e + 3, e] = 1.0
    return {"ropeq": f(ropeq), "ropek": f(ropek), "misc": f(misc), "pick": f(pick), "ident": f(np.eye(P))}


def decoder(nc, a, out):
    with ExitStack() as ctx:
        def sb(name, shape, dt=F32):
            return ctx.enter_context(nc.sbuf_tensor(name, shape, dt))

        def psum(name, shape, dt=F32):
            return ctx.enter_context(nc.psum_tensor(name, shape, dt))

        def sem(name):
            return ctx.enter_context(nc.semaphore(name))

        sorted_x = nc.dram_tensor("sorted_x", [TILES * P, D], F32, kind="Internal").ap()
        sorted_y = nc.dram_tensor("sorted_y", [TILES * P, D], F32, kind="Internal").ap()

        x = sb("x", [T, B, D])
        w1 = sb("w1", [P, E, KC, F])
        w2 = sb("w2", [P, E, FC, D])
        ident = sb("ident", [P, P])
        misc = sb("misc", [P, 456])
        head_of = misc[:, 0:8]
        logits = sb("logits", [T, B, E])
        mean_rstd3 = sb("mean_rstd3", [T, B, 2])
        bias_rows = sb("bias_rows", [P, F + D], BF16)
        pick = sb("pick", [P, E, P], BF16)
        small = sb("small", [P, 64])
        ones = sb("ones", [P, P], BF16)
        neghalf = sb("neghalf", [P, KT])
        score = sb("score", [T, B])
        tri = sb("tri", [T, T], BF16)
        ones_f = sb("ones_f", [T, E])
        slot_i = sb("slot_i", [T, B], I32)
        ysb = sb("ysb", [P, D])
        arena = sb("arena", [P, ARENA])
        used = [0]

        def carve(rows, shape, dt=F32):
            n = int(np.prod(shape))
            words = (n * (1 if dt == U8 else 2 if dt == BF16 else 4) + 3) // 4
            v = arena[0:rows, used[0]:used[0] + words]
            used[0] += words
            assert used[0] <= ARENA, used
            if dt != F32:
                v = v.bitcast(dt)[:, 0:n]
            names = "abc"[0:len(shape)]
            if len(shape) == 1:
                return v
            return v.rearrange("p (" + " ".join(names) + ") -> p " + " ".join(names),
                               **{k: s for k, s in zip(names, shape)})

        wkv = carve(P, [KC, 2 * GD])
        wred = carve(P, [KC, HD])
        wgT = carve(HD, [E])
        ropeq = carve(T, [2 * GD])
        ropek = carve(KP, [KT, 2 * GD])
        xn = carve(T, [D])
        xnT = carve(P, [KC, T])
        kT = carve(P, [KC, T])
        v1 = carve(T, [H, HD + 1])
        kxT = carve(R, [S])
        qxT = carve(R, [G * T])
        vx = carve(KP, [KT, R])
        mask_row = carve(R, [S], U8)
        nm = carve(T, [H])
        nmx = carve(T, [G])
        ctxn = carve(KP, [KT, D])
        xn2 = carve(T, [D])
        xn2T = carve(P, [KC, T])
        xn3 = carve(T, [D])
        xn3T = carve(P, [KC, T])
        tmp1 = carve(T, [D])
        ropea = carve(T, [D])
        ropeb = carve(T, [D])
        qrot = carve(T, [D])
        kraw = carve(KP, [KT, GD])
        kra = carve(KP, [KT, GD])
        krb = carve(KP, [KT, GD])
        krot = carve(KP, [KT, GD])
        enc = carve(T, [D])
        encT = carve(P, [KC, T])
        redT = carve(HD, [T])
        stats = carve(T, [3, 6])
        mv = carve(T, [3, 2])
        rs = carve(T, [3, 2])
        ss = carve(KP, [KT])
        ssm = carve(KP, [KT])
        rc = carve(KP, [KT])
        den = carve(T, [H])
        denx = carve(T, [G])
        late = [w1[:, E - LATE:E, :, :].rearrange("p e k f -> p (e k f)"),
                w2[:, E - LATE:E, :, :].rearrange("p e k f -> p (e k f)")]
        taken = [0, 0]

        def over(where, rows, n):
            v = late[where][0:rows, taken[where]:taken[where] + n]
            taken[where] += n
            assert taken[where] <= LATE * KC * F
            return v

        qexp = [over(0, P, HC * T).rearrange("p (h t) -> p h t", h=HC) for _ in range(KC)]
        prob = over(0, T, H * T).rearrange("p (h t) -> p h t", h=H)
        neg_diag = over(1, T, H * T // 2).bitcast(BF16).rearrange("p (h t) -> p h t", h=H)
        probx = over(1, KP, KT * G * T).rearrange("p (k n) -> p k n", k=KT)
        neg_diagx = over(1, T, G * T // 2).bitcast(BF16)
        ctxT = over(1, P, KC * S).rearrange("p (k s) -> p k s", k=KC)
        square = over(1, KP, D)
        wqk, wv, wxq, wo = (over(0, P, KC * n).rearrange("p (c n) -> p c n", c=KC) for n in (2 * D, D, D, D))
        used[0] = 0
        gmax = carve(T, [B])
        gdiff = carve(T, [B, E])
        gexp = carve(T, [B, E])
        gsum = carve(T, [B])
        cand = carve(T, [B, E])
        best = carve(T, [B])
        onehot = carve(T, [B, E])
        onehot_b = carve(T, [E, B], BF16)
        totals = carve(T, [E * B])
        running = carve(T, [E * B])
        place = carve(T, [E, B])
        over_t = carve(T, [E, 28])
        tiles_e = carve(T, [E])
        ends = carve(T, [E])
        starts = carve(T, [E])
        slot = carve(T, [B])
        past = carve(1, [36, E])
        tile_e = carve(1, [36])
        tile_e_i = carve(1, [36], I32)
        xs3 = [carve(T, [D]) for n in range(4)]
        hid = carve(P, [F])
        shared = used[0]
        b3 = carve(E, [3, F + D], BF16)
        braw2 = carve(E, [F + D])
        braw3 = carve(E, [F + D])
        used[0] = shared
        xs = carve(P, [D])
        xsT = carve(P, [KC, P])
        hidT = carve(P, [FC, P])
        NY = 4
        yg = [carve(T, [D]) for n in range(NY)]

        bank = [psum(f"bank{n}", [P, NB]) for n in range(4, 8)]
        b4, b5, b6, b7 = bank
        U = [psum(f"pair{n}", [P, 2, NB]) for n in range(2)]
        xT_ps = b4[:, 0:KC * T].rearrange("p (k t) -> p k t", k=KC)
        q_ps = b4[0:T, 0:D]
        pvx_ps = b4[0:T, 0:G * R].rearrange("p (g r) -> p g r", g=G)
        x2T_ps = b5[:, 0:KC * T].rearrange("p (k t) -> p k t", k=KC)
        qxT_ps = b5[0:GD, 0:G * T]
        kv_ps = b5[0:KP, 0:KT * 2 * GD].rearrange("p (k n) -> p k n", k=KT)
        kxT_ps = b5[0:GD, 0:S]
        qk_ps = b6[:, 0:4 * T].rearrange("p (k t) -> p k t", k=4)
        pv_ps = b6[0:T, 0:H * (HD + 1)].rearrange("p (h r) -> p h r", h=H)
        encT_ps = b6[:, 0:KC * T].rearrange("p (k t) -> p k t", k=KC)
        v_ps = b7[0:T, 0:D]
        x3T_ps = b7[:, 0:KC * T].rearrange("p (k t) -> p k t", k=KC)
        redT_ps = b7[0:HD, 0:T]
        logit_ps = b7[0:T, 0:E]
        out_ps = b7[0:T, 0:D]

        S_ = {}

        def s(name):
            if name not in S_:
                S_[name] = sem(name)
            return S_[name]

        names = ["ld_const", "ld_w", "ld_x", "ld_ctxn", "ld_ctxT", "ld_mask", "ld_early", "ld_late", "zero_ready", "zero_sent",
                 "ones_ready", "weights_ready", "setup_dve", "setup_pe", "setup_pool", "setup_act",
                 "pe_xT", "pe_x2T", "pe_qk", "pe_v", "pe_q", "pe_smax", "pe_qT", "pe_xmax", "pe_sexp", "pe_x3T",
                 "pe_xexp", "pe_red", "pe_pv", "pe_logit", "pe_xpv", "pe_kv", "pe_encT", "pe_kT", "pe_out",
                 "act_xT", "act_x2T", "act_kT", "act_v", "act_qT", "act_sexp", "act_x3T", "act_xexp", "act_red",
                 "act_sq", "act_kxT", "act_encT",
                 "dve_qexp", "dve_rope", "dve_x3", "dve_smax", "dve_xmax", "dve_x1", "dve_bn2", "dve_bn1", "dve_bn3",
                 "dve_st2", "dve_st1", "dve_st3", "dve_xn2", "dve_xn1", "dve_enc", "dve_logit", "dve_krope",
                 "dve_vx", "dve_x2", "dve_keep3", "c_rope", "c_krope", "c_x1", "c_enc",
                 "pool_v1", "pool_r1", "pool_v2", "pool_r2", "pool_v3", "pool_r3", "pool_vc", "pool_rc", "pool_D",
                 "pool_Dx", "act_mask",
                 "g_dve", "g_act", "g_pe", "g_scatter", "f_x3", "f_xs", "f_xT", "f_xsT", "f_h", "f_gelu", "c_setup", "bias_sent", "pick_ready", "c_route", "setup_norm", "bias_parts", "g_diff", "g_slots", "g_score", "c_pool", "ld_bias", "f_hT",
                 "f_hTs", "f_y", "f_ysb", "f_ystored", "f_gath", "f_out", "f_stored"]
        for n in names:
            s(n)
        Z = S_
        f_x3s = [sem(f"f_x3sent{n}") for n in range(4)]
        f_gaths = [sem(f"f_gathered{n}") for n in range(NY)]
        f_sts = [sem(f"f_stored{n}") for n in range(NY)]
        block = ctx.enter_context(nc.Block())

        def plain(eng):
            eng.nop(nofuse=True)

        @block.sync
        def _(sp):
            for dst, name in ((ident[:], "ident"), (misc[:], "misc"), (wqk, "wqk"), (wv, "wv")):
                sp.dma_start(dst, a[name]).then_inc(Z["ld_const"], 16)
            sp.dma_start(x[:, 0, :], a["x"][0]).then_inc(Z["ld_x"], 16)
            for dst, name in ((ropeq, "ropeq"), (ropek, "ropek"), (wxq, "wxq"), (wkv, "wkv"),
                              (wo, "wo"), (wred, "wred")):
                sp.dma_start(dst, a[name]).then_inc(Z["ld_w"], 16)
            sp.dma_start(small[:, 0:2], a["rms"]).then_inc(Z["ld_w"], 16)
            sp.dma_start(small[0:E, 16:32], a["wg"]).then_inc(Z["ld_w"], 16)

            def context(b):
                sp.wait_ge(Z["pe_kv"], b)
                sp.dma_start(ctxT, a["ctxT"][b]).then_inc(Z["ld_ctxT"], 16)
                sp.wait_ge(Z["act_sq"], KT * b)
                sp.dma_start(ctxn[:], a["ctx"][b]).then_inc(Z["ld_ctxn"], 16)
                sp.wait_ge(Z["act_mask"], b)
                plain(sp)
                sp.dma_start(mask_row[GD:R, :], a["mask"][b]).then_inc(Z["ld_mask"], 16)

            def tokens(b):
                sp.wait_ge(Z["ld_x"], 16 * b)
                sp.dma_start(x[:, b, :], a["x"][b]).then_inc(Z["ld_x"], 16)

            context(0)
            tokens(1)
            with sp.Fori(1, B - 1) as b:
                context(b)
                tokens(b + 1)
            context(B - 1)
            sp.wait_ge(Z["dve_logit"], B)
            sp.dma_start(w1[:, E - LATE:E, :, :], a["w1"][:, E - LATE:E]).then_inc(Z["ld_late"], 16)
            sp.dma_start(w2[:, E - LATE:E, :, :], a["w2"][:, E - LATE:E]).then_inc(Z["ld_late"], 16)

            sp.wait_ge(Z["g_dve"], 1)
            sp.dma_start(hid[:, :], a["pick"]).then_inc(Z["ld_bias"], 16)
            sp.dma_start(braw2[:, 0:F], a["b1"]).then_inc(Z["ld_bias"], 16)
            sp.dma_start(braw2[:, F:F + D], a["b2"]).then_inc(Z["ld_bias"], 16)
            sp.wait_ge(Z["bias_parts"], 1)
            for part in range(3):
                sp.dma_start(bias_rows[part:3 * E:3, :], b3[:, part, :]).then_inc(Z["bias_sent"], 16)

            sp.wait_ge(Z["bias_sent"], 48)
            for n in range(4):
                sp.wait_ge(f_x3s[n], 16 * (B // 4))

            sp.dma_start(xs[:], sorted_x[0:P, :]).then_inc(Z["f_xs"], 16)
            with sp.Fori(1, TILES) as j:
                sp.wait_ge(Z["f_xT"], j)
                sp.dma_start(xs[:], sorted_x[bass.ds(j * P, P), :]).then_inc(Z["f_xs"], 16)
                sp.wait_ge(Z["f_ysb"], j)
                sp.dma_start(sorted_y[bass.ds((j - 1) * P, P), :], ysb[:]).then_inc(Z["f_ystored"], 16)
            sp.wait_ge(Z["f_ysb"], TILES)
            sp.dma_start(sorted_y[(TILES - 1) * P:TILES * P, :], ysb[:]).then_inc(Z["f_ystored"], 16)
            sp.wait_ge(Z["f_ystored"], 16 * TILES)

            for b in range(B):
                sp.wait_ge(Z["f_out"], b + 1)
                sp.dma_start(out[b], yg[b % NY][:]).then_inc(f_sts[b % NY], 16)
            for n in range(NY):
                sp.wait_ge(f_sts[n], 16 * (B // NY))
            sp.wait_ge(Z["zero_sent"], 16)

        @block.tensor
        def _(pe):
            def turn(dst, src, rows, cols):
                plain(pe)
                return pe.transpose(dst, src, ident[0:rows, 0:rows])

            def kv(b):
                pe.wait_ge(Z["ld_ctxT"], 16 * (b + 1))
                pe.wait_ge(Z["act_qT"], b)
                for t in range(KT):
                    for c in range(KC):
                        mm = pe.matmul(kv_ps[:, t, :], ctxT[:, c, KP * t:KP * t + KP], wkv[:, c, :],
                                       start=(c == 0), stop=(c == KC - 1))
                mm.then_inc(Z["pe_kv"], 1)

            def k_turn(b):
                pe.wait_ge(Z["dve_krope"], b + 1)
                pe.wait_ge(Z["dve_vx"], b + 1)
                for t in range(KT):
                    mm = turn(kxT_ps[:, KP * t:KP * t + KP], krot[:, t, :], KP, GD)
                mm.then_inc(Z["pe_kT"], 1)

            def x_turn(b):
                pe.wait_ge(Z["dve_xn1"], b + 1)
                if not (isinstance(b, int) and b == 0):
                    pe.wait_ge(Z["dve_enc"], b - 1)
                for c in range(KC):
                    mm = turn(xT_ps[:, c, :], xn[:, P * c:P * c + P], T, P)
                mm.then_inc(Z["pe_xT"], 1)

            def x2_turn(b):
                pe.wait_ge(Z["dve_xn2"], b + 1)
                pe.wait_ge(Z["act_kxT"], b + 1)
                for c in range(KC):
                    mm = turn(x2T_ps[:, c, :], xn2[:, P * c:P * c + P], T, P)
                mm.then_inc(Z["pe_x2T"], 1)

            def qkv(b):
                pe.wait_ge(Z["act_xT"], b + 1)
                pe.wait_ge(Z["dve_x1"], b)
                if not (isinstance(b, int) and b == 0):
                    pe.wait_ge(Z["act_encT"], b - 1)
                for o in range(4):
                    for c in range(KC):
                        mm = pe.matmul(qk_ps[:, o, :], wqk[:, c, P * o:P * o + P], xnT[:, c, :],
                                       start=(c == 0), stop=(c == KC - 1))
                mm.then_inc(Z["pe_qk"], 1)
                if not (isinstance(b, int) and b == 0):
                    pe.wait_ge(Z["dve_x2"], b - 1)
                for c in range(KC):
                    mm = pe.matmul(v_ps, xnT[:, c, :], wv[:, c, :], start=(c == 0), stop=(c == KC - 1))
                mm.then_inc(Z["pe_v"], 1)

            def q_proj(b):
                pe.wait_ge(Z["act_x2T"], b + 1)
                pe.wait_ge(Z["dve_enc"], b)
                for c in range(KC):
                    mm = pe.matmul(q_ps, xn2T[:, c, :], wxq[:, c, :], start=(c == 0), stop=(c == KC - 1))
                mm.then_inc(Z["pe_q"], 1)

            def top(ap):
                return ap.bitcast(BF16)[:, 1::2]

            def self_max(b):
                pe.wait_ge(Z["act_kT"], b + 1)
                for c in range(KC):
                    pe.wait_ge(Z["dve_qexp"], KC * b + c + 1)
                    if not (isinstance(b, int) and b == 0):
                        pe.wait_ge(Z["act_xexp"], KT * (b - 1))
                    for h in range(HC):
                        mm = pe.matmul(U[c][0:T, h // 4, (h % 4) * T:(h % 4 + 1) * T], top(qexp[c][:, h, :]),
                                       top(kT[:, c, :]), start=True, stop=True)
                    mm.then_inc(Z["pe_smax"], 1)

            def q_turn(b):
                pe.wait_ge(Z["dve_rope"], b + 1)
                for g in range(G):
                    mm = turn(qxT_ps[:, g * T:(g + 1) * T], qrot[:, g * GD:(g + 1) * GD], T, GD)
                mm.then_inc(Z["pe_qT"], 1)

            def cross_max(b, smaxed):
                pe.wait_ge(Z["act_qT"], b + 1)
                pe.wait_ge(Z["act_kxT"], b + 1)
                pe.wait_ge(Z["act_mask"], b + 1)
                for u in range(2):
                    pe.wait_ge(Z["dve_smax"], smaxed + u + 1)
                    for n in range(2):
                        g = 2 * u + n
                        mm = pe.matmul(U[u][0:T, n, 0:S], top(qxT[:, g * T:(g + 1) * T]), top(kxT[:, :]),
                                       start=True, stop=True)
                    mm.then_inc(Z["pe_xmax"], 1)

            def self_exp(b, xmaxed):
                for c in range(KC):
                    pe.wait_ge(Z["pool_D"], KC * b + c + 1)
                    if xmaxed is not None:
                        pe.wait_ge(Z["dve_xmax"], xmaxed + c)
                    for n in range(2):
                        dst = U[c][0:T, n, 0:4 * T]
                        pe.matmul(dst, kT[:, c, :], qexp[c][:, 4 * n:4 * n + 4, :], start=True, stop=False)
                        mm = pe.matmul(dst, ones[0:T, 0:T],
                                       neg_diag[:, HC * c + 4 * n:HC * c + 4 * n + 4, :], start=False, stop=True)
                    mm.then_inc(Z["pe_sexp"], 1)

            def cross_exp(b, sexped):
                pe.wait_ge(Z["pool_Dx"], b + 1)
                for t in range(KT):
                    pe.wait_ge(Z["act_sexp"], sexped + t // 2 + 1)
                    dst = U[t // 2][0:KP, t % 2, 0:G * T]
                    pe.matmul(dst, kxT[:, KP * t:KP * t + KP], qxT[:, :], start=True, stop=False)
                    mm = pe.matmul(dst, ones[0:T, 0:KP], neg_diagx, start=False, stop=True)
                    mm.then_inc(Z["pe_xexp"], 1)

            def self_pv(b):
                pe.wait_ge(Z["act_v"], b + 1)
                for c in range(KC):
                    pe.wait_ge(Z["act_sexp"], KC * b + c + 1)
                    for h in range(HC * c, HC * c + HC):
                        mm = pe.matmul(pv_ps[:, h, :], prob[:, h, :], v1[:, h, :], start=True, stop=True)
                mm.then_inc(Z["pe_pv"], 1)

            def cross_pv(b):
                pe.wait_ge(Z["dve_vx"], b + 1)
                pe.wait_ge(Z["act_xexp"], KT * (b + 1))
                for g in range(G):
                    for t in range(KT):
                        mm = pe.matmul(pvx_ps[:, g, :], probx[:, t, g * T:(g + 1) * T], vx[:, t, :],
                                       start=(t == 0), stop=(t == KT - 1))
                mm.then_inc(Z["pe_xpv"], 1)

            def enc_turn(b, pvs):
                pe.wait_ge(Z["dve_enc"], b + 1)
                pe.wait_ge(Z["dve_x1"], pvs)
                for c in range(KC):
                    mm = turn(encT_ps[:, c, :], enc[:, P * c:P * c + P], T, P)
                mm.then_inc(Z["pe_encT"], 1)

            def out_proj(b, vs):
                pe.wait_ge(Z["act_encT"], b + 1)
                pe.wait_ge(Z["dve_logit"], b)
                pe.wait_ge(Z["act_v"], vs)
                for c in range(KC):
                    mm = pe.matmul(out_ps, encT[:, c, :], wo[:, c, :], start=(c == 0), stop=(c == KC - 1))
                mm.then_inc(Z["pe_out"], 1)

            def x3_turn(b, vs):
                pe.wait_ge(Z["dve_x3"], b + 1)
                pe.wait_ge(Z["act_v"], vs)
                for c in range(KC):
                    mm = turn(x3T_ps[:, c, :], xn3[:, P * c:P * c + P], T, P)
                mm.then_inc(Z["pe_x3T"], 1)

            def router_red(b):
                pe.wait_ge(Z["act_x3T"], b + 1)
                for c in range(KC):
                    mm = pe.matmul(redT_ps, wred[:, c, :], xn3T[:, c, :], start=(c == 0), stop=(c == KC - 1))
                mm.then_inc(Z["pe_red"], 1)

            def router_logits(b):
                pe.wait_ge(Z["act_red"], b + 1)
                pe.matmul(logit_ps, redT[:, :], wgT[:, :], start=True, stop=True).then_inc(Z["pe_logit"], 1)

            pe.wait_ge(Z["ld_const"], 16 * 4)
            pe.wait_ge(Z["ones_ready"], 1)
            x_turn(0)
            qkv(0)
            self_max(0)
            self_exp(0, None)
            self_pv(0)
            pe.wait_ge(Z["weights_ready"], 1)
            kv(0)
            turn(b7[0:HD, 0:E], small[0:E, 32:48], E, HD).then_inc(Z["setup_pe"], 1)
            k_turn(0)
            pe.wait_ge(Z["setup_dve"], 1)

            def iteration(i, first=False, last=False):
                if not last:
                    x_turn(i + 1)
                x2_turn(i)
                if not last:
                    qkv(i + 1)
                q_proj(i)
                if not last:
                    self_max(i + 1)
                q_turn(i)
                cross_max(i, KC * (i + 1) if not last else KC * i)
                if not last:
                    self_exp(i + 1, KC * i + 1)
                if not first:
                    x3_turn(i - 1, B if last else i + 2)
                cross_exp(i, KC * (i + 1) if not last else KC * i)
                if not first:
                    router_red(i - 1)
                if not last:
                    self_pv(i + 1)
                if not first:
                    router_logits(i - 1)
                cross_pv(i)
                if not last:
                    kv(i + 1)
                enc_turn(i, B if last else i + 2)
                if not last:
                    k_turn(i + 1)
                out_proj(i, B if last else i + 2)

            iteration(0, first=True)
            with pe.Fori(1, B - 1) as i:
                iteration(i)
            iteration(B - 1, last=True)
            x3_turn(B - 1, B)
            router_red(B - 1)
            router_logits(B - 1)

            pe.wait_ge(Z["g_dve"], 1)
            pe.matmul(U[0][0:T, 0, 0:E * B], tri[:, :], onehot_b[:], start=True, stop=True)
            pe.matmul(U[0][0:T, 1, 0:E * B], ones[0:T, 0:T], onehot_b[:], start=True, stop=True)\
              .then_inc(Z["g_pe"], 1)

            h_ps = U[0][:, :, :].rearrange("p a n -> p (a n)")
            hT_ps = U[1][:, :, :].rearrange("p a (k t) -> p (a k) t", t=P)
            xsT_ps = b4[:, 0:KC * P].rearrange("p (k t) -> p k t", k=KC)
            y_ps = b5[:, 0:D]

            def expert(j):
                return pe.value_load(tile_e_i[0:1, bass.ds(j, 1)], min_val=0, max_val=E - 1)

            def tile_turn(j):
                pe.wait_ge(Z["f_xs"], 16 * (j + 1))
                for c in range(KC):
                    mm = pe.transpose(xsT_ps[:, c, :], xs[:, P * c:P * c + P], ident[:, :])
                mm.then_inc(Z["f_xT"], 1)

            def up(j, e):
                pe.wait_ge(Z["f_xsT"], j + 1)
                pe.wait_ge(Z["f_gelu"], 2 * j)
                for n in range(2):
                    for c in range(KC):
                        pe.matmul(h_ps[:, NB * n:NB * n + NB], xsT[:, c, :], w1[:, e, c, NB * n:NB * n + NB],
                                  start=(c == 0), stop=False)
                    pe.matmul(h_ps[:, NB * n:NB * n + NB], pick[:, e, :], bias_rows[:, NB * n:NB * n + NB],
                              start=False, stop=True).then_inc(Z["f_h"], 1)

            def hidden_turn(j):
                for n in range(2):
                    pe.wait_ge(Z["f_gelu"], 2 * j + n + 1)
                    pe.wait_ge(Z["f_hTs"], 2 * j)
                    for k in range(4 * n, 4 * n + 4):
                        mm = pe.transpose(hT_ps[:, k, :], hid[:, P * k:P * k + P], ident[:, :])
                    mm.then_inc(Z["f_hT"], 1)

            def down(j, e):
                pe.wait_ge(Z["f_ysb"], j)
                pe.matmul(y_ps, pick[:, e, :], bias_rows[:, F:F + D], start=True, stop=False)
                for k in range(FC):
                    if k % 4 == 0:
                        pe.wait_ge(Z["f_hTs"], 2 * j + k // 4 + 1)
                    mm = pe.matmul(y_ps, hidT[:, k, :], w2[:, e, k, :], start=False, stop=(k == FC - 1))
                mm.then_inc(Z["f_y"], 1)

            pe.wait_ge(Z["g_dve"], 2)
            pe.wait_ge(Z["ld_late"], 32)
            pe.wait_ge(Z["ld_early"], 16 * 2 * (E - LATE))
            pe.wait_ge(Z["bias_sent"], 48)
            pe.wait_ge(Z["pick_ready"], 1)
            tile_turn(0)
            up(0, expert(0))
            tile_turn(1)

            def tile(j, ahead=True):
                hidden_turn(j)
                up(j + 1, expert(j + 1))
                down(j, expert(j))
                if ahead:
                    tile_turn(j + 2)

            tile(0)
            with pe.Fori(1, TILES - 2) as j:
                tile(j)
            tile(TILES - 2, ahead=False)
            hidden_turn(TILES - 1)
            down(TILES - 1, expert(TILES - 1))

        @block.scalar
        def _(act):
            def copy(dst, src):
                return act.activation(dst, src, ACT.Copy)

            def squares(b):
                act.wait_ge(Z["ld_ctxn"], 16 * (b + 1))
                act.wait_ge(Z["pool_vc"], b)
                for t in range(KT):
                    if not (isinstance(b, int) and b == 0 and t == 0):
                        act.wait_ge(Z["act_sq"], KT * b + t)
                    act.activation(square, ctxn[:, t, :], ACT.Square, accum_out=ss[:, t:t + 1])\
                       .then_inc(Z["act_sq"], 1)

            def x_copy(b):
                act.wait_ge(Z["pe_xT"], b + 1)
                act.wait_ge(Z["pe_v"], b)
                copy(xnT[:], xT_ps).then_inc(Z["act_xT"], 1)

            def x2_copy(b):
                act.wait_ge(Z["pe_x2T"], b + 1)
                act.wait_ge(Z["pe_q"], b)
                copy(xn2T[:], x2T_ps).then_inc(Z["act_x2T"], 1)

            def kv_copy(b):
                act.wait_ge(Z["pe_qk"], b + 1)
                act.wait_ge(Z["pe_sexp"], KC * b)
                copy(kT[:], qk_ps[:, KC:2 * KC, :]).then_inc(Z["act_kT"], 1)
                act.wait_ge(Z["pe_v"], b + 1)
                act.wait_ge(Z["pe_pv"], b)
                copy(v1[:, :, 0:HD], v_ps.rearrange("p (h d) -> p h d", h=H)).then_inc(Z["act_v"], 1)

            def q_copy(b):
                act.wait_ge(Z["pe_qT"], b + 1)
                act.wait_ge(Z["pe_xexp"], KT * b)
                copy(qxT[0:GD, :], qxT_ps).then_inc(Z["act_qT"], 1)

            def self_exp(b):
                for c in range(KC):
                    act.wait_ge(Z["pe_sexp"], KC * b + c + 1)
                    act.wait_ge(Z["pe_pv"], b)
                    act.activation(prob[:, HC * c:HC * c + HC, :].rearrange("p (a h) t -> p a (h t)", a=2),
                                   U[c][0:T, :, 0:4 * T], ACT.Exp, scale=HD ** -0.5).then_inc(Z["act_sexp"], 1)

            def x3_copy(b):
                act.wait_ge(Z["pe_x3T"], b + 1)
                act.wait_ge(Z["pe_red"], b)
                copy(xn3T[:], x3T_ps).then_inc(Z["act_x3T"], 1)

            def cross_exp(b):
                act.wait_ge(Z["pe_xpv"], b)
                for t in range(KT):
                    act.wait_ge(Z["pe_xexp"], KT * b + t + 1)
                    act.activation(probx[:, t, :], U[t // 2][0:KP, t % 2, 0:G * T], ACT.Exp,
                                   scale=GD ** -0.5).then_inc(Z["act_xexp"], 1)

            def red_copy(b):
                act.wait_ge(Z["pe_red"], b + 1)
                act.wait_ge(Z["pe_logit"], b)
                copy(redT[:], redT_ps).then_inc(Z["act_red"], 1)

            def enc_copy(b):
                act.wait_ge(Z["pe_encT"], b + 1)
                act.wait_ge(Z["pe_out"], b)
                copy(encT[:], encT_ps).then_inc(Z["act_encT"], 1)

            def k_copy(b):
                act.wait_ge(Z["pe_kT"], b + 1)
                act.wait_ge(Z["pe_xexp"], KT * b)
                copy(kxT[0:GD, :], kxT_ps).then_inc(Z["act_kxT"], 1)
                act.wait_ge(Z["ld_mask"], 16 * (b + 1))
                act.activation(kxT[GD:R, :], mask_row[GD:R, :], ACT.Copy, bias=-BIG, scale=BIG)\
                   .then_inc(Z["act_mask"], 1)

            x_copy(0)
            kv_copy(0)
            self_exp(0)
            squares(0)
            k_copy(0)

            def iteration(i, first=False, last=False):
                if not last:
                    x_copy(i + 1)
                x2_copy(i)
                if not last:
                    kv_copy(i + 1)
                    squares(i + 1)
                q_copy(i)
                if not last:
                    self_exp(i + 1)
                if not first:
                    x3_copy(i - 1)
                cross_exp(i)
                if not first:
                    red_copy(i - 1)
                enc_copy(i)
                if not last:
                    k_copy(i + 1)

            iteration(0, first=True)
            iteration(1)
            with act.Fori(2, B - 1) as i:
                iteration(i)
            iteration(B - 1, last=True)
            x3_copy(B - 1)
            red_copy(B - 1)

            act.wait_ge(Z["g_diff"], 1)
            act.activation(gexp[:], gdiff[:], ACT.Exp).then_inc(Z["g_act"], 1)

            def tile_copy(j):
                act.wait_ge(Z["f_xT"], j + 1)
                if not (isinstance(j, int) and j == 0):
                    act.wait_ge(Z["f_h"], 2 * j)
                copy(xsT[:], b4[:, 0:KC * P].rearrange("p (k t) -> p k t", k=KC)).then_inc(Z["f_xsT"], 1)

            def gelu(j):
                if not (isinstance(j, int) and j == 0):
                    act.wait_ge(Z["f_hT"], 2 * j)
                for n in range(2):
                    act.wait_ge(Z["f_h"], 2 * j + n + 1)
                    act.activation(hid[:, NB * n:NB * n + NB], U[0][:, n, :], ACT.Gelu).then_inc(Z["f_gelu"], 1)

            tile_copy(0)
            gelu(0)
            tile_copy(1)
            with act.Fori(1, TILES - 1) as j:
                gelu(j)
                tile_copy(j + 1)
            gelu(TILES - 1)

        @block.vector
        def _(dve):
            def norm_stats(b, n):
                bn, st = (("dve_bn1", "dve_st1"), ("dve_bn2", "dve_st2"), ("dve_bn3", "dve_st3"))[n]
                plain(dve)
                dve.bn_stats(stats[:, n, :], x[:, b, :]).then_inc(Z[bn], 1)
                dve.wait_ge(Z[bn], b + 1)
                plain(dve)
                dve.bn_aggr(mv[:, n, :], stats[:, n, :]).then_inc(Z[st], 1)

            def norm_apply(b, n, dst, done):
                dve.wait_ge(Z[("pool_r1", "pool_r2", "pool_r3")[n]], b + 1)
                dve.tensor_scalar(dst[:], x[:, b, :], mv[:, n, 0:1], rs[:, n, 1:2], ALU.subtract, ALU.mult)\
                   .then_inc(Z[done], 1)

            def stats1(b):
                dve.wait_ge(Z["ld_x"], 16 * (b + 1))
                norm_stats(b, 0)

            def apply1(b):
                dve.wait_ge(Z["pe_xT"], b)
                norm_apply(b, 0, xn, "dve_xn1")

            def stats2(b):
                dve.wait_ge(Z["dve_x1"], b + 1)
                norm_stats(b, 1)

            def apply2(b):
                dve.wait_ge(Z["pe_x2T"], b)
                norm_apply(b, 1, xn2, "dve_xn2")

            def stats3(b):
                dve.wait_ge(Z["dve_x2"], b + 1)
                norm_stats(b, 2)

            def apply3(b):
                dve.wait_ge(Z["pe_x3T"], b)
                norm_apply(b, 2, xn3, "dve_x3")
                dve.tensor_copy(mean_rstd3[:, b, 0:1], mv[:, 2, 0:1])
                dve.tensor_copy(mean_rstd3[:, b, 1:2], rs[:, 2, 1:2]).then_inc(Z["dve_keep3"], 1)

            def q_expand(b):
                dve.wait_ge(Z["act_kT"], b + 1)
                dve.wait_ge(Z["pe_sexp"], KC * b)
                for c in range(KC):
                    dve.tensor_tensor(qexp[c], qk_ps[:, c, :].unsqueeze(1).to_broadcast([P, HC, T]),
                                      head_of.unsqueeze(2).to_broadcast([P, HC, T]), ALU.mult)\
                       .then_inc(Z["dve_qexp"], 1)

            def q_rope(b):
                dve.wait_ge(Z["pe_q"], b + 1)
                if not (isinstance(b, int) and b == 0):
                    dve.wait_ge(Z["pe_qT"], b)
                q4 = q_ps.rearrange("p (g d) -> p g d", g=G)
                a4 = ropea[:].rearrange("p (g d) -> p g d", g=G)
                r4 = ropeb[:].rearrange("p (g d) -> p g d", g=G)
                hf = GD // 2
                dve.tensor_tensor(a4, q4, ropeq[:, 0:GD].unsqueeze(1).to_broadcast([T, G, GD]), ALU.mult)\
                   .then_inc(Z["c_rope"], 1)
                dve.tensor_tensor(r4[:, :, 0:hf], q4[:, :, hf:GD],
                                  ropeq[:, GD:GD + hf].unsqueeze(1).to_broadcast([T, G, hf]), ALU.mult)\
                   .then_inc(Z["c_rope"], 1)
                dve.tensor_tensor(r4[:, :, hf:GD], q4[:, :, 0:hf],
                                  ropeq[:, GD + hf:2 * GD].unsqueeze(1).to_broadcast([T, G, hf]), ALU.mult)\
                   .then_inc(Z["c_rope"], 1)
                dve.wait_ge(Z["c_rope"], 3 * (b + 1))
                dve.tensor_tensor(qrot[:], ropea[:], ropeb[:], ALU.add).then_inc(Z["dve_rope"], 1)

            def self_max(b):
                for c in range(KC):
                    dve.wait_ge(Z["pe_smax"], KC * b + c + 1)
                    dve.wait_ge(Z["pool_D"], KC * b)
                    dve.tensor_reduce(nm[:, HC * c:HC * c + HC].rearrange("p (a h) -> p a h", a=2),
                                      U[c][0:T, :, 0:4 * T].rearrange("p a (h t) -> p a h t", t=T), AX.X, ALU.max,
                                      negate=True).then_inc(Z["dve_smax"], 1)

            def cross_max(b):
                dve.wait_ge(Z["pool_Dx"], b)
                for u in range(2):
                    dve.wait_ge(Z["pe_xmax"], 2 * b + u + 1)
                    dve.tensor_reduce(nmx[:, 2 * u:2 * u + 2], U[u][0:T, :, 0:S], AX.X, ALU.max, negate=True)\
                       .then_inc(Z["dve_xmax"], 1)

            def self_out(b):
                dve.wait_ge(Z["pe_pv"], b + 1)
                dve.reciprocal(den[:].unsqueeze(2), pv_ps[:, :, HD:HD + 1]).then_inc(Z["c_x1"], 1)
                dve.wait_ge(Z["c_x1"], 2 * b + 1)
                dve.tensor_tensor(tmp1[:].rearrange("p (h d) -> p h d", h=H), pv_ps[:, :, 0:HD],
                                  den[:].unsqueeze(2).to_broadcast([T, H, HD]), ALU.mult).then_inc(Z["c_x1"], 1)
                dve.wait_ge(Z["c_x1"], 2 * b + 2)
                dve.tensor_tensor(x[:, b, :], x[:, b, :], tmp1[:], ALU.add).then_inc(Z["dve_x1"], 1)

            def cross_enc(b):
                dve.wait_ge(Z["pe_xpv"], b + 1)
                dve.reciprocal(denx[:].unsqueeze(2), pvx_ps[:, :, GD:R]).then_inc(Z["c_enc"], 1)
                dve.wait_ge(Z["c_enc"], b + 1)
                dve.wait_ge(Z["pe_encT"], b)
                dve.tensor_tensor(enc[:].rearrange("p (g d) -> p g d", g=G), pvx_ps[:, :, 0:GD],
                                  denx[:].unsqueeze(2).to_broadcast([T, G, GD]), ALU.mult).then_inc(Z["dve_enc"], 1)

            def logits_out(b):
                dve.wait_ge(Z["pe_logit"], b + 1)
                dve.tensor_copy(logits[:, b, :], logit_ps).then_inc(Z["dve_logit"], 1)

            def kv_out(b):
                dve.wait_ge(Z["pe_kv"], b + 1)
                dve.wait_ge(Z["pool_rc"], b + 1)
                r = rc[:].unsqueeze(2).to_broadcast([KP, KT, GD])
                dve.tensor_tensor(kraw[:], kv_ps[:, :, 0:GD], r, ALU.mult).then_inc(Z["c_krope"], 1)
                dve.wait_ge(Z["pe_xpv"], b)
                dve.tensor_tensor(vx[:, :, 0:GD], kv_ps[:, :, GD:2 * GD], r, ALU.mult).then_inc(Z["dve_vx"], 1)
                dve.wait_ge(Z["c_krope"], 4 * b + 1)
                hf = GD // 2
                dve.tensor_tensor(kra[:], kraw[:], ropek[:, :, 0:GD], ALU.mult).then_inc(Z["c_krope"], 1)
                dve.tensor_tensor(krb[:, :, 0:hf], kraw[:, :, hf:GD], ropek[:, :, GD:GD + hf], ALU.mult)\
                   .then_inc(Z["c_krope"], 1)
                dve.tensor_tensor(krb[:, :, hf:GD], kraw[:, :, 0:hf], ropek[:, :, GD + hf:2 * GD], ALU.mult)\
                   .then_inc(Z["c_krope"], 1)
                dve.wait_ge(Z["c_krope"], 4 * b + 4)
                if not (isinstance(b, int) and b == 0):
                    dve.wait_ge(Z["pe_kT"], b)
                dve.tensor_tensor(krot[:], kra[:], krb[:], ALU.add).then_inc(Z["dve_krope"], 1)

            def cross_out(b):
                dve.wait_ge(Z["pe_out"], b + 1)
                dve.tensor_tensor(x[:, b, :], out_ps, x[:, b, :], ALU.add).then_inc(Z["dve_x2"], 1)

            step = [0]

            def link(ins):
                step[0] += 1
                ins.then_inc(Z["c_setup"], 1)
                dve.wait_ge(Z["c_setup"], step[0])

            dve.memset(ones[:], 1.0)
            dve.memset(v1[:, :, HD:HD + 1], 1.0)
            dve.memset(vx[:, :, GD:R], 1.0)
            dve.memset(neghalf[:], -0.5)
            dve.memset(ones_f[:], 1.0)
            dve.memset(qxT[GD:R, :], 1.0).then_inc(Z["ones_ready"], 1)
            dve.wait_ge(Z["ld_const"], 16 * 4)
            stats1(0)
            apply1(0)
            q_expand(0)
            self_max(0)
            self_out(0)
            stats2(0)
            stats1(1)
            dve.wait_ge(Z["ld_w"], 16 * 8)
            link(dve.tensor_scalar(small[:, 2:4], small[:, 0:2], 1.0, None, ALU.add))
            for c in range(KC):
                dve.tensor_scalar(wxq[:, c, :], wxq[:, c, :], small[:, 2 + c:3 + c], None, ALU.mult)
                dve.tensor_scalar(wkv[:, c, :], wkv[:, c, :], small[:, 2 + c:3 + c], None, ALU.mult)
            link(dve.tensor_tensor(small[0:E, 48:64], small[0:E, 16:32], small[0:E, 16:32], ALU.mult))
            link(dve.tensor_reduce(small[0:E, 5:6], small[0:E, 48:64], AX.X, ALU.add))
            dve.tensor_copy(small[0:E, 6:7], small[0:E, 5:6]).then_inc(Z["setup_norm"], 1)
            dve.wait_ge(Z["setup_pool"], 1)
            link(dve.tensor_scalar(small[0:E, 8:9], small[0:E, 7:8], 0.0001, None, ALU.max))
            link(dve.reciprocal(small[0:E, 9:10], small[0:E, 8:9]))
            dve.tensor_scalar(small[0:E, 32:48], small[0:E, 16:32], small[0:E, 9:10], None, ALU.mult)\
               .then_inc(Z["weights_ready"], 1)
            dve.wait_ge(Z["setup_pe"], 1)
            dve.tensor_copy(wgT[:], b7[0:HD, 0:E]).then_inc(Z["setup_dve"], 1)
            dve.tensor_copy(tri[:], misc[0:T, 344:456]).then_inc(Z["setup_dve"], 1)
            kv_out(0)
            apply2(0)
            apply1(1)

            def iteration(i, first=False, last=False, ahead=True):
                if not first:
                    stats3(i - 1)
                if not last:
                    q_expand(i + 1)
                q_rope(i)
                if not first:
                    apply3(i - 1)
                if not last:
                    self_max(i + 1)
                cross_max(i)
                if not last:
                    self_out(i + 1)
                    stats2(i + 1)
                if ahead:
                    stats1(i + 2)
                cross_enc(i)
                if not first:
                    logits_out(i - 1)
                if not last:
                    kv_out(i + 1)
                    apply2(i + 1)
                if ahead:
                    apply1(i + 2)
                cross_out(i)

            iteration(0, first=True)
            iteration(1)
            with dve.Fori(2, B - 2) as i:
                iteration(i)
            iteration(B - 2, ahead=False)
            iteration(B - 1, last=True, ahead=False)
            stats3(B - 1)
            apply3(B - 1)
            logits_out(B - 1)

            step[0] = 0

            def then(ins):
                step[0] += 1
                ins.then_inc(Z["c_route"], 1)
                dve.wait_ge(Z["c_route"], step[0])

            dve.wait_ge(Z["dve_logit"], B)
            then(dve.tensor_reduce(gmax[:], logits[:], AX.X, ALU.max))
            gm = gmax[:].unsqueeze(2).to_broadcast([T, B, E])
            dve.tensor_tensor(gdiff[:], logits[:], gm, ALU.subtract).then_inc(Z["g_diff"], 1)
            then(dve.tensor_tensor(cand[:], logits[:], gm, ALU.is_ge))
            nums = misc[0:T, 8:16].unsqueeze(1).to_broadcast([T, B, E])
            then(dve.tensor_tensor(cand[:], cand[:], nums, ALU.mult))
            then(dve.tensor_reduce(best[:], cand[:], AX.X, ALU.min))
            then(dve.tensor_tensor(onehot[:], nums, best[:].unsqueeze(2).to_broadcast([T, B, E]), ALU.is_equal))
            dve.tensor_copy(onehot_b[:], onehot[:].rearrange("p b e -> p e b")).then_inc(Z["g_dve"], 1)
            dve.wait_ge(Z["g_pe"], 1)
            then(dve.tensor_copy(totals[:], U[0][0:T, 1, 0:E * B]))
            then(dve.tensor_tensor_scan(running[:], misc[0:T, 44:300], totals[:], 0.0, ALU.mult, ALU.add))
            then(dve.tensor_tensor(place[:].rearrange("p e b -> p (e b)"), running[:], totals[:], ALU.subtract))
            then(dve.tensor_tensor(place[:].rearrange("p e b -> p (e b)"), U[0][0:T, 0, 0:E * B],
                                   place[:].rearrange("p e b -> p (e b)"), ALU.add))
            count = running[:].rearrange("p (e b) -> p e b", e=E)[:, :, B - 1:B]
            then(dve.tensor_tensor(over_t[:], count.to_broadcast([T, E, 28]),
                                   misc[0:T, 16:44].unsqueeze(1).to_broadcast([T, E, 28]), ALU.is_gt))
            then(dve.tensor_reduce(tiles_e[:], over_t[:], AX.X, ALU.add))
            then(dve.tensor_tensor_scan(ends[:], ones_f[0:T, :], tiles_e[:], 0.0, ALU.mult, ALU.add))
            then(dve.tensor_tensor(starts[:], ends[:], tiles_e[:], ALU.subtract))
            then(dve.tensor_scalar(starts[:], starts[:], float(P), None, ALU.mult))
            then(dve.tensor_tensor(place[:], place[:], starts[:].unsqueeze(2).to_broadcast([T, E, B]), ALU.add))
            then(dve.tensor_tensor(place[:], place[:], onehot[:].rearrange("p b e -> p e b"), ALU.mult))
            then(dve.tensor_reduce(slot[:], place[:].rearrange("p e b -> p b e"), AX.X, ALU.add))
            dve.tensor_copy(slot_i[:], slot[:]).then_inc(Z["g_slots"], 1)
            then(dve.tensor_tensor(past[:], misc[0:1, 308:344].unsqueeze(2).to_broadcast([1, 36, E]),
                                   ends[0:1, :].unsqueeze(1).to_broadcast([1, 36, E]), ALU.is_ge))
            then(dve.tensor_reduce(tile_e[:], past[:], AX.X, ALU.add))
            then(dve.tensor_scalar(tile_e[:], tile_e[:], float(E - 1), None, ALU.min))
            dve.tensor_copy(tile_e_i[:], tile_e[:]).then_inc(Z["g_dve"], 1)

            dve.wait_ge(Z["dve_keep3"], B)
            for b in range(B):
                if b >= 4:
                    dve.wait_ge(f_x3s[b % 4], 16 * (b // 4))
                dve.tensor_scalar(xs3[b % 4][:], x[:, b, :], mean_rstd3[:, b, 0:1], mean_rstd3[:, b, 1:2],
                                  ALU.subtract, ALU.mult).then_inc(Z["f_x3"], 1)
            dve.wait_ge(Z["ld_bias"], 48)
            dve.tensor_copy(pick[:].rearrange("p e n -> p (e n)"), hid[:]).then_inc(Z["pick_ready"], 1)
            then(dve.tensor_copy(b3[:, 0, :], braw2[:]))
            then(dve.tensor_tensor(braw3[:], braw2[:], b3[:, 0, :], ALU.subtract))
            then(dve.tensor_copy(b3[:, 1, :], braw3[:]))
            then(dve.tensor_tensor(braw2[:], braw3[:], b3[:, 1, :], ALU.subtract))
            dve.tensor_copy(b3[:, 2, :], braw2[:]).then_inc(Z["bias_parts"], 1)
            dve.wait_ge(Z["g_act"], 1)
            then(dve.tensor_reduce(gsum[:], gexp[:], AX.X, ALU.add))
            dve.reciprocal(score[:], gsum[:]).then_inc(Z["g_score"], 1)

            def hidden_copy(j):
                if not (isinstance(j, int) and j == 0):
                    dve.wait_ge(Z["f_y"], j)
                for n in range(2):
                    dve.wait_ge(Z["f_hT"], 2 * j + n + 1)
                    dve.tensor_copy(hidT[:, 4 * n:4 * n + 4, :], U[1][:, n, :].rearrange("p (k t) -> p k t", t=P))\
                       .then_inc(Z["f_hTs"], 1)

            def y_copy(j):
                dve.wait_ge(Z["f_y"], j + 1)
                if not (isinstance(j, int) and j == 0):
                    dve.wait_ge(Z["f_ystored"], 16 * j)
                dve.tensor_copy(ysb[:], b5[:, 0:D]).then_inc(Z["f_ysb"], 1)

            hidden_copy(0)
            y_copy(0)
            with dve.Fori(1, TILES) as j:
                hidden_copy(j)
                y_copy(j)

            dve.wait_ge(Z["g_score"], 1)
            for b in range(B):
                n = b % NY
                dve.wait_ge(f_gaths[n], 16 * (b // NY + 1))
                dve.scalar_tensor_tensor(yg[n][:], yg[n][:], score[:, b:b + 1], x[:, b, :], ALU.mult, ALU.add)\
                   .then_inc(Z["f_out"], 1)

        @block.gpsimd
        def _(pool):
            pool.memset(ysb[:], 0.0).then_inc(Z["zero_ready"], 1)
            pool.memset(bias_rows[:], 0.0).then_inc(Z["zero_ready"], 1)

            def power(b, n, mult, add, v, r):
                pool.wait_ge(Z[("dve_st1", "dve_st2", "dve_st3")[n]], b + 1)
                pool.wait_ge(Z[("dve_xn1", "dve_xn2", "dve_keep3")[n]], b)
                plain(pool)
                pool.tensor_scalar(rs[:, n, 0:1], mv[:, n, 1:2], mult, add, ALU.mult, ALU.add).then_inc(Z[v], 1)
                pool.wait_ge(Z[v], b + 1)
                pool.tensor_tensor(rs[:, n, 1:2], rs[:, n, 0:1], neghalf[0:T, 0:1], ALU.pow).then_inc(Z[r], 1)

            def rstd1(b):
                power(b, 0, 1.0, 1e-5, "pool_v1", "pool_r1")

            def rstd2(b):
                power(b, 1, 1.0 + 1e-6, 1e-11, "pool_v2", "pool_r2")

            def rstd3(b):
                power(b, 2, 1.0, 1e-5, "pool_v3", "pool_r3")

            def rstd_ctx(b):
                pool.wait_ge(Z["act_sq"], KT * (b + 1))
                pool.wait_ge(Z["dve_vx"], b)
                pool.wait_ge(Z["c_krope"], 4 * b)
                plain(pool)
                pool.tensor_scalar(ssm[:], ss[:], 1.0 / D, 1e-6, ALU.mult, ALU.add).then_inc(Z["pool_vc"], 1)
                pool.wait_ge(Z["pool_vc"], b + 1)
                pool.tensor_tensor(rc[:], ssm[:], neghalf[0:KP, 0:KT], ALU.pow).then_inc(Z["pool_rc"], 1)

            def diag(b):
                pool.wait_ge(Z["pe_sexp"], KC * b)
                for c in range(KC):
                    pool.wait_ge(Z["dve_smax"], KC * b + c + 1)
                    plain(pool)
                    pool.affine_select(neg_diag[:, HC * c:HC * c + HC, :],
                                       nm[:, HC * c:HC * c + HC].unsqueeze(2).to_broadcast([T, HC, T]),
                                       [[0, HC], [1, T]], ALU.is_equal, 0.0, base=0, channel_multiplier=-1)\
                        .then_inc(Z["pool_D"], 1)

            def diagx(b):
                pool.wait_ge(Z["pe_xexp"], KT * b)
                pool.wait_ge(Z["dve_xmax"], 2 * (b + 1))
                plain(pool)
                pool.affine_select(neg_diagx.rearrange("p (g t) -> p g t", g=G),
                                   nmx[:].unsqueeze(2).to_broadcast([T, G, T]),
                                   [[0, G], [1, T]], ALU.is_equal, 0.0, base=0, channel_multiplier=-1)\
                    .then_inc(Z["pool_Dx"], 1)

            pool.wait_ge(Z["ones_ready"], 1)
            rstd1(0)
            diag(0)
            for e in range(E - LATE):
                pool.dma_start(w1[:, e, :, :], a["w1"][:, e]).then_inc(Z["ld_early"], 16)
                pool.dma_start(w2[:, e, :, :], a["w2"][:, e]).then_inc(Z["ld_early"], 16)
            rstd2(0)
            rstd1(1)
            pool.wait_ge(Z["setup_norm"], 1)
            pool.tensor_scalar(small[0:E, 10:11], neghalf[0:E, 0:1], -1.0, None, ALU.mult).then_inc(Z["c_pool"], 1)
            pool.wait_ge(Z["c_pool"], 1)
            pool.tensor_tensor(small[0:E, 7:8], small[0:E, 6:7], small[0:E, 10:11], ALU.pow)\
                .then_inc(Z["setup_pool"], 1)
            rstd_ctx(0)
            pool.wait_ge(Z["zero_ready"], 2)
            pool.dma_start(sorted_x.rearrange("(n p) d -> p n d", p=P),
                           ysb[:].unsqueeze(1).to_broadcast([P, TILES, D])).then_inc(Z["zero_sent"], 16)

            def iteration(i, first=False, last=False, ahead=True):
                if not first:
                    rstd3(i - 1)
                if not last:
                    rstd_ctx(i + 1)
                    diag(i + 1)
                diagx(i)
                if not last:
                    rstd2(i + 1)
                if ahead:
                    rstd1(i + 2)

            iteration(0, first=True)
            iteration(1)
            with pool.Fori(2, B - 2) as i:
                iteration(i)
            iteration(B - 2, ahead=False)
            iteration(B - 1, last=True, ahead=False)
            rstd3(B - 1)

            pool.wait_ge(Z["g_slots"], 1)
            pool.wait_ge(Z["zero_sent"], 16)
            for b in range(B):
                pool.wait_ge(Z["f_x3"], b + 1)
                pool.indirect_dma_start(out=sorted_x, out_offset=bass.IndirectOffsetOnAxis(ap=slot_i[:, b:b + 1], axis=0),
                                        in_=xs3[b % 4][:], in_offset=None).then_inc(f_x3s[b % 4], 16)
            pool.wait_ge(Z["f_ystored"], 16 * TILES)
            for b in range(B):
                n = b % NY
                if b >= NY:
                    pool.wait_ge(f_sts[n], 16 * (b // NY))
                pool.indirect_dma_start(out=yg[n][:], out_offset=None, in_=sorted_y,
                                        in_offset=bass.IndirectOffsetOnAxis(ap=slot_i[:, b:b + 1], axis=0))\
                    .then_inc(f_gaths[n], 16)


def kernel(**inputs):
    import numpy as _np
    import concourse.bacc as _bacc
    from concourse import mybir as _mybir
    from concourse.bass_utils import run_bass_kernel_spmd as _run

    g = {k: _np.asarray(v) for k, v in inputs.items()}

    def chunks(w):
        return _np.ascontiguousarray(w.reshape(KC, P, -1).transpose(1, 0, 2))

    arrays = {
        "x": g["x"],
        "ctx": _np.ascontiguousarray(g["ctx_1024"].reshape(B, KT, KP, D).transpose(0, 2, 1, 3)),
        "ctxT": _np.ascontiguousarray(g["ctx_1024"].transpose(0, 2, 1).reshape(B, KC, P, S).transpose(0, 2, 1, 3)),
        "mask": g["mask_BxS2_bk0"].reshape(B, 1, S),
        "wqk": chunks(_np.concatenate([g["L0_attn_Wq"].T, g["L0_attn_Wk"].T], 1)),
        "wv": chunks(g["L0_attn_Wv"].T),
        "rms": _np.ascontiguousarray(g["L0_xattn_rms_scale"].reshape(KC, P).T),
        "wxq": chunks(g["L0_xattn_q_w"].transpose(1, 0, 2).reshape(D, G * GD)),
        "wkv": chunks(_np.concatenate([g["L0_xattn_kv_w"][0, 0], g["L0_xattn_kv_w"][1, 0]], 1)),
        "wo": chunks(g["L0_xattn_out_w"].reshape(G * GD, D)),
        "wred": chunks(g["L0_ffn_w_red"]),
        "wg": g["L0_ffn_wg"],
        "w1": _np.ascontiguousarray(g["L0_ffn_w1"].reshape(E, KC, P, F).transpose(2, 0, 1, 3)),
        "b1": g["L0_ffn_b1"],
        "w2": _np.ascontiguousarray(g["L0_ffn_w2"].reshape(E, FC, P, D).transpose(2, 0, 1, 3)),
        "b2": g["L0_ffn_b2"],
    }
    consts = constants()
    consts["pick"] = consts["pick"].reshape(P, E * P)
    arrays.update(consts)
    nc = _bacc.Bacc("TRN2", target_bir_lowering=False, num_devices=1)
    feed, aps = {}, {}
    for name, v in arrays.items():
        v = _np.ascontiguousarray(v)
        feed[f"in_{name}"] = v
        aps[name] = nc.dram_tensor(f"in_{name}", v.shape, _mybir.dt.from_np(v.dtype), kind="ExternalInput").ap()
    out = nc.dram_tensor("out_x", (B, T, D), F32, kind="ExternalOutput").ap()
    decoder(nc, aps, out)
    r = _run(nc, [feed], core_ids=[0])
    return r.results[0]["out_x"]
```

```python
from contextlib import ExitStack

import numpy as np

import concourse.bass as bass
from concourse import mybir

F32 = mybir.dt.float32
BF16 = mybir.dt.bfloat16
I32 = mybir.dt.int32
U8 = mybir.dt.uint8
ALU = mybir.AluOpType
ACT = mybir.ActivationFunctionType
AX = mybir.AxisListType

P = 128
B, T, D = 32, 112, 256
S = 375
KT, KP = 3, 125
KC = D // P
H, HD = 16, 16
HC = P // HD
G, GD = 4, 64
E, F = 8, 1024
FC = F // P
NB = 512
TILES = B * T // P + E - 1
BIG = 2.0 ** 100
ARENA = 9600
PIECES = 20
LATE = 3
R = GD + 1


def constants():
    half = GD // 2
    timescale = (np.float32(10000.0) ** (np.float32(2.0 / GD) * np.arange(half, dtype=np.float32))).astype(np.float32)
    def table(pos):
        rad = (pos.astype(np.float32)[:, None] / timescale[None, :]).astype(np.float32)
        s, c = np.sin(rad).astype(np.float32), np.cos(rad).astype(np.float32)
        return np.concatenate([c, c, -s, s], 1)
    ropeq = table(np.arange(S, S + T))
    ropek = table(np.arange(S)).reshape(KT, KP, 4 * half).transpose(1, 0, 2)
    p = np.arange(P)
    f = lambda a: np.ascontiguousarray(a, dtype=np.float32)
    misc = np.zeros((P, 8 + 8 + 28 + 256 + 8 + 36 + 112), np.float32)
    misc[:, 0:8] = p[:, None] // HD == np.arange(HC)[None]
    misc[:, 8:16] = np.arange(E)[None] - E
    misc[:, 16:44] = P * np.arange(28)[None]
    misc[:, 44:300] = (np.arange(256) % B != 0)[None]
    misc[:, 300:308] = (np.arange(E) != 0)[None]
    misc[:, 308:344] = np.arange(36)[None]
    misc[:T, 344:456] = (np.arange(T)[:, None] < np.arange(T)[None])
    pick = np.zeros((P, E, P), np.float32)
    for e in range(E):
        pick[3 * e:3 * e + 3, e] = 1.0
    return {"ropeq": f(ropeq), "ropek": f(ropek), "misc": f(misc), "pick": f(pick), "ident": f(np.eye(P))}


def decoder(nc, a, out):
    with ExitStack() as ctx:
        def sb(name, shape, dt=F32):
            return ctx.enter_context(nc.sbuf_tensor(name, shape, dt))

        def psum(name, shape, dt=F32):
            return ctx.enter_context(nc.psum_tensor(name, shape, dt))

        def sem(name):
            return ctx.enter_context(nc.semaphore(name))

        sorted_x = nc.dram_tensor("sorted_x", [TILES * P, D], F32, kind="Internal").ap()
        sorted_y = nc.dram_tensor("sorted_y", [TILES * P, D], F32, kind="Internal").ap()

        x = sb("x", [T, B, D])
        w1 = sb("w1", [P, E, KC, F])
        w2 = sb("w2", [P, E, FC, D])
        ident = sb("ident", [P, P])
        misc = sb("misc", [P, 456])
        head_of = misc[:, 0:8]
        logits = sb("logits", [T, B, E])
        mean_rstd3 = sb("mean_rstd3", [T, B, 2])
        bias_rows = sb("bias_rows", [P, F + D], BF16)
        pick = sb("pick", [P, E, P], BF16)
        small = sb("small", [P, 64])
        ones = sb("ones", [P, P], BF16)
        neghalf = sb("neghalf", [P, KT])
        score = sb("score", [T, B])
        tri = sb("tri", [T, T], BF16)
        ones_f = sb("ones_f", [T, E])
        slot_i = sb("slot_i", [T, B], I32)
        ysb = sb("ysb", [P, D])
        arena = sb("arena", [P, ARENA])
        used = [0]

        def carve(rows, shape, dt=F32):
            n = int(np.prod(shape))
            words = (n * (1 if dt == U8 else 2 if dt == BF16 else 4) + 3) // 4
            v = arena[0:rows, used[0]:used[0] + words]
            used[0] += words
            assert used[0] <= ARENA, used
            if dt != F32:
                v = v.bitcast(dt)[:, 0:n]
            names = "abc"[0:len(shape)]
            if len(shape) == 1:
                return v
            return v.rearrange("p (" + " ".join(names) + ") -> p " + " ".join(names),
                               **{k: s for k, s in zip(names, shape)})

        wkv = carve(P, [KC, 2 * GD])
        wred = carve(P, [KC, HD])
        wgT = carve(HD, [E])
        ropeq = carve(T, [2 * GD])
        ropek = carve(KP, [KT, 2 * GD])
        xn = carve(T, [D])
        xnT = carve(P, [KC, T])
        kT = carve(P, [KC, T])
        v1 = carve(T, [H, HD + 1])
        kxT = carve(R, [S])
        qxT = carve(R, [G * T])
        vx = carve(KP, [KT, R])
        mask_row = carve(R, [S], U8)
        nm = carve(T, [H])
        nmx = carve(T, [G])
        ctxn = carve(KP, [KT, D])
        xn2 = carve(T, [D])
        xn2T = carve(P, [KC, T])
        xn3 = carve(T, [D])
        xn3T = carve(P, [KC, T])
        tmp1 = carve(T, [D])
        ropea = carve(T, [D])
        ropeb = carve(T, [D])
        qrot = carve(T, [D])
        kraw = carve(KP, [KT, GD])
        kra = carve(KP, [KT, GD])
        krb = carve(KP, [KT, GD])
        krot = carve(KP, [KT, GD])
        enc = carve(T, [D])
        encT = carve(P, [KC, T])
        redT = carve(HD, [T])
        stats = carve(T, [3, 6])
        mv = carve(T, [3, 2])
        rs = carve(T, [3, 2])
        ss = carve(KP, [KT])
        ssm = carve(KP, [KT])
        rc = carve(KP, [KT])
        den = carve(T, [H])
        denx = carve(T, [G])
        late = [w1[:, E - LATE:E, :, :].rearrange("p e k f -> p (e k f)"),
                w2[:, E - LATE:E, :, :].rearrange("p e k f -> p (e k f)")]
        taken = [0, 0]

        def over(where, rows, n):
            v = late[where][0:rows, taken[where]:taken[where] + n]
            taken[where] += n
            assert taken[where] <= LATE * KC * F
            return v

        qexp = [over(0, P, HC * T).rearrange("p (h t) -> p h t", h=HC) for _ in range(KC)]
        prob = over(0, T, H * T).rearrange("p (h t) -> p h t", h=H)
        neg_diag = over(1, T, H * T // 2).bitcast(BF16).rearrange("p (h t) -> p h t", h=H)
        probx = over(1, KP, KT * G * T).rearrange("p (k n) -> p k n", k=KT)
        neg_diagx = over(1, T, G * T // 2).bitcast(BF16)
        ctxT = over(1, P, KC * S).rearrange("p (k s) -> p k s", k=KC)
        square = over(1, KP, D)
        wqk, wv, wxq, wo = (over(0, P, KC * n).rearrange("p (c n) -> p c n", c=KC) for n in (2 * D, D, D, D))
        used[0] = 0
        gmax = carve(T, [B])
        gdiff = carve(T, [B, E])
        gexp = carve(T, [B, E])
        gsum = carve(T, [B])
        cand = carve(T, [B, E])
        best = carve(T, [B])
        onehot = carve(T, [B, E])
        onehot_b = carve(T, [E, B], BF16)
        totals = carve(T, [E * B])
        running = carve(T, [E * B])
        place = carve(T, [E, B])
        over_t = carve(T, [E, 28])
        tiles_e = carve(T, [E])
        ends = carve(T, [E])
        starts = carve(T, [E])
        slot = carve(T, [B])
        past = carve(1, [36, E])
        tile_e = carve(1, [36])
        tile_e_i = carve(1, [36], I32)
        xs3 = [carve(T, [D]) for n in range(4)]
        hid = carve(P, [F])
        shared = used[0]
        b3 = carve(E, [3, F + D], BF16)
        braw2 = carve(E, [F + D])
        braw3 = carve(E, [F + D])
        used[0] = shared
        xs = carve(P, [D])
        xsT = carve(P, [KC, P])
        hidT = carve(P, [FC, P])
        NY = 4
        yg = [carve(T, [D]) for n in range(NY)]

        bank = [psum(f"bank{n}", [P, NB]) for n in range(4, 8)]
        b4, b5, b6, b7 = bank
        U = [psum(f"pair{n}", [P, 2, NB]) for n in range(2)]
        xT_ps = b4[:, 0:KC * T].rearrange("p (k t) -> p k t", k=KC)
        x2T_ps = xT_ps
        q_ps = b4[0:T, 0:D]
        qxT_ps = b4[0:GD, 0:G * T]
        pvx_ps = b5[0:T, 0:G * R].rearrange("p (g r) -> p g r", g=G)
        encT_ps = b5[:, 0:KC * T].rearrange("p (k t) -> p k t", k=KC)
        out_ps = b5[0:T, 0:D]
        qk_ps = b6[:, 0:4 * T].rearrange("p (k t) -> p k t", k=4)
        v_ps = b6[0:T, 0:D]
        pv_ps = b6[0:T, 0:H * (HD + 1)].rearrange("p (h r) -> p h r", h=H)
        kv_ps = b7[0:KP, 0:KT * 2 * GD].rearrange("p (k n) -> p k n", k=KT)
        kxT_ps = b7[0:GD, 0:S]
        x3T_ps = b7[:, 0:KC * T].rearrange("p (k t) -> p k t", k=KC)
        redT_ps = b7[0:HD, 0:T]
        logit_ps = b7[0:T, 0:E]

        S_ = {}

        def s(name):
            if name not in S_:
                S_[name] = sem(name)
            return S_[name]

        names = ["ld_const", "ld_w", "ld_x", "ld_ctxn", "ld_ctxT", "ld_mask", "ld_early", "ld_late", "zero_ready", "zero_sent",
                 "ones_ready", "weights_ready", "setup_dve", "setup_pe", "setup_pool", "setup_act",
                 "pe_xT", "pe_x2T", "pe_qk", "pe_v", "pe_q", "pe_smax", "pe_qT", "pe_xmax", "pe_sexp", "pe_x3T",
                 "pe_xexp", "pe_red", "pe_pv", "pe_logit", "pe_xpv", "pe_kv", "pe_encT", "pe_kT", "pe_out",
                 "act_xT", "act_x2T", "act_kT", "act_v", "act_qT", "act_sexp", "act_x3T", "act_xexp", "act_red",
                 "act_sq", "act_kxT", "act_encT",
                 "dve_qexp", "dve_rope", "dve_x3", "dve_smax", "dve_xmax", "dve_x1", "dve_bn2", "dve_bn1", "dve_bn3",
                 "dve_st2", "dve_st1", "dve_st3", "dve_xn2", "dve_xn1", "dve_enc", "dve_logit", "dve_krope",
                 "act_vx", "act_kraw", "dve_x2", "dve_keep3", "c_rope", "c_krope", "c_x1", "c_enc",
                 "pool_v1", "pool_r1", "pool_v2", "pool_r2", "pool_v3", "pool_r3", "pool_vc", "pool_rc", "pool_D",
                 "pool_Dx", "act_mask",
                 "g_dve", "g_act", "g_pe", "g_scatter", "f_x3", "f_xs", "f_xT", "f_xsT", "f_h", "f_gelu", "c_setup", "bias_sent", "pick_ready", "c_route", "setup_norm", "bias_parts", "g_diff", "g_slots", "g_score", "c_pool", "ld_bias", "f_hT",
                 "f_hTs", "f_y", "f_ysb", "f_ystored", "f_gath", "f_out", "f_stored"]
        for n in names:
            s(n)
        Z = S_
        f_x3s = [sem(f"f_x3sent{n}") for n in range(4)]
        f_gaths = [sem(f"f_gathered{n}") for n in range(NY)]
        f_sts = [sem(f"f_stored{n}") for n in range(NY)]
        block = ctx.enter_context(nc.Block())

        def plain(eng):
            eng.nop(nofuse=True)

        @block.sync
        def _(sp):
            for dst, name in ((ident[:], "ident"), (misc[:], "misc"), (wqk, "wqk"), (wv, "wv")):
                sp.dma_start(dst, a[name]).then_inc(Z["ld_const"], 16)
            sp.dma_start(x[:, 0, :], a["x"][0]).then_inc(Z["ld_x"], 16)
            for dst, name in ((ropeq, "ropeq"), (ropek, "ropek"), (wxq, "wxq"), (wkv, "wkv"),
                              (wo, "wo"), (wred, "wred")):
                sp.dma_start(dst, a[name]).then_inc(Z["ld_w"], 16)
            sp.dma_start(small[:, 0:2], a["rms"]).then_inc(Z["ld_w"], 16)
            sp.dma_start(small[0:E, 16:32], a["wg"]).then_inc(Z["ld_w"], 16)

            def context(b):
                sp.wait_ge(Z["pe_kv"], b)
                sp.dma_start(ctxT, a["ctxT"][b]).then_inc(Z["ld_ctxT"], 16)
                sp.wait_ge(Z["act_mask"], b)
                plain(sp)
                sp.dma_start(mask_row[GD:R, :], a["mask"][b]).then_inc(Z["ld_mask"], 16)

            def context_rows(b):
                sp.wait_ge(Z["act_sq"], KT * b)
                sp.dma_start(ctxn[:], a["ctx"][b]).then_inc(Z["ld_ctxn"], 16)

            def tokens(b):
                sp.wait_ge(Z["ld_x"], 16 * b)
                sp.dma_start(x[:, b, :], a["x"][b]).then_inc(Z["ld_x"], 16)

            w1_early, w2_early = (w[:, 0:E - LATE, :, :].rearrange("p e k f -> p (e k f)") for w in (w1, w2))
            w1_from, w2_from = (a[n][:, 0:E - LATE].rearrange("p e k f -> p (e k f)") for n in ("w1", "w2"))
            PIECE = (E - LATE) * KC * F // PIECES

            def weights(n):
                at = bass.ds(n * PIECE, PIECE)
                sp.dma_start(w1_early[:, at], w1_from[:, at]).then_inc(Z["ld_early"], 16)
                sp.dma_start(w2_early[:, at], w2_from[:, at]).then_inc(Z["ld_early"], 16)

            context_rows(0)
            tokens(1)
            context(0)
            context_rows(1)
            tokens(2)
            with sp.Fori(1, PIECES + 1) as b:
                context(b)
                context_rows(b + 1)
                tokens(b + 2)
                weights(b - 1)
            with sp.Fori(PIECES + 1, B - 2) as b:
                context(b)
                context_rows(b + 1)
                tokens(b + 2)
            context(B - 2)
            context_rows(B - 1)
            context(B - 1)
            sp.wait_ge(Z["dve_logit"], B)
            sp.dma_start(w1[:, E - LATE:E, :, :], a["w1"][:, E - LATE:E]).then_inc(Z["ld_late"], 16)
            sp.dma_start(w2[:, E - LATE:E, :, :], a["w2"][:, E - LATE:E]).then_inc(Z["ld_late"], 16)

            sp.wait_ge(Z["g_dve"], 1)
            sp.dma_start(hid[:, :], a["pick"]).then_inc(Z["ld_bias"], 16)
            sp.dma_start(braw2[:, 0:F], a["b1"]).then_inc(Z["ld_bias"], 16)
            sp.dma_start(braw2[:, F:F + D], a["b2"]).then_inc(Z["ld_bias"], 16)
            sp.wait_ge(Z["bias_parts"], 1)
            for part in range(3):
                sp.dma_start(bias_rows[part:3 * E:3, :], b3[:, part, :]).then_inc(Z["bias_sent"], 16)

            sp.wait_ge(Z["bias_sent"], 48)
            for n in range(4):
                sp.wait_ge(f_x3s[n], 16 * (B // 4))

            sp.dma_start(xs[:], sorted_x[0:P, :]).then_inc(Z["f_xs"], 16)
            with sp.Fori(1, TILES) as j:
                sp.wait_ge(Z["f_xT"], j)
                sp.dma_start(xs[:], sorted_x[bass.ds(j * P, P), :]).then_inc(Z["f_xs"], 16)

            for b in range(B):
                sp.wait_ge(Z["f_out"], b + 1)
                sp.dma_start(out[b], yg[b % NY][:]).then_inc(f_sts[b % NY], 16)
            for n in range(NY):
                sp.wait_ge(f_sts[n], 16 * (B // NY))
            sp.wait_ge(Z["zero_sent"], 16)

        @block.tensor
        def _(pe):
            def turn(dst, src, rows, cols):
                plain(pe)
                return pe.transpose(dst, src, ident[0:rows, 0:rows])

            def kv(b):
                pe.wait_ge(Z["ld_ctxT"], 16 * (b + 1))
                if not isinstance(b, int) or b > 2:
                    pe.wait_ge(Z["dve_logit"], b - 2)
                for t in range(KT):
                    for c in range(KC):
                        mm = pe.matmul(kv_ps[:, t, :], ctxT[:, c, KP * t:KP * t + KP], wkv[:, c, :],
                                       start=(c == 0), stop=(c == KC - 1))
                mm.then_inc(Z["pe_kv"], 1)

            def k_turn(b):
                pe.wait_ge(Z["dve_krope"], b + 1)
                pe.wait_ge(Z["act_vx"], b + 1)
                for t in range(KT):
                    mm = turn(kxT_ps[:, KP * t:KP * t + KP], krot[:, t, :], KP, GD)
                mm.then_inc(Z["pe_kT"], 1)

            def x_turn(b):
                pe.wait_ge(Z["dve_xn1"], b + 1)
                if not isinstance(b, int) or b > 1:
                    pe.wait_ge(Z["act_qT"], b - 1)
                for c in range(KC):
                    mm = turn(xT_ps[:, c, :], xn[:, P * c:P * c + P], T, P)
                mm.then_inc(Z["pe_xT"], 1)

            def x2_turn(b):
                pe.wait_ge(Z["dve_xn2"], b + 1)
                pe.wait_ge(Z["act_qT"], b)
                for c in range(KC):
                    mm = turn(x2T_ps[:, c, :], xn2[:, P * c:P * c + P], T, P)
                mm.then_inc(Z["pe_x2T"], 1)

            def qk(b):
                pe.wait_ge(Z["act_xT"], b + 1)
                pe.wait_ge(Z["dve_x1"], b)
                for o in range(4):
                    for c in range(KC):
                        mm = pe.matmul(qk_ps[:, o, :], wqk[:, c, P * o:P * o + P], xnT[:, c, :],
                                       start=(c == 0), stop=(c == KC - 1))
                mm.then_inc(Z["pe_qk"], 1)

            def v(b):
                pe.wait_ge(Z["dve_qexp"], KC * (b + 1))
                for c in range(KC):
                    mm = pe.matmul(v_ps, xnT[:, c, :], wv[:, c, :], start=(c == 0), stop=(c == KC - 1))
                mm.then_inc(Z["pe_v"], 1)

            def q_proj(b):
                pe.wait_ge(Z["act_x2T"], b + 1)
                for c in range(KC):
                    mm = pe.matmul(q_ps, xn2T[:, c, :], wxq[:, c, :], start=(c == 0), stop=(c == KC - 1))
                mm.then_inc(Z["pe_q"], 1)

            def top(ap):
                return ap.bitcast(BF16)[:, 1::2]

            def self_max(b, c):
                pe.wait_ge(Z["act_kT"], b + 1)
                pe.wait_ge(Z["dve_qexp"], KC * b + c + 1)
                if not isinstance(b, int) or b > 1:
                    pe.wait_ge(Z["act_xexp"], KT * (b - 1))
                for h in range(HC):
                    mm = pe.matmul(U[c][0:T, h // 4, (h % 4) * T:(h % 4 + 1) * T], top(qexp[c][:, h, :]),
                                   top(kT[:, c, :]), start=True, stop=True)
                mm.then_inc(Z["pe_smax"], 1)

            def q_turn(b):
                pe.wait_ge(Z["dve_rope"], b + 1)
                for g in range(G):
                    mm = turn(qxT_ps[:, g * T:(g + 1) * T], qrot[:, g * GD:(g + 1) * GD], T, GD)
                mm.then_inc(Z["pe_qT"], 1)

            def cross_max(b, S_on):
                pe.wait_ge(Z["act_qT"], b + 1)
                pe.wait_ge(Z["act_kxT"], b + 1)
                pe.wait_ge(Z["act_mask"], b + 1)
                for u in range(2):
                    if S_on:
                        pe.wait_ge(Z["dve_smax"], KC * (b + 1) + u + 1)
                    for n in range(2):
                        g = 2 * u + n
                        mm = pe.matmul(U[u][0:T, n, 0:S], top(qxT[:, g * T:(g + 1) * T]), top(kxT[:, :]),
                                       start=True, stop=True)
                    mm.then_inc(Z["pe_xmax"], 1)

            def self_exp(b):
                for c in range(KC):
                    pe.wait_ge(Z["pool_D"], KC * b + c + 1)
                    if not isinstance(b, int) or b > 0:
                        pe.wait_ge(Z["dve_xmax"], 2 * (b - 1) + c + 1)
                    for n in range(2):
                        dst = U[c][0:T, n, 0:4 * T]
                        pe.matmul(dst, kT[:, c, :], qexp[c][:, 4 * n:4 * n + 4, :], start=True, stop=False)
                        mm = pe.matmul(dst, ones[0:T, 0:T],
                                       neg_diag[:, HC * c + 4 * n:HC * c + 4 * n + 4, :], start=False, stop=True)
                    mm.then_inc(Z["pe_sexp"], 1)

            def cross_exp(b, S_on):
                pe.wait_ge(Z["pool_Dx"], b + 1)
                for t in range(KT):
                    if S_on:
                        pe.wait_ge(Z["act_sexp"], KC * (b + 1) + t // 2 + 1)
                    dst = U[t // 2][0:KP, t % 2, 0:G * T]
                    pe.matmul(dst, kxT[:, KP * t:KP * t + KP], qxT[:, :], start=True, stop=False)
                    mm = pe.matmul(dst, ones[0:T, 0:KP], neg_diagx, start=False, stop=True)
                    mm.then_inc(Z["pe_xexp"], 1)

            def self_pv(b):
                pe.wait_ge(Z["act_v"], b + 1)
                for c in range(KC):
                    pe.wait_ge(Z["act_sexp"], KC * b + c + 1)
                    for h in range(HC * c, HC * c + HC):
                        mm = pe.matmul(pv_ps[:, h, :], prob[:, h, :], v1[:, h, :], start=True, stop=True)
                mm.then_inc(Z["pe_pv"], 1)

            def cross_pv(b):
                pe.wait_ge(Z["act_xexp"], KT * (b + 1))
                pe.wait_ge(Z["dve_x2"], b)
                for g in range(G):
                    for t in range(KT):
                        mm = pe.matmul(pvx_ps[:, g, :], probx[:, t, g * T:(g + 1) * T], vx[:, t, :],
                                       start=(t == 0), stop=(t == KT - 1))
                mm.then_inc(Z["pe_xpv"], 1)

            def enc_turn(b):
                pe.wait_ge(Z["dve_enc"], b + 1)
                for c in range(KC):
                    mm = turn(encT_ps[:, c, :], enc[:, P * c:P * c + P], T, P)
                mm.then_inc(Z["pe_encT"], 1)

            def out_proj(b):
                pe.wait_ge(Z["act_encT"], b + 1)
                for c in range(KC):
                    mm = pe.matmul(out_ps, encT[:, c, :], wo[:, c, :], start=(c == 0), stop=(c == KC - 1))
                mm.then_inc(Z["pe_out"], 1)

            def x3_turn(b):
                pe.wait_ge(Z["dve_x3"], b + 1)
                pe.wait_ge(Z["dve_logit"], b)
                for c in range(KC):
                    mm = turn(x3T_ps[:, c, :], xn3[:, P * c:P * c + P], T, P)
                mm.then_inc(Z["pe_x3T"], 1)

            def router_red(b):
                pe.wait_ge(Z["act_x3T"], b + 1)
                for c in range(KC):
                    mm = pe.matmul(redT_ps, wred[:, c, :], xn3T[:, c, :], start=(c == 0), stop=(c == KC - 1))
                mm.then_inc(Z["pe_red"], 1)

            def router_logits(b):
                pe.wait_ge(Z["act_red"], b + 1)
                pe.matmul(logit_ps, redT[:, :], wgT[:, :], start=True, stop=True).then_inc(Z["pe_logit"], 1)

            pe.wait_ge(Z["ld_const"], 16 * 4)
            pe.wait_ge(Z["ones_ready"], 1)
            def iteration(i, S_on=True, C_on=True, L_on=True, R_on=True):
                S, C, L, R = i + 1, i, i - 1, i - 2
                if S_on:
                    x_turn(S)
                if L_on:
                    cross_pv(L)
                if S_on:
                    qk(S)
                if C_on:
                    x2_turn(C)
                    kv(C)
                    q_proj(C)
                if S_on:
                    self_max(S, 0)
                if L_on:
                    enc_turn(L)
                if S_on:
                    self_max(S, 1)
                if C_on:
                    k_turn(C)
                if S_on:
                    v(S)
                if C_on:
                    q_turn(C)
                if L_on:
                    out_proj(L)
                if C_on:
                    cross_max(C, S_on)
                if R_on:
                    x3_turn(R)
                if S_on:
                    self_exp(S)
                if R_on:
                    router_red(R)
                if C_on:
                    cross_exp(C, S_on)
                if R_on:
                    router_logits(R)
                if S_on:
                    self_pv(S)

            iteration(-1, C_on=False, L_on=False, R_on=False)
            pe.wait_ge(Z["weights_ready"], 1)
            turn(b7[0:HD, 0:E], small[0:E, 32:48], E, HD).then_inc(Z["setup_pe"], 1)
            pe.wait_ge(Z["setup_dve"], 1)
            iteration(0, L_on=False, R_on=False)
            iteration(1, R_on=False)
            iteration(2)
            with pe.Fori(3, B - 1) as i:
                iteration(i)
            iteration(B - 1, S_on=False)
            iteration(B, S_on=False, C_on=False)
            iteration(B + 1, S_on=False, C_on=False, L_on=False)

            pe.wait_ge(Z["g_dve"], 1)
            pe.matmul(U[0][0:T, 0, 0:E * B], tri[:, :], onehot_b[:], start=True, stop=True)
            pe.matmul(U[0][0:T, 1, 0:E * B], ones[0:T, 0:T], onehot_b[:], start=True, stop=True)\
              .then_inc(Z["g_pe"], 1)

            h_ps = U[0][:, :, :].rearrange("p a n -> p (a n)")
            hT_ps = U[1][:, :, :].rearrange("p a (k t) -> p (a k) t", t=P)
            xsT_ps = b4[:, 0:KC * P].rearrange("p (k t) -> p k t", k=KC)
            y_ps = b5[:, 0:D]

            def expert(j):
                return pe.value_load(tile_e_i[0:1, bass.ds(j, 1)], min_val=0, max_val=E - 1)

            def tile_turn(j):
                pe.wait_ge(Z["f_xs"], 16 * (j + 1))
                for c in range(KC):
                    mm = pe.transpose(xsT_ps[:, c, :], xs[:, P * c:P * c + P], ident[:, :])
                mm.then_inc(Z["f_xT"], 1)

            def up(j, e):
                pe.wait_ge(Z["f_xsT"], j + 1)
                pe.wait_ge(Z["f_gelu"], 2 * j)
                for n in range(2):
                    for c in range(KC):
                        pe.matmul(h_ps[:, NB * n:NB * n + NB], xsT[:, c, :], w1[:, e, c, NB * n:NB * n + NB],
                                  start=(c == 0), stop=False)
                    pe.matmul(h_ps[:, NB * n:NB * n + NB], pick[:, e, :], bias_rows[:, NB * n:NB * n + NB],
                              start=False, stop=True).then_inc(Z["f_h"], 1)

            def hidden_turn(j):
                for n in range(2):
                    pe.wait_ge(Z["f_gelu"], 2 * j + n + 1)
                    pe.wait_ge(Z["f_hTs"], 2 * j)
                    for k in range(4 * n, 4 * n + 4):
                        mm = pe.transpose(hT_ps[:, k, :], hid[:, P * k:P * k + P], ident[:, :])
                    mm.then_inc(Z["f_hT"], 1)

            def down(j, e):
                pe.wait_ge(Z["f_ysb"], j)
                pe.matmul(y_ps, pick[:, e, :], bias_rows[:, F:F + D], start=True, stop=False)
                for k in range(FC):
                    if k % 4 == 0:
                        pe.wait_ge(Z["f_hTs"], 2 * j + k // 4 + 1)
                    mm = pe.matmul(y_ps, hidT[:, k, :], w2[:, e, k, :], start=False, stop=(k == FC - 1))
                mm.then_inc(Z["f_y"], 1)

            pe.wait_ge(Z["g_dve"], 2)
            pe.wait_ge(Z["ld_late"], 32)
            pe.wait_ge(Z["ld_early"], 16 * 2 * PIECES)
            pe.wait_ge(Z["bias_sent"], 48)
            pe.wait_ge(Z["pick_ready"], 1)
            tile_turn(0)
            up(0, expert(0))
            tile_turn(1)

            def tile(j, ahead=True):
                hidden_turn(j)
                up(j + 1, expert(j + 1))
                down(j, expert(j))
                if ahead:
                    tile_turn(j + 2)

            tile(0)
            with pe.Fori(1, TILES - 2) as j:
                tile(j)
            tile(TILES - 2, ahead=False)
            hidden_turn(TILES - 1)
            down(TILES - 1, expert(TILES - 1))

        @block.scalar
        def _(act):
            def copy(dst, src):
                return act.activation(dst, src, ACT.Copy)

            def squares(b):
                act.wait_ge(Z["ld_ctxn"], 16 * (b + 1))
                act.wait_ge(Z["pool_vc"], b)
                for t in range(KT):
                    if not (isinstance(b, int) and b == 0 and t == 0):
                        act.wait_ge(Z["act_sq"], KT * b + t)
                    act.activation(square, ctxn[:, t, :], ACT.Square, accum_out=ss[:, t:t + 1])\
                       .then_inc(Z["act_sq"], 1)

            def x_copy(b):
                act.wait_ge(Z["pe_xT"], b + 1)
                act.wait_ge(Z["pe_v"], b)
                copy(xnT[:], xT_ps).then_inc(Z["act_xT"], 1)

            def x2_copy(b):
                act.wait_ge(Z["pe_x2T"], b + 1)
                act.wait_ge(Z["pe_q"], b)
                copy(xn2T[:], x2T_ps).then_inc(Z["act_x2T"], 1)

            def kT_copy(b):
                act.wait_ge(Z["pe_qk"], b + 1)
                act.wait_ge(Z["pe_sexp"], KC * b)
                copy(kT[:], qk_ps[:, KC:2 * KC, :]).then_inc(Z["act_kT"], 1)

            def v_copy(b):
                act.wait_ge(Z["pe_v"], b + 1)
                act.wait_ge(Z["pe_pv"], b)
                copy(v1[:, :, 0:HD], v_ps.rearrange("p (h d) -> p h d", h=H)).then_inc(Z["act_v"], 1)

            def kv_copy(b):
                act.wait_ge(Z["pe_kv"], b + 1)
                act.wait_ge(Z["pool_rc"], b + 1)
                act.wait_ge(Z["c_krope"], 3 * b)
                for t in range(KT):
                    k = act.activation(kraw[:, t, :], kv_ps[:, t, 0:GD], ACT.Copy, scale=rc[:, t:t + 1])
                k.then_inc(Z["act_kraw"], 1)
                act.wait_ge(Z["pe_xpv"], b)
                for t in range(KT):
                    k = act.activation(vx[:, t, 0:GD], kv_ps[:, t, GD:2 * GD], ACT.Copy, scale=rc[:, t:t + 1])
                k.then_inc(Z["act_vx"], 1)

            def q_copy(b):
                act.wait_ge(Z["pe_qT"], b + 1)
                act.wait_ge(Z["pe_xexp"], KT * b)
                copy(qxT[0:GD, :], qxT_ps).then_inc(Z["act_qT"], 1)

            def self_exp(b):
                for c in range(KC):
                    act.wait_ge(Z["pe_sexp"], KC * b + c + 1)
                    act.wait_ge(Z["pe_pv"], b)
                    act.activation(prob[:, HC * c:HC * c + HC, :].rearrange("p (a h) t -> p a (h t)", a=2),
                                   U[c][0:T, :, 0:4 * T], ACT.Exp, scale=HD ** -0.5).then_inc(Z["act_sexp"], 1)

            def x3_copy(b):
                act.wait_ge(Z["pe_x3T"], b + 1)
                act.wait_ge(Z["pe_red"], b)
                copy(xn3T[:], x3T_ps).then_inc(Z["act_x3T"], 1)

            def cross_exp(b):
                act.wait_ge(Z["pe_xpv"], b)
                for t in range(KT):
                    act.wait_ge(Z["pe_xexp"], KT * b + t + 1)
                    act.activation(probx[:, t, :], U[t // 2][0:KP, t % 2, 0:G * T], ACT.Exp,
                                   scale=GD ** -0.5).then_inc(Z["act_xexp"], 1)

            def red_copy(b):
                act.wait_ge(Z["pe_red"], b + 1)
                act.wait_ge(Z["pe_logit"], b)
                copy(redT[:], redT_ps).then_inc(Z["act_red"], 1)

            def enc_copy(b):
                act.wait_ge(Z["pe_encT"], b + 1)
                act.wait_ge(Z["pe_out"], b)
                copy(encT[:], encT_ps).then_inc(Z["act_encT"], 1)

            def k_copy(b):
                act.wait_ge(Z["pe_kT"], b + 1)
                act.wait_ge(Z["pe_xexp"], KT * b)
                copy(kxT[0:GD, :], kxT_ps).then_inc(Z["act_kxT"], 1)
                act.wait_ge(Z["ld_mask"], 16 * (b + 1))
                act.activation(kxT[GD:R, :], mask_row[GD:R, :], ACT.Copy, bias=-BIG, scale=BIG)\
                   .then_inc(Z["act_mask"], 1)

            def iteration(i, S_on=True, C_on=True, L_on=True, R_on=True, next_on=True):
                S, C, L, R = i + 1, i, i - 1, i - 2
                if S_on:
                    x_copy(S)
                    kT_copy(S)
                if C_on:
                    x2_copy(C)
                    kv_copy(C)
                if L_on:
                    enc_copy(L)
                if C_on:
                    k_copy(C)
                if S_on:
                    v_copy(S)
                if C_on:
                    q_copy(C)
                if next_on:
                    squares(C + 1)
                if R_on:
                    x3_copy(R)
                if S_on:
                    self_exp(S)
                if R_on:
                    red_copy(R)
                if C_on:
                    cross_exp(C)

            act.wait_ge(Z["ones_ready"], 1)
            iteration(-1, C_on=False, L_on=False, R_on=False)
            iteration(0, L_on=False, R_on=False)
            iteration(1, R_on=False)
            iteration(2)
            with act.Fori(3, B - 1) as i:
                iteration(i)
            iteration(B - 1, S_on=False, next_on=False)
            iteration(B, S_on=False, C_on=False, next_on=False)
            iteration(B + 1, S_on=False, C_on=False, L_on=False, next_on=False)

            act.wait_ge(Z["g_diff"], 1)
            act.activation(gexp[:], gdiff[:], ACT.Exp).then_inc(Z["g_act"], 1)

            def tile_copy(j):
                act.wait_ge(Z["f_xT"], j + 1)
                if not (isinstance(j, int) and j == 0):
                    act.wait_ge(Z["f_h"], 2 * j)
                copy(xsT[:], b4[:, 0:KC * P].rearrange("p (k t) -> p k t", k=KC)).then_inc(Z["f_xsT"], 1)

            def gelu(j):
                if not (isinstance(j, int) and j == 0):
                    act.wait_ge(Z["f_hT"], 2 * j)
                for n in range(2):
                    act.wait_ge(Z["f_h"], 2 * j + n + 1)
                    act.activation(hid[:, NB * n:NB * n + NB], U[0][:, n, :], ACT.Gelu).then_inc(Z["f_gelu"], 1)

            tile_copy(0)
            gelu(0)
            tile_copy(1)
            with act.Fori(1, TILES - 1) as j:
                gelu(j)
                tile_copy(j + 1)
            gelu(TILES - 1)

        @block.vector
        def _(dve):
            def norm_stats(b, n):
                bn, st = (("dve_bn1", "dve_st1"), ("dve_bn2", "dve_st2"), ("dve_bn3", "dve_st3"))[n]
                plain(dve)
                dve.bn_stats(stats[:, n, :], x[:, b, :]).then_inc(Z[bn], 1)
                dve.wait_ge(Z[bn], b + 1)
                plain(dve)
                dve.bn_aggr(mv[:, n, :], stats[:, n, :]).then_inc(Z[st], 1)

            def norm_apply(b, n, dst, done):
                dve.wait_ge(Z[("pool_r1", "pool_r2", "pool_r3")[n]], b + 1)
                dve.tensor_scalar(dst[:], x[:, b, :], mv[:, n, 0:1], rs[:, n, 1:2], ALU.subtract, ALU.mult)\
                   .then_inc(Z[done], 1)

            def stats1(b):
                dve.wait_ge(Z["ld_x"], 16 * (b + 1))
                norm_stats(b, 0)

            def apply1(b):
                dve.wait_ge(Z["pe_xT"], b)
                norm_apply(b, 0, xn, "dve_xn1")

            def stats2(b):
                dve.wait_ge(Z["dve_x1"], b + 1)
                norm_stats(b, 1)

            def apply2(b):
                dve.wait_ge(Z["pe_x2T"], b)
                norm_apply(b, 1, xn2, "dve_xn2")

            def stats3(b):
                dve.wait_ge(Z["dve_x2"], b + 1)
                norm_stats(b, 2)

            def apply3(b):
                dve.wait_ge(Z["pe_x3T"], b)
                norm_apply(b, 2, xn3, "dve_x3")
                dve.tensor_copy(mean_rstd3[:, b, 0:1], mv[:, 2, 0:1])
                dve.tensor_copy(mean_rstd3[:, b, 1:2], rs[:, 2, 1:2]).then_inc(Z["dve_keep3"], 1)

            def q_expand(b):
                dve.wait_ge(Z["act_kT"], b + 1)
                dve.wait_ge(Z["pe_sexp"], KC * b)
                for c in range(KC):
                    dve.tensor_tensor(qexp[c], qk_ps[:, c, :].unsqueeze(1).to_broadcast([P, HC, T]),
                                      head_of.unsqueeze(2).to_broadcast([P, HC, T]), ALU.mult)\
                       .then_inc(Z["dve_qexp"], 1)

            def q_rope(b):
                dve.wait_ge(Z["pe_q"], b + 1)
                if not (isinstance(b, int) and b == 0):
                    dve.wait_ge(Z["pe_qT"], b)
                q4 = q_ps.rearrange("p (g d) -> p g d", g=G)
                a4 = ropea[:].rearrange("p (g d) -> p g d", g=G)
                r4 = ropeb[:].rearrange("p (g d) -> p g d", g=G)
                hf = GD // 2
                dve.tensor_tensor(a4, q4, ropeq[:, 0:GD].unsqueeze(1).to_broadcast([T, G, GD]), ALU.mult)\
                   .then_inc(Z["c_rope"], 1)
                dve.tensor_tensor(r4[:, :, 0:hf], q4[:, :, hf:GD],
                                  ropeq[:, GD:GD + hf].unsqueeze(1).to_broadcast([T, G, hf]), ALU.mult)\
                   .then_inc(Z["c_rope"], 1)
                dve.tensor_tensor(r4[:, :, hf:GD], q4[:, :, 0:hf],
                                  ropeq[:, GD + hf:2 * GD].unsqueeze(1).to_broadcast([T, G, hf]), ALU.mult)\
                   .then_inc(Z["c_rope"], 1)
                dve.wait_ge(Z["c_rope"], 3 * (b + 1))
                dve.tensor_tensor(qrot[:], ropea[:], ropeb[:], ALU.add).then_inc(Z["dve_rope"], 1)

            def self_max(b):
                for c in range(KC):
                    dve.wait_ge(Z["pe_smax"], KC * b + c + 1)
                    dve.wait_ge(Z["pool_D"], KC * b)
                    dve.tensor_reduce(nm[:, HC * c:HC * c + HC].rearrange("p (a h) -> p a h", a=2),
                                      U[c][0:T, :, 0:4 * T].rearrange("p a (h t) -> p a h t", t=T), AX.X, ALU.max,
                                      negate=True).then_inc(Z["dve_smax"], 1)

            def cross_max(b):
                dve.wait_ge(Z["pool_Dx"], b)
                for u in range(2):
                    dve.wait_ge(Z["pe_xmax"], 2 * b + u + 1)
                    dve.tensor_reduce(nmx[:, 2 * u:2 * u + 2], U[u][0:T, :, 0:S], AX.X, ALU.max, negate=True)\
                       .then_inc(Z["dve_xmax"], 1)

            def self_out(b):
                dve.wait_ge(Z["pe_pv"], b + 1)
                dve.reciprocal(den[:].unsqueeze(2), pv_ps[:, :, HD:HD + 1]).then_inc(Z["c_x1"], 1)
                dve.wait_ge(Z["c_x1"], 2 * b + 1)
                dve.tensor_tensor(tmp1[:].rearrange("p (h d) -> p h d", h=H), pv_ps[:, :, 0:HD],
                                  den[:].unsqueeze(2).to_broadcast([T, H, HD]), ALU.mult).then_inc(Z["c_x1"], 1)
                dve.wait_ge(Z["c_x1"], 2 * b + 2)
                dve.tensor_tensor(x[:, b, :], x[:, b, :], tmp1[:], ALU.add).then_inc(Z["dve_x1"], 1)

            def cross_enc(b):
                dve.wait_ge(Z["pe_xpv"], b + 1)
                dve.reciprocal(denx[:].unsqueeze(2), pvx_ps[:, :, GD:R]).then_inc(Z["c_enc"], 1)
                dve.wait_ge(Z["c_enc"], b + 1)
                dve.wait_ge(Z["pe_encT"], b)
                dve.tensor_tensor(enc[:].rearrange("p (g d) -> p g d", g=G), pvx_ps[:, :, 0:GD],
                                  denx[:].unsqueeze(2).to_broadcast([T, G, GD]), ALU.mult).then_inc(Z["dve_enc"], 1)

            def logits_out(b):
                dve.wait_ge(Z["pe_logit"], b + 1)
                dve.tensor_copy(logits[:, b, :], logit_ps).then_inc(Z["dve_logit"], 1)

            def k_rope(b):
                dve.wait_ge(Z["act_kraw"], b + 1)
                hf = GD // 2
                dve.tensor_tensor(kra[:], kraw[:], ropek[:, :, 0:GD], ALU.mult).then_inc(Z["c_krope"], 1)
                dve.tensor_tensor(krb[:, :, 0:hf], kraw[:, :, hf:GD], ropek[:, :, GD:GD + hf], ALU.mult)\
                   .then_inc(Z["c_krope"], 1)
                dve.tensor_tensor(krb[:, :, hf:GD], kraw[:, :, 0:hf], ropek[:, :, GD + hf:2 * GD], ALU.mult)\
                   .then_inc(Z["c_krope"], 1)
                dve.wait_ge(Z["c_krope"], 3 * b + 3)
                dve.wait_ge(Z["pe_kT"], b)
                dve.tensor_tensor(krot[:], kra[:], krb[:], ALU.add).then_inc(Z["dve_krope"], 1)

            def cross_out(b):
                dve.wait_ge(Z["pe_out"], b + 1)
                dve.tensor_tensor(x[:, b, :], out_ps, x[:, b, :], ALU.add).then_inc(Z["dve_x2"], 1)

            step = [0]

            def link(ins):
                step[0] += 1
                ins.then_inc(Z["c_setup"], 1)
                dve.wait_ge(Z["c_setup"], step[0])

            dve.memset(ones[:], 1.0)
            dve.memset(v1[:, :, HD:HD + 1], 1.0)
            dve.memset(vx[:, :, GD:R], 1.0)
            dve.memset(neghalf[:], -0.5)
            dve.memset(ones_f[:], 1.0)
            dve.memset(qxT[GD:R, :], 1.0).then_inc(Z["ones_ready"], 1)
            dve.wait_ge(Z["ld_const"], 16 * 4)
            stats1(0)
            apply1(0)
            q_expand(0)
            self_max(0)
            stats1(1)
            apply1(1)
            dve.wait_ge(Z["ld_w"], 16 * 8)
            link(dve.tensor_scalar(small[:, 2:4], small[:, 0:2], 1.0, None, ALU.add))
            for c in range(KC):
                dve.tensor_scalar(wxq[:, c, :], wxq[:, c, :], small[:, 2 + c:3 + c], None, ALU.mult)
                dve.tensor_scalar(wkv[:, c, :], wkv[:, c, :], small[:, 2 + c:3 + c], None, ALU.mult)
            link(dve.tensor_tensor(small[0:E, 48:64], small[0:E, 16:32], small[0:E, 16:32], ALU.mult))
            link(dve.tensor_reduce(small[0:E, 5:6], small[0:E, 48:64], AX.X, ALU.add))
            dve.tensor_copy(small[0:E, 6:7], small[0:E, 5:6]).then_inc(Z["setup_norm"], 1)
            dve.wait_ge(Z["setup_pool"], 1)
            link(dve.tensor_scalar(small[0:E, 8:9], small[0:E, 7:8], 0.0001, None, ALU.max))
            link(dve.reciprocal(small[0:E, 9:10], small[0:E, 8:9]))
            dve.tensor_scalar(small[0:E, 32:48], small[0:E, 16:32], small[0:E, 9:10], None, ALU.mult)\
               .then_inc(Z["weights_ready"], 1)
            dve.wait_ge(Z["setup_pe"], 1)
            dve.tensor_copy(wgT[:], b7[0:HD, 0:E]).then_inc(Z["setup_dve"], 1)
            dve.tensor_copy(tri[:], misc[0:T, 344:456]).then_inc(Z["setup_dve"], 1)

            def iteration(i, S_on=True, C_on=True, L_on=True, R_on=True, ahead=True):
                S, C, L, R = i + 1, i, i - 1, i - 2
                if C_on:
                    self_out(C)
                    stats2(C)
                if L_on:
                    cross_enc(L)
                if C_on:
                    apply2(C)
                if S_on:
                    q_expand(S)
                if C_on:
                    k_rope(C)
                    q_rope(C)
                if S_on:
                    self_max(S)
                if L_on:
                    cross_out(L)
                if C_on:
                    cross_max(C)
                if L_on:
                    stats3(L)
                if ahead:
                    stats1(S + 1)
                if R_on:
                    logits_out(R)
                if L_on:
                    apply3(L)
                if ahead:
                    apply1(S + 1)

            iteration(0, L_on=False, R_on=False)
            iteration(1, R_on=False)
            iteration(2)
            with dve.Fori(3, B - 2) as i:
                iteration(i)
            iteration(B - 2, ahead=False)
            iteration(B - 1, S_on=False, ahead=False)
            iteration(B, S_on=False, C_on=False, ahead=False)
            logits_out(B - 1)

            step[0] = 0

            def then(ins):
                step[0] += 1
                ins.then_inc(Z["c_route"], 1)
                dve.wait_ge(Z["c_route"], step[0])

            dve.wait_ge(Z["dve_logit"], B)
            then(dve.tensor_reduce(gmax[:], logits[:], AX.X, ALU.max))
            gm = gmax[:].unsqueeze(2).to_broadcast([T, B, E])
            dve.tensor_tensor(gdiff[:], logits[:], gm, ALU.subtract).then_inc(Z["g_diff"], 1)
            then(dve.tensor_tensor(cand[:], logits[:], gm, ALU.is_ge))
            nums = misc[0:T, 8:16].unsqueeze(1).to_broadcast([T, B, E])
            then(dve.tensor_tensor(cand[:], cand[:], nums, ALU.mult))
            then(dve.tensor_reduce(best[:], cand[:], AX.X, ALU.min))
            then(dve.tensor_tensor(onehot[:], nums, best[:].unsqueeze(2).to_broadcast([T, B, E]), ALU.is_equal))
            dve.tensor_copy(onehot_b[:], onehot[:].rearrange("p b e -> p e b")).then_inc(Z["g_dve"], 1)
            dve.wait_ge(Z["g_pe"], 1)
            then(dve.tensor_copy(totals[:], U[0][0:T, 1, 0:E * B]))
            then(dve.tensor_tensor_scan(running[:], misc[0:T, 44:300], totals[:], 0.0, ALU.mult, ALU.add))
            then(dve.tensor_tensor(place[:].rearrange("p e b -> p (e b)"), running[:], totals[:], ALU.subtract))
            then(dve.tensor_tensor(place[:].rearrange("p e b -> p (e b)"), U[0][0:T, 0, 0:E * B],
                                   place[:].rearrange("p e b -> p (e b)"), ALU.add))
            count = running[:].rearrange("p (e b) -> p e b", e=E)[:, :, B - 1:B]
            then(dve.tensor_tensor(over_t[:], count.to_broadcast([T, E, 28]),
                                   misc[0:T, 16:44].unsqueeze(1).to_broadcast([T, E, 28]), ALU.is_gt))
            then(dve.tensor_reduce(tiles_e[:], over_t[:], AX.X, ALU.add))
            then(dve.tensor_tensor_scan(ends[:], ones_f[0:T, :], tiles_e[:], 0.0, ALU.mult, ALU.add))
            then(dve.tensor_tensor(starts[:], ends[:], tiles_e[:], ALU.subtract))
            then(dve.tensor_scalar(starts[:], starts[:], float(P), None, ALU.mult))
            then(dve.tensor_tensor(place[:], place[:], starts[:].unsqueeze(2).to_broadcast([T, E, B]), ALU.add))
            then(dve.tensor_tensor(place[:], place[:], onehot[:].rearrange("p b e -> p e b"), ALU.mult))
            then(dve.tensor_reduce(slot[:], place[:].rearrange("p e b -> p b e"), AX.X, ALU.add))
            dve.tensor_copy(slot_i[:], slot[:]).then_inc(Z["g_slots"], 1)
            then(dve.tensor_tensor(past[:], misc[0:1, 308:344].unsqueeze(2).to_broadcast([1, 36, E]),
                                   ends[0:1, :].unsqueeze(1).to_broadcast([1, 36, E]), ALU.is_ge))
            then(dve.tensor_reduce(tile_e[:], past[:], AX.X, ALU.add))
            then(dve.tensor_scalar(tile_e[:], tile_e[:], float(E - 1), None, ALU.min))
            dve.tensor_copy(tile_e_i[:], tile_e[:]).then_inc(Z["g_dve"], 1)

            dve.wait_ge(Z["dve_keep3"], B)
            for b in range(B):
                if b >= 4:
                    dve.wait_ge(f_x3s[b % 4], 16 * (b // 4))
                dve.tensor_scalar(xs3[b % 4][:], x[:, b, :], mean_rstd3[:, b, 0:1], mean_rstd3[:, b, 1:2],
                                  ALU.subtract, ALU.mult).then_inc(Z["f_x3"], 1)
            dve.wait_ge(Z["ld_bias"], 48)
            dve.tensor_copy(pick[:].rearrange("p e n -> p (e n)"), hid[:]).then_inc(Z["pick_ready"], 1)
            then(dve.tensor_copy(b3[:, 0, :], braw2[:]))
            then(dve.tensor_tensor(braw3[:], braw2[:], b3[:, 0, :], ALU.subtract))
            then(dve.tensor_copy(b3[:, 1, :], braw3[:]))
            then(dve.tensor_tensor(braw2[:], braw3[:], b3[:, 1, :], ALU.subtract))
            dve.tensor_copy(b3[:, 2, :], braw2[:]).then_inc(Z["bias_parts"], 1)
            dve.wait_ge(Z["g_act"], 1)
            then(dve.tensor_reduce(gsum[:], gexp[:], AX.X, ALU.add))
            dve.reciprocal(score[:], gsum[:]).then_inc(Z["g_score"], 1)

            def hidden_copy(j):
                if not (isinstance(j, int) and j == 0):
                    dve.wait_ge(Z["f_y"], j)
                for n in range(2):
                    dve.wait_ge(Z["f_hT"], 2 * j + n + 1)
                    dve.tensor_copy(hidT[:, 4 * n:4 * n + 4, :], U[1][:, n, :].rearrange("p (k t) -> p k t", t=P))\
                       .then_inc(Z["f_hTs"], 1)

            def y_copy(j):
                dve.wait_ge(Z["f_y"], j + 1)
                if not (isinstance(j, int) and j == 0):
                    dve.wait_ge(Z["f_ystored"], 16 * j)
                dve.tensor_copy(ysb[:], b5[:, 0:D]).then_inc(Z["f_ysb"], 1)

            hidden_copy(0)
            y_copy(0)
            with dve.Fori(1, TILES) as j:
                hidden_copy(j)
                y_copy(j)

            dve.wait_ge(Z["g_score"], 1)
            for b in range(B):
                n = b % NY
                dve.wait_ge(f_gaths[n], 16 * (b // NY + 1))
                dve.scalar_tensor_tensor(yg[n][:], yg[n][:], score[:, b:b + 1], x[:, b, :], ALU.mult, ALU.add)\
                   .then_inc(Z["f_out"], 1)

        @block.gpsimd
        def _(pool):
            pool.memset(ysb[:], 0.0).then_inc(Z["zero_ready"], 1)
            pool.memset(bias_rows[:], 0.0).then_inc(Z["zero_ready"], 1)

            def power(b, n, mult, add, v, r):
                pool.wait_ge(Z[("dve_st1", "dve_st2", "dve_st3")[n]], b + 1)
                pool.wait_ge(Z[("dve_xn1", "dve_xn2", "dve_keep3")[n]], b)
                plain(pool)
                pool.tensor_scalar(rs[:, n, 0:1], mv[:, n, 1:2], mult, add, ALU.mult, ALU.add).then_inc(Z[v], 1)
                pool.wait_ge(Z[v], b + 1)
                pool.tensor_tensor(rs[:, n, 1:2], rs[:, n, 0:1], neghalf[0:T, 0:1], ALU.pow).then_inc(Z[r], 1)

            def rstd1(b):
                power(b, 0, 1.0, 1e-5, "pool_v1", "pool_r1")

            def rstd2(b):
                power(b, 1, 1.0 + 1e-6, 1e-11, "pool_v2", "pool_r2")

            def rstd3(b):
                power(b, 2, 1.0, 1e-5, "pool_v3", "pool_r3")

            def rstd_ctx(b):
                pool.wait_ge(Z["act_sq"], KT * (b + 1))
                pool.wait_ge(Z["act_vx"], b)
                plain(pool)
                pool.tensor_scalar(ssm[:], ss[:], 1.0 / D, 1e-6, ALU.mult, ALU.add).then_inc(Z["pool_vc"], 1)
                pool.wait_ge(Z["pool_vc"], b + 1)
                pool.tensor_tensor(rc[:], ssm[:], neghalf[0:KP, 0:KT], ALU.pow).then_inc(Z["pool_rc"], 1)

            def diag(b):
                pool.wait_ge(Z["pe_sexp"], KC * b)
                for c in range(KC):
                    pool.wait_ge(Z["dve_smax"], KC * b + c + 1)
                    plain(pool)
                    pool.affine_select(neg_diag[:, HC * c:HC * c + HC, :],
                                       nm[:, HC * c:HC * c + HC].unsqueeze(2).to_broadcast([T, HC, T]),
                                       [[0, HC], [1, T]], ALU.is_equal, 0.0, base=0, channel_multiplier=-1)\
                        .then_inc(Z["pool_D"], 1)

            def diagx(b):
                pool.wait_ge(Z["pe_xexp"], KT * b)
                pool.wait_ge(Z["dve_xmax"], 2 * (b + 1))
                plain(pool)
                pool.affine_select(neg_diagx.rearrange("p (g t) -> p g t", g=G),
                                   nmx[:].unsqueeze(2).to_broadcast([T, G, T]),
                                   [[0, G], [1, T]], ALU.is_equal, 0.0, base=0, channel_multiplier=-1)\
                    .then_inc(Z["pool_Dx"], 1)

            pool.wait_ge(Z["ones_ready"], 1)
            rstd1(0)
            diag(0)
            rstd1(1)
            pool.wait_ge(Z["setup_norm"], 1)
            pool.tensor_scalar(small[0:E, 10:11], neghalf[0:E, 0:1], -1.0, None, ALU.mult).then_inc(Z["c_pool"], 1)
            pool.wait_ge(Z["c_pool"], 1)
            pool.tensor_tensor(small[0:E, 7:8], small[0:E, 6:7], small[0:E, 10:11], ALU.pow)\
                .then_inc(Z["setup_pool"], 1)
            rstd_ctx(0)
            pool.wait_ge(Z["zero_ready"], 2)
            pool.dma_start(sorted_x.rearrange("(n p) d -> p n d", p=P),
                           ysb[:].unsqueeze(1).to_broadcast([P, TILES, D])).then_inc(Z["zero_sent"], 16)

            def iteration(i, S_on=True, C_on=True, L_on=True, next_on=True, ahead=True):
                S, C, L = i + 1, i, i - 1
                if C_on:
                    rstd2(C)
                if S_on:
                    diag(S)
                if C_on:
                    diagx(C)
                if next_on:
                    rstd_ctx(C + 1)
                if L_on:
                    rstd3(L)
                if ahead:
                    rstd1(S + 1)

            iteration(0, L_on=False)
            iteration(1)
            iteration(2)
            with pool.Fori(3, B - 2) as i:
                iteration(i)
            iteration(B - 2, ahead=False)
            iteration(B - 1, S_on=False, next_on=False, ahead=False)
            iteration(B, S_on=False, C_on=False, next_on=False, ahead=False)

            pool.wait_ge(Z["g_slots"], 1)
            pool.wait_ge(Z["zero_sent"], 16)
            for b in range(B):
                pool.wait_ge(Z["f_x3"], b + 1)
                pool.indirect_dma_start(out=sorted_x, out_offset=bass.IndirectOffsetOnAxis(ap=slot_i[:, b:b + 1], axis=0),
                                        in_=xs3[b % 4][:], in_offset=None).then_inc(f_x3s[b % 4], 16)
            def store_y(j):
                pool.wait_ge(Z["f_ysb"], j + 1)
                pool.dma_start(sorted_y[bass.ds(j * P, P), :], ysb[:]).then_inc(Z["f_ystored"], 16)

            store_y(0)
            with pool.Fori(1, TILES) as j:
                store_y(j)
            pool.wait_ge(Z["f_ystored"], 16 * TILES)
            for b in range(B):
                n = b % NY
                if b >= NY:
                    pool.wait_ge(f_sts[n], 16 * (b // NY))
                pool.indirect_dma_start(out=yg[n][:], out_offset=None, in_=sorted_y,
                                        in_offset=bass.IndirectOffsetOnAxis(ap=slot_i[:, b:b + 1], axis=0))\
                    .then_inc(f_gaths[n], 16)


def kernel(**inputs):
    import numpy as _np
    import concourse.bacc as _bacc
    from concourse import mybir as _mybir
    from concourse.bass_utils import run_bass_kernel_spmd as _run

    g = {k: _np.asarray(v) for k, v in inputs.items()}

    def chunks(w):
        return _np.ascontiguousarray(w.reshape(KC, P, -1).transpose(1, 0, 2))

    arrays = {
        "x": g["x"],
        "ctx": _np.ascontiguousarray(g["ctx_1024"].reshape(B, KT, KP, D).transpose(0, 2, 1, 3)),
        "ctxT": _np.ascontiguousarray(g["ctx_1024"].transpose(0, 2, 1).reshape(B, KC, P, S).transpose(0, 2, 1, 3)),
        "mask": g["mask_BxS2_bk0"].reshape(B, 1, S),
        "wqk": chunks(_np.concatenate([g["L0_attn_Wq"].T, g["L0_attn_Wk"].T], 1)),
        "wv": chunks(g["L0_attn_Wv"].T),
        "rms": _np.ascontiguousarray(g["L0_xattn_rms_scale"].reshape(KC, P).T),
        "wxq": chunks(g["L0_xattn_q_w"].transpose(1, 0, 2).reshape(D, G * GD)),
        "wkv": chunks(_np.concatenate([g["L0_xattn_kv_w"][0, 0], g["L0_xattn_kv_w"][1, 0]], 1)),
        "wo": chunks(g["L0_xattn_out_w"].reshape(G * GD, D)),
        "wred": chunks(g["L0_ffn_w_red"]),
        "wg": g["L0_ffn_wg"],
        "w1": _np.ascontiguousarray(g["L0_ffn_w1"].reshape(E, KC, P, F).transpose(2, 0, 1, 3)),
        "b1": g["L0_ffn_b1"],
        "w2": _np.ascontiguousarray(g["L0_ffn_w2"].reshape(E, FC, P, D).transpose(2, 0, 1, 3)),
        "b2": g["L0_ffn_b2"],
    }
    consts = constants()
    consts["pick"] = consts["pick"].reshape(P, E * P)
    arrays.update(consts)
    nc = _bacc.Bacc("TRN2", target_bir_lowering=False, num_devices=1)
    feed, aps = {}, {}
    for name, v in arrays.items():
        v = _np.ascontiguousarray(v)
        feed[f"in_{name}"] = v
        aps[name] = nc.dram_tensor(f"in_{name}", v.shape, _mybir.dt.from_np(v.dtype), kind="ExternalInput").ap()
    out = nc.dram_tensor("out_x", (B, T, D), F32, kind="ExternalOutput").ap()
    decoder(nc, aps, out)
    r = _run(nc, [feed], core_ids=[0])
    return r.results[0]["out_x"]
```

```python
from contextlib import ExitStack

import numpy as np

import concourse.bass as bass
from concourse import mybir

F32 = mybir.dt.float32
BF16 = mybir.dt.bfloat16
I32 = mybir.dt.int32
U8 = mybir.dt.uint8
ALU = mybir.AluOpType
ACT = mybir.ActivationFunctionType
AX = mybir.AxisListType

P = 128
B, T, D = 32, 112, 256
S = 375
KT, KP = 3, 125
KC = D // P
H, HD = 16, 16
HC = P // HD
G, GD = 4, 64
E, F = 8, 1024
FC = F // P
NB = 512
TILES = B * T // P + E - 1
REGION = B * T + P
ROW = 2 * D + 2
BIG = 2.0 ** 100
ARENA = 11400
PIECES = 20
WE = 2 * KC * F
EARLY = 5 * WE
SELF = 6 * 1024
PH = 6
PG = -(-H // PH)
PR = PH * (HD + 1)
R = GD + 1


def constants():
    half = GD // 2
    timescale = (np.float32(10000.0) ** (np.float32(2.0 / GD) * np.arange(half, dtype=np.float32))).astype(np.float32)
    def table(pos):
        rad = (pos.astype(np.float32)[:, None] / timescale[None, :]).astype(np.float32)
        s, c = np.sin(rad).astype(np.float32), np.cos(rad).astype(np.float32)
        return np.concatenate([c, c, -s, s], 1)
    ropeq = table(np.arange(S, S + T))
    ropek = table(np.arange(S)).reshape(KT, KP, 4 * half).transpose(1, 0, 2)
    p = np.arange(P)
    f = lambda a: np.ascontiguousarray(a, dtype=np.float32)
    misc = np.zeros((P, 8 + 8 + 28 + 8 + 36 + 36 + T), np.float32)
    misc[:, 0:8] = p[:, None] // HD == np.arange(HC)[None]
    misc[:, 8:16] = np.arange(E)[None] - E
    misc[:, 16:44] = P * np.arange(28)[None]
    misc[:, 44:52] = REGION * np.arange(E)[None]
    misc[:, 52:88] = np.arange(36)[None]
    misc[:, 88:124] = P * np.arange(36)[None]
    misc[:T, 124:124 + T] = (np.arange(T)[:, None] < np.arange(T)[None])
    token = np.concatenate([np.arange(B)[None] * T + p[:, None], B * T + p[:, None]], 1).astype(np.int32)
    pick = np.zeros((P, E, P), np.float32)
    for e in range(E):
        pick[3 * e:3 * e + 3, e] = 1.0
    return {"ropeq": f(ropeq), "ropek": f(ropek), "misc": f(misc), "pick": f(pick), "ident": f(np.eye(P)),
            "token": token}


def decoder(nc, a, out):
    with ExitStack() as ctx:
        def sb(name, shape, dt=F32):
            return ctx.enter_context(nc.sbuf_tensor(name, shape, dt))

        def psum(name, shape, dt=F32):
            return ctx.enter_context(nc.psum_tensor(name, shape, dt))

        def sem(name):
            return ctx.enter_context(nc.semaphore(name))

        sorted_x = nc.dram_tensor("sorted_x", [E * REGION + P, ROW], F32, kind="Internal").ap()

        mem = sb("mem", [P, EARLY + SELF + B * D])
        w1 = mem[:, 0:E * WE].rearrange("p (e c f) -> p e c f", e=E, c=2 * KC)
        w2 = mem[:, 0:E * WE].rearrange("p (e c d) -> p e c d", e=E, c=2 * FC)
        x = mem[0:T, EARLY + SELF:EARLY + SELF + B * D].rearrange("p (b d) -> p b d", b=B)
        x_over = (E * WE - EARLY - SELF) // D
        ident = sb("ident", [P, P])
        misc = sb("misc", [P, 124 + T])
        head_of = misc[:, 0:8]
        token = sb("token", [P, B + 1], I32)
        mean_rstd3 = sb("mean_rstd3", [T, B, 2])
        bias_rows = sb("bias_rows", [P, D], BF16)
        b1 = sb("b1", [P, E, FC])
        pick = sb("pick", [P, E, P], BF16)
        small = sb("small", [P, 64])
        ones = sb("ones", [P, P], BF16)
        neghalf = sb("neghalf", [P, KT])
        tri = sb("tri", [T, T], BF16)
        ones_f = sb("ones_f", [T, E])
        out_row = sb("out_row", [P, D])
        out_token = sb("out_token", [P, 1], I32)
        row = sb("row", [T, ROW])
        pad = sb("pad", [P, ROW])
        logits = sb("logits", [T, E])
        gmax = sb("gmax", [T, 1])
        gdiff = sb("gdiff", [T, E])
        gexp = sb("gexp", [T, E])
        gsum = sb("gsum", [T, 1])
        cand = sb("cand", [T, E])
        best = sb("best", [T, 1])
        onehot = sb("onehot", [T, E], BF16)
        base = sb("base", [T, E])
        place = sb("place", [T, E])
        slot = sb("slot", [T, 1])
        slot_i = sb("slot_i", [T, 1], I32)
        arena = sb("arena", [P, ARENA])
        used = [0]

        def carve(rows, shape, dt=F32):
            n = int(np.prod(shape))
            words = (n * (1 if dt == U8 else 2 if dt == BF16 else 4) + 3) // 4
            v = arena[0:rows, used[0]:used[0] + words]
            used[0] += words
            assert used[0] <= ARENA, used
            if dt != F32:
                v = v.bitcast(dt)[:, 0:n]
            names = "abc"[0:len(shape)]
            if len(shape) == 1:
                return v
            return v.rearrange("p (" + " ".join(names) + ") -> p " + " ".join(names),
                               **{k: s for k, s in zip(names, shape)})

        wkv = carve(P, [KC, 2 * GD])
        wred = carve(P, [KC, HD])
        wgT = carve(HD, [E])
        ropeq = carve(T, [2 * GD])
        ropek = carve(KP, [KT, 2 * GD])
        xn = carve(T, [D])
        xnT = carve(P, [KC, T])
        kT = carve(P, [KC, T])
        v1_flat = carve(T, [(H + 1) * PR])
        v1 = v1_flat[:, 0:H * PR].rearrange("p (h r) -> p h r", h=H)
        pvT = carve(PR, [PG, T])
        kxT = carve(R, [S])
        qxT = carve(R, [G * T])
        vx = carve(KP, [KT, R])
        mask_row = carve(R, [S], U8)
        nm = carve(T, [H])
        nmx = carve(T, [G])
        ctxn = carve(KP, [KT, D])
        xn2 = carve(T, [D])
        xn2T = carve(P, [KC, T])
        xn3 = carve(T, [D])
        xn3T = carve(P, [KC, T])
        tmp1 = carve(T, [D])
        ropea = carve(T, [D])
        ropeb = carve(T, [D])
        qrot = carve(T, [D])
        kraw = carve(KP, [KT, GD])
        kra = carve(KP, [KT, GD])
        krb = carve(KP, [KT, GD])
        krot = carve(KP, [KT, GD])
        enc = carve(T, [D])
        encT = carve(P, [KC, T])
        pvxT = carve(R, [G * T])
        redT = carve(HD, [T])
        stats = carve(T, [3, 6])
        mv = carve(T, [3, 2])
        rs = carve(T, [3, 2])
        ss = carve(KP, [KT])
        ssm = carve(KP, [KT])
        rc = carve(KP, [KT])
        den = carve(T, [H])
        denx = carve(T, [G])
        taken = [EARLY]

        def over(rows, n):
            v = mem[0:rows, taken[0]:taken[0] + n]
            taken[0] += n
            assert taken[0] <= EARLY + SELF
            return v

        qexp = [over(P, HC * T).rearrange("p (h t) -> p h t", h=HC) for _ in range(KC)]
        prob = over(T, H * T).rearrange("p (h t) -> p h t", h=H)
        neg_diag = over(T, H * T // 2).bitcast(BF16).rearrange("p (h t) -> p h t", h=H)
        wqk, wv = (over(P, KC * n).rearrange("p (c n) -> p c n", c=KC) for n in (2 * D, D))
        probx = sb("probx", [KP, KT, G * T])[:]
        neg_diagx = sb("neg_diagx", [T, G * T], BF16)[:]
        ctxT = sb("ctxT", [P, KC, S])[:]
        square = sb("square", [KP, D])[:]
        wxq = sb("wxq", [P, KC, D])[:]
        wo = sb("wo", [P, KC, D])[:]
        BIAS_AT = EARLY - 2 * 1024
        pick_f = mem[:, BIAS_AT:BIAS_AT + E * P]
        b3 = mem[0:E, BIAS_AT + 1024:BIAS_AT + 1024 + 3 * D // 2].bitcast(BF16)\
            .rearrange("p (a n) -> p a n", a=3)
        braw2, braw3 = (mem[0:E, BIAS_AT + at:BIAS_AT + at + D] for at in (1536, 1792))
        used[0] = 0
        count = carve(1, [E])
        over_t = carve(1, [E, 28])
        tiles_e = carve(1, [E])
        ends = carve(1, [E])
        skip = carve(1, [E])
        past = carve(1, [36, E])
        tile_e = carve(1, [36])
        tile_row = carve(1, [36])
        base_i = carve(1, [E], I32)
        tile_e_i = carve(1, [36], I32)
        tile_row_i = carve(1, [36], I32)
        xs = carve(P, [D])
        xr = carve(P, [D + 2])
        xsT = carve(P, [KC, P])
        w1_now = carve(P, [KC, F])
        b1_now = carve(P, [FC])
        hidT = carve(P, [FC, P])

        bank = [psum(f"bank{n}", [P, NB]) for n in range(4, 8)]
        b4, b5, b6, b7 = bank
        U = [psum(f"pair{n}", [P, 2, NB]) for n in range(2)]
        xT_ps = b4[:, 0:KC * T].rearrange("p (k t) -> p k t", k=KC)
        x2T_ps = xT_ps
        q_ps = b4[0:T, 0:D]
        qxT_ps = b4[0:GD, 0:G * T]
        pvxT_ps = b5[0:R, 0:G * T]
        pvx_ps = b5[0:T, 0:G * R].rearrange("p (g r) -> p g r", g=G)
        encT_ps = b5[:, 0:KC * T].rearrange("p (k t) -> p k t", k=KC)
        out_ps = b5[0:T, 0:D]
        qk_ps = b6[:, 0:4 * T].rearrange("p (k t) -> p k t", k=4)
        v_ps = b6[0:T, 0:D]
        pvT_ps = b5[0:PR, 0:PG * T].rearrange("p (g t) -> p g t", g=PG)
        pv_ps = b5[0:T, 0:H * (HD + 1)].rearrange("p (h r) -> p h r", h=H)
        kv_ps = b7[0:KP, 0:KT * 2 * GD].rearrange("p (k n) -> p k n", k=KT)
        kxT_ps = b7[0:GD, 0:S]
        x3T_ps = b7[:, 0:KC * T].rearrange("p (k t) -> p k t", k=KC)
        redT_ps = b7[0:HD, 0:T]
        logit_ps = b7[0:T, 0:E]
        count_ps = b7[0:T, 0:2 * E].rearrange("p (a e) -> p a e", a=2)

        hT_ps = [u[:, :, :].rearrange("p a (k t) -> p (a k) t", t=P) for u in U]
        xsT_ps = b4[:, 0:KC * P].rearrange("p (k t) -> p k t", k=KC)
        y_ps = b5[:, 0:D]

        S_ = {}

        def s(name):
            if name not in S_:
                S_[name] = sem(name)
            return S_[name]

        names = ["ld_const", "ld_w", "ld_x", "ld_ctxn", "ld_ctxT", "ld_mask", "ld_early", "ld_late", "zero_ready",
                 "ones_ready", "weights_ready", "setup_dve", "setup_pe", "setup_pool",
                 "pe_xT", "pe_x2T", "pe_qk", "pe_v", "pe_q", "pe_smax", "pe_qT", "pe_xmax", "pe_sexp", "pe_x3T",
                 "pe_xexp", "pe_red", "pe_pv", "pe_logit", "pe_xpv", "pe_pvT", "pe_pvx", "pe_kv", "pe_encT", "pe_kT", "pe_out",
                 "act_xT", "act_x2T", "act_kT", "act_v", "act_qT", "act_sexp", "act_x3T", "act_xexp", "act_red",
                 "act_sq", "act_kxT", "act_pvT", "act_pvx", "act_encT",
                 "dve_qexp", "dve_rope", "dve_x3", "dve_smax", "dve_xmax", "dve_x1", "dve_bn2", "dve_bn1", "dve_bn3",
                 "dve_st2", "dve_st1", "dve_st3", "dve_xn2", "dve_xn1", "dve_enc", "dve_logit", "dve_krope",
                 "act_vx", "act_kraw", "dve_x2", "dve_keep3", "c_rope", "c_krope", "c_x1", "c_enc",
                 "pool_v1", "pool_r1", "pool_v2", "pool_r2", "pool_v3", "pool_r3", "pool_vc", "pool_rc", "pool_D",
                 "pool_Dx", "act_mask",
                 "gate_max", "gate_diff", "gate_cand", "gate_best", "gate_onehot", "act_gate", "pe_count", "dve_place",
                 "c_place", "row_dve", "row_act", "row_sent", "g_base", "g_table", "pad_ready", "pad_sent",
                 "setup_norm", "c_setup", "c_bias", "c_table", "c_pool", "ld_bias", "bias_sent",
                 "pick_ready",
                 "f_xs", "f_xr", "f_xT", "f_xsT", "f_w_dve", "f_w_act", "f_b1", "f_h", "f_gelu", "f_y", "f_out", "f_sent"]
        for n in names:
            s(n)
        Z = S_
        block = ctx.enter_context(nc.Block())

        def v_places(g, heads, n):
            step = PR + HD + 1
            first = PH * g * PR
            return v1_flat[:, first:first + heads * step].rearrange("p (h s) -> p h s", s=step)[:, :, 0:n]

        def plain(eng):
            eng.nop(nofuse=True)

        @block.sync
        def _(sp):
            for dst, name in ((ident[:], "ident"), (misc[:], "misc"), (wqk, "wqk"), (wv, "wv")):
                sp.dma_start(dst, a[name]).then_inc(Z["ld_const"], 16)
            sp.dma_start(x[:, 0, :], a["x"][0]).then_inc(Z["ld_x"], 16)
            for dst, name in ((ropeq, "ropeq"), (ropek, "ropek"), (wxq, "wxq"), (wkv, "wkv"),
                              (wo, "wo"), (wred, "wred"), (token[:], "token")):
                sp.dma_start(dst, a[name]).then_inc(Z["ld_w"], 16)
            sp.dma_start(small[:, 0:2], a["rms"]).then_inc(Z["ld_w"], 16)
            sp.dma_start(small[0:E, 16:32], a["wg"]).then_inc(Z["ld_w"], 16)
            sp.dma_start(pick_f, a["pick"]).then_inc(Z["ld_bias"], 16)
            sp.dma_start(braw2, a["b2"]).then_inc(Z["ld_bias"], 16)
            sp.dma_start(b1[:], a["b1"]).then_inc(Z["ld_bias"], 16)

            def context(b):
                sp.wait_ge(Z["pe_kv"], b)
                sp.dma_start(ctxT, a["ctxT"][b]).then_inc(Z["ld_ctxT"], 16)
                sp.wait_ge(Z["act_mask"], b)
                plain(sp)
                sp.dma_start(mask_row[GD:R, :], a["mask"][b]).then_inc(Z["ld_mask"], 16)

            def context_rows(b):
                sp.wait_ge(Z["act_sq"], KT * b)
                sp.dma_start(ctxn[:], a["ctx"][b]).then_inc(Z["ld_ctxn"], 16)

            def tokens(b):
                sp.wait_ge(Z["ld_x"], 16 * b)
                sp.dma_start(x[:, b, :], a["x"][b]).then_inc(Z["ld_x"], 16)

            PIECE = EARLY // PIECES

            def weights(n):
                at = bass.ds(n * PIECE, PIECE)
                sp.dma_start(mem[:, at], a["w"][:, at]).then_inc(Z["ld_early"], 16)

            context_rows(0)
            tokens(1)
            context(0)
            context_rows(1)
            tokens(2)
            BIAS_PIECE = BIAS_AT // PIECE
            with sp.Fori(1, BIAS_PIECE + 1) as b:
                context(b)
                context_rows(b + 1)
                tokens(b + 2)
                weights(b - 1)
            sp.wait_ge(Z["bias_sent"], 48)
            sp.wait_ge(Z["pick_ready"], 1)
            with sp.Fori(BIAS_PIECE + 1, PIECES + 1) as b:
                context(b)
                context_rows(b + 1)
                tokens(b + 2)
                weights(b - 1)
            with sp.Fori(PIECES + 1, B - 2) as b:
                context(b)
                context_rows(b + 1)
                tokens(b + 2)
            context(B - 2)
            context_rows(B - 1)
            sp.wait_ge(Z["row_dve"], x_over)
            sp.wait_ge(Z["row_act"], x_over)
            sp.dma_start(mem[:, EARLY + SELF:E * WE], a["w"][:, EARLY + SELF:E * WE]).then_inc(Z["ld_late"], 16)
            context(B - 1)
            sp.wait_ge(Z["pe_pv"], B)
            sp.dma_start(mem[:, EARLY:EARLY + SELF], a["w"][:, EARLY:EARLY + SELF]).then_inc(Z["ld_late"], 16)

            sp.wait_ge(Z["pad_ready"], 1)
            sp.wait_ge(Z["setup_dve"], 4)
            sp.dma_start(sorted_x[E * REGION:E * REGION + P, :], pad[:]).then_inc(Z["pad_sent"], 16)
            sp.wait_ge(Z["g_base"], 1)
            with sp.Fori(0, E // 2) as e:
                end = sp.value_load(base_i[0:1, bass.ds(e, 1)], min_val=0, max_val=E * REGION - P)
                sp.dma_start(sorted_x[bass.ds(end, P), :], pad[:]).then_inc(Z["pad_sent"], 16)

            sp.wait_ge(Z["g_table"], 1)
            sp.wait_ge(Z["pad_sent"], 16 * (E + 1))
            sp.wait_ge(Z["row_sent"], 16 * B)

            def tile_load(j):
                at = sp.value_load(tile_row_i[0:1, bass.ds(j, 1)], min_val=0, max_val=E * REGION)
                sp.dma_start(xs[:], sorted_x[bass.ds(at, P), 0:D]).then_inc(Z["f_xs"], 16)

            tile_load(0)
            with sp.Fori(1, TILES) as j:
                sp.wait_ge(Z["f_xT"], j)
                tile_load(j)

        @block.tensor
        def _(pe):
            def turn(dst, src, rows, cols):
                plain(pe)
                return pe.transpose(dst, src, ident[0:rows, 0:rows])

            def kv(b):
                pe.wait_ge(Z["ld_ctxT"], 16 * (b + 1))
                if not isinstance(b, int) or b > 2:
                    pe.wait_ge(Z["dve_place"], b - 2)
                for t in range(KT):
                    for c in range(KC):
                        mm = pe.matmul(kv_ps[:, t, :], ctxT[:, c, KP * t:KP * t + KP], wkv[:, c, :],
                                       start=(c == 0), stop=(c == KC - 1))
                mm.then_inc(Z["pe_kv"], 1)

            def k_turn(b):
                pe.wait_ge(Z["dve_krope"], b + 1)
                pe.wait_ge(Z["act_vx"], b + 1)
                for t in range(KT):
                    mm = turn(kxT_ps[:, KP * t:KP * t + KP], krot[:, t, :], KP, GD)
                mm.then_inc(Z["pe_kT"], 1)

            def x_turn(b):
                pe.wait_ge(Z["dve_xn1"], b + 1)
                if not isinstance(b, int) or b > 1:
                    pe.wait_ge(Z["act_qT"], b - 1)
                for c in range(KC):
                    mm = turn(xT_ps[:, c, :], xn[:, P * c:P * c + P], T, P)
                mm.then_inc(Z["pe_xT"], 1)

            def x2_turn(b):
                pe.wait_ge(Z["dve_xn2"], b + 1)
                pe.wait_ge(Z["act_qT"], b)
                for c in range(KC):
                    mm = turn(x2T_ps[:, c, :], xn2[:, P * c:P * c + P], T, P)
                mm.then_inc(Z["pe_x2T"], 1)

            def qk(b):
                pe.wait_ge(Z["act_xT"], b + 1)
                pe.wait_ge(Z["act_v"], b)
                for o in range(4):
                    for c in range(KC):
                        mm = pe.matmul(qk_ps[:, o, :], wqk[:, c, P * o:P * o + P], xnT[:, c, :],
                                       start=(c == 0), stop=(c == KC - 1))
                mm.then_inc(Z["pe_qk"], 1)

            def v(b):
                pe.wait_ge(Z["dve_qexp"], KC * (b + 1))
                for c in range(KC):
                    mm = pe.matmul(v_ps, xnT[:, c, :], wv[:, c, :], start=(c == 0), stop=(c == KC - 1))
                mm.then_inc(Z["pe_v"], 1)

            def q_proj(b):
                pe.wait_ge(Z["act_x2T"], b + 1)
                for c in range(KC):
                    mm = pe.matmul(q_ps, xn2T[:, c, :], wxq[:, c, :], start=(c == 0), stop=(c == KC - 1))
                mm.then_inc(Z["pe_q"], 1)

            def top(ap):
                return ap.bitcast(BF16)[:, 1::2]

            def self_max(b, c):
                pe.wait_ge(Z["act_kT"], b + 1)
                pe.wait_ge(Z["dve_qexp"], KC * b + c + 1)
                if not isinstance(b, int) or b > 1:
                    pe.wait_ge(Z["act_xexp"], KT * (b - 1))
                for h in range(HC):
                    mm = pe.matmul(U[c][0:T, h // 4, (h % 4) * T:(h % 4 + 1) * T], top(qexp[c][:, h, :]),
                                   top(kT[:, c, :]), start=True, stop=True)
                mm.then_inc(Z["pe_smax"], 1)

            def q_turn(b):
                pe.wait_ge(Z["dve_rope"], b + 1)
                for g in range(G):
                    mm = turn(qxT_ps[:, g * T:(g + 1) * T], qrot[:, g * GD:(g + 1) * GD], T, GD)
                mm.then_inc(Z["pe_qT"], 1)

            def cross_max(b, u, S_on):
                pe.wait_ge(Z["act_qT"], b + 1)
                pe.wait_ge(Z["act_kxT"], b + 1)
                pe.wait_ge(Z["act_mask"], b + 1)
                if S_on:
                    pe.wait_ge(Z["act_sexp"], KC * (b + 1) + u + 1)
                for n in range(2):
                    g = 2 * u + n
                    mm = pe.matmul(U[u][0:T, n, 0:S], top(qxT[:, g * T:(g + 1) * T]), top(kxT[:, :]),
                                   start=True, stop=True)
                mm.then_inc(Z["pe_xmax"], 1)

            def self_exp(b, c):
                pe.wait_ge(Z["pool_D"], KC * b + c + 1)
                for n in range(2):
                    dst = U[c][0:T, n, 0:4 * T]
                    pe.matmul(dst, kT[:, c, :], qexp[c][:, 4 * n:4 * n + 4, :], start=True, stop=False)
                    mm = pe.matmul(dst, ones[0:T, 0:T],
                                   neg_diag[:, HC * c + 4 * n:HC * c + 4 * n + 4, :], start=False, stop=True)
                mm.then_inc(Z["pe_sexp"], 1)

            def cross_exp(b):
                pe.wait_ge(Z["pool_Dx"], b + 1)
                for t in range(KT):
                    dst = U[t // 2][0:KP, t % 2, 0:G * T]
                    pe.matmul(dst, kxT[:, KP * t:KP * t + KP], qxT[:, :], start=True, stop=False)
                    mm = pe.matmul(dst, ones[0:T, 0:KP], neg_diagx, start=False, stop=True)
                    mm.then_inc(Z["pe_xexp"], 1)

            def self_pv(b, c):
                pe.wait_ge(Z["act_v"], b + 1)
                if not isinstance(b, int) or b > 1:
                    pe.wait_ge(Z["dve_x2"], b - 1)
                pe.wait_ge(Z["act_sexp"], KC * b + c + 1)
                for h in range(HC * c, HC * c + HC):
                    mm = pe.matmul(pvT_ps[:, h // PH, :], v1[:, h, :], prob[:, h, :],
                                   start=(h % PH == 0), stop=(h % PH == PH - 1 or h == H - 1))
                if c == KC - 1:
                    mm.then_inc(Z["pe_pv"], 1)

            def pv_turn(b):
                pe.wait_ge(Z["act_pvT"], b + 1)
                for g in range(PG):
                    rows = min(H - PH * g, PH) * (HD + 1)
                    mm = turn(b5[0:T, PR * g:PR * g + rows], pvT[0:rows, g, :], rows, T)
                mm.then_inc(Z["pe_pvT"], 1)

            def cross_pv(b, C_on):
                pe.wait_ge(Z["act_xexp"], KT * (b + 1))
                pe.wait_ge(Z["dve_x1"], b + 2 if C_on else b + 1)
                for t in range(KT):
                    mm = pe.matmul(pvxT_ps, vx[:, t, :], probx[:, t, :], start=(t == 0), stop=(t == KT - 1))
                mm.then_inc(Z["pe_xpv"], 1)

            def pvx_turn(b):
                pe.wait_ge(Z["act_pvx"], b + 1)
                for g in range(G):
                    mm = turn(pvx_ps[:, g, :], pvxT[:, g * T:(g + 1) * T], R, T)
                mm.then_inc(Z["pe_pvx"], 1)

            def enc_turn(b):
                pe.wait_ge(Z["dve_enc"], b + 1)
                for c in range(KC):
                    mm = turn(encT_ps[:, c, :], enc[:, P * c:P * c + P], T, P)
                mm.then_inc(Z["pe_encT"], 1)

            def out_proj(b):
                pe.wait_ge(Z["act_encT"], b + 1)
                for c in range(KC):
                    mm = pe.matmul(out_ps, encT[:, c, :], wo[:, c, :], start=(c == 0), stop=(c == KC - 1))
                mm.then_inc(Z["pe_out"], 1)

            def x3_turn(b, C_on):
                pe.wait_ge(Z["dve_x3"], b + 1)
                if C_on:
                    pe.wait_ge(Z["act_kxT"], b + 3)
                pe.wait_ge(Z["dve_place"], b)
                for c in range(KC):
                    mm = turn(x3T_ps[:, c, :], xn3[:, P * c:P * c + P], T, P)
                mm.then_inc(Z["pe_x3T"], 1)

            def router_red(b):
                pe.wait_ge(Z["act_x3T"], b + 1)
                for c in range(KC):
                    mm = pe.matmul(redT_ps, wred[:, c, :], xn3T[:, c, :], start=(c == 0), stop=(c == KC - 1))
                mm.then_inc(Z["pe_red"], 1)

            def router_logits(b):
                pe.wait_ge(Z["act_red"], b + 1)
                pe.matmul(logit_ps, redT[:, :], wgT[:, :], start=True, stop=True).then_inc(Z["pe_logit"], 1)

            def router_count(b):
                pe.wait_ge(Z["gate_onehot"], b + 1)
                pe.matmul(count_ps[:, 0, :], tri[:, :], onehot[:, :], start=True, stop=True)
                pe.matmul(count_ps[:, 1, :], ones[0:T, 0:T], onehot[:, :], start=True, stop=True)\
                  .then_inc(Z["pe_count"], 1)

            pe.wait_ge(Z["ld_const"], 16 * 4)
            pe.wait_ge(Z["ones_ready"], 1)
            def iteration(i, N_on=True, S_on=True, C_on=True, L_on=True, R_on=True, Q_on=True):
                N, S, C, L, R, Q = i + 2, i + 1, i, i - 1, i - 2, i - 3
                if C_on:
                    self_pv(C, 0)
                if L_on:
                    cross_max(L, 1, C_on)
                if Q_on:
                    router_count(Q)
                if C_on:
                    self_pv(C, 1)
                if S_on:
                    qk(S)
                if C_on:
                    pv_turn(C)
                if L_on:
                    cross_exp(L)
                if C_on:
                    kv(C)
                if L_on:
                    cross_pv(L, C_on)
                if C_on:
                    x2_turn(C)
                if S_on:
                    self_max(S, 0)
                if C_on:
                    q_proj(C)
                if S_on:
                    self_max(S, 1)
                if L_on:
                    pvx_turn(L)
                if C_on:
                    k_turn(C)
                if S_on:
                    v(S)
                if C_on:
                    q_turn(C)
                if L_on:
                    enc_turn(L)
                if R_on:
                    x3_turn(R, C_on)
                if S_on:
                    self_exp(S, 0)
                if L_on:
                    out_proj(L)
                if R_on:
                    router_red(R)
                if S_on:
                    self_exp(S, 1)
                if R_on:
                    router_logits(R)
                if C_on:
                    cross_max(C, 0, S_on)
                if N_on:
                    x_turn(N)

            x_turn(0)
            iteration(-1, C_on=False, L_on=False, R_on=False, Q_on=False)
            pe.wait_ge(Z["weights_ready"], 1)
            turn(b7[0:HD, 0:E], small[0:E, 32:48], E, HD).then_inc(Z["setup_pe"], 1)
            pe.wait_ge(Z["setup_dve"], 1)
            iteration(0, L_on=False, R_on=False, Q_on=False)
            iteration(1, R_on=False, Q_on=False)
            iteration(2, Q_on=False)
            iteration(3)
            with pe.Fori(4, B - 2) as i:
                iteration(i)
            iteration(B - 2, N_on=False)
            iteration(B - 1, N_on=False, S_on=False)
            iteration(B, N_on=False, S_on=False, C_on=False)
            iteration(B + 1, N_on=False, S_on=False, C_on=False, L_on=False)
            iteration(B + 2, N_on=False, S_on=False, C_on=False, L_on=False, R_on=False)


            def expert(j):
                return pe.value_load(tile_e_i[0:1, bass.ds(j, 1)], min_val=0, max_val=E - 1)

            def tile_turn(j):
                pe.wait_ge(Z["f_xs"], 16 * (j + 1))
                for c in range(KC):
                    mm = pe.transpose(xsT_ps[:, c, :], xs[:, P * c:P * c + P], ident[:, :])
                mm.then_inc(Z["f_xT"], 1)

            def up(j, odd):
                pe.wait_ge(Z["f_xsT"], j + 1)
                pe.wait_ge(Z["f_w_dve"], j + 1)
                pe.wait_ge(Z["f_w_act"], j + 1)
                if not isinstance(j, int) or j >= 2:
                    pe.wait_ge(Z["f_gelu"], 2 * (j - 1))
                for k in range(FC):
                    for c in range(KC):
                        mm = pe.matmul(hT_ps[odd][:, k, :], w1_now[:, c, P * k:P * k + P], xsT[:, c, :],
                                       start=(c == 0), stop=(c == KC - 1))
                    if k % 4 == 3:
                        mm.then_inc(Z["f_h"], 1)

            def down(j, e):
                pe.wait_ge(Z["f_out"], j)
                pe.matmul(y_ps, pick[:, e, :], bias_rows[:, :], start=True, stop=False)
                for k in range(FC):
                    if k % 4 == 0:
                        pe.wait_ge(Z["f_gelu"], 2 * j + k // 4 + 1)
                    mm = pe.matmul(y_ps, hidT[:, k, :], w2[:, e, FC + k, :], start=False, stop=(k == FC - 1))
                mm.then_inc(Z["f_y"], 1)

            pe.wait_ge(Z["g_table"], 1)
            pe.wait_ge(Z["ld_late"], 32)
            pe.wait_ge(Z["ld_early"], 16 * PIECES)
            pe.wait_ge(Z["bias_sent"], 48)
            pe.wait_ge(Z["pick_ready"], 1)
            tile_turn(0)
            up(0, 0)
            tile_turn(1)

            def tile(j, odd, ahead=True):
                up(j + 1, 1 - odd)
                if ahead:
                    tile_turn(j + 2)
                down(j, expert(j))

            tile(0, 0)
            tile(1, 1)
            with pe.Fori(2, TILES - 3, 2) as j:
                tile(j, 0)
                tile(j + 1, 1)
            tile(TILES - 3, 0)
            tile(TILES - 2, 1, ahead=False)
            down(TILES - 1, expert(TILES - 1))

        @block.scalar
        def _(act):
            def copy(dst, src):
                return act.activation(dst, src, ACT.Copy)

            def squares(b):
                act.wait_ge(Z["ld_ctxn"], 16 * (b + 1))
                act.wait_ge(Z["pool_vc"], b)
                for t in range(KT):
                    if not (isinstance(b, int) and b == 0 and t == 0):
                        act.wait_ge(Z["act_sq"], KT * b + t)
                    act.activation(square, ctxn[:, t, :], ACT.Square, accum_out=ss[:, t:t + 1])\
                       .then_inc(Z["act_sq"], 1)

            def x_copy(b):
                act.wait_ge(Z["pe_xT"], b + 1)
                act.wait_ge(Z["pe_v"], b)
                copy(xnT[:], xT_ps).then_inc(Z["act_xT"], 1)

            def x2_copy(b):
                act.wait_ge(Z["pe_x2T"], b + 1)
                act.wait_ge(Z["pe_q"], b)
                copy(xn2T[:], x2T_ps).then_inc(Z["act_x2T"], 1)

            def kT_copy(b):
                act.wait_ge(Z["pe_qk"], b + 1)
                act.wait_ge(Z["pe_sexp"], KC * b)
                copy(kT[:], qk_ps[:, KC:2 * KC, :]).then_inc(Z["act_kT"], 1)

            def v_copy(b):
                act.wait_ge(Z["pe_v"], b + 1)
                act.wait_ge(Z["pe_pv"], b)
                for g in range(PG):
                    heads = min(H - PH * g, PH)
                    v = act.activation(v_places(g, heads, HD), v_ps[:, PH * HD * g:PH * HD * g + HD * heads]
                                       .rearrange("p (h d) -> p h d", h=heads), ACT.Copy)
                v.then_inc(Z["act_v"], 1)

            def pvT_copy(b):
                act.wait_ge(Z["pe_pv"], b + 1)
                act.wait_ge(Z["pe_pvT"], b)
                copy(pvT[:], pvT_ps).then_inc(Z["act_pvT"], 1)

            def ctx_k_copy(b):
                act.wait_ge(Z["pe_kv"], b + 1)
                act.wait_ge(Z["pool_rc"], b + 1)
                act.wait_ge(Z["c_krope"], 3 * b)
                for t in range(KT):
                    k = act.activation(kraw[:, t, :], kv_ps[:, t, 0:GD], ACT.Copy, scale=rc[:, t:t + 1])
                k.then_inc(Z["act_kraw"], 1)

            def ctx_v_copy(b):
                act.wait_ge(Z["pe_xpv"], b)
                for t in range(KT):
                    k = act.activation(vx[:, t, 0:GD], kv_ps[:, t, GD:2 * GD], ACT.Copy, scale=rc[:, t:t + 1])
                k.then_inc(Z["act_vx"], 1)

            def q_copy(b):
                act.wait_ge(Z["pe_qT"], b + 1)
                act.wait_ge(Z["pe_xexp"], KT * b)
                copy(qxT[0:GD, :], qxT_ps).then_inc(Z["act_qT"], 1)

            def self_exp(b, c):
                act.wait_ge(Z["pe_sexp"], KC * b + c + 1)
                act.wait_ge(Z["pe_pv"], b)
                act.activation(prob[:, HC * c:HC * c + HC, :].rearrange("p (a h) t -> p a (h t)", a=2),
                               U[c][0:T, :, 0:4 * T], ACT.Exp, scale=HD ** -0.5).then_inc(Z["act_sexp"], 1)

            def x3_copy(b):
                act.wait_ge(Z["pe_x3T"], b + 1)
                act.wait_ge(Z["pe_red"], b)
                copy(xn3T[:], x3T_ps).then_inc(Z["act_x3T"], 1)

            def cross_exp(b):
                act.wait_ge(Z["pe_xpv"], b)
                for t in range(KT):
                    act.wait_ge(Z["pe_xexp"], KT * b + t + 1)
                    act.activation(probx[:, t, :], U[t // 2][0:KP, t % 2, 0:G * T], ACT.Exp,
                                   scale=GD ** -0.5).then_inc(Z["act_xexp"], 1)

            def red_copy(b):
                act.wait_ge(Z["pe_red"], b + 1)
                act.wait_ge(Z["pe_logit"], b)
                copy(redT[:], redT_ps).then_inc(Z["act_red"], 1)

            def pvx_copy(b):
                act.wait_ge(Z["pe_xpv"], b + 1)
                act.wait_ge(Z["pe_pvx"], b)
                copy(pvxT[:], pvxT_ps).then_inc(Z["act_pvx"], 1)

            def enc_copy(b):
                act.wait_ge(Z["pe_encT"], b + 1)
                act.wait_ge(Z["pe_out"], b)
                copy(encT[:], encT_ps).then_inc(Z["act_encT"], 1)

            def k_copy(b):
                act.wait_ge(Z["pe_kT"], b + 1)
                act.wait_ge(Z["pe_xexp"], KT * b)
                copy(kxT[0:GD, :], kxT_ps).then_inc(Z["act_kxT"], 1)
                act.wait_ge(Z["ld_mask"], 16 * (b + 1))
                act.activation(kxT[GD:R, :], mask_row[GD:R, :], ACT.Copy, bias=-BIG, scale=BIG)\
                   .then_inc(Z["act_mask"], 1)

            def gate_exp(b):
                act.wait_ge(Z["gate_diff"], b + 1)
                act.activation(gexp[:], gdiff[:], ACT.Exp, accum_out=gsum[:]).then_inc(Z["act_gate"], 1)

            def row_residual(b):
                if not isinstance(b, int) or b > 0:
                    act.wait_ge(Z["row_sent"], 16 * b)
                copy(row[:, D:2 * D], x[:, b, :]).then_inc(Z["row_act"], 1)

            def iteration(i, N_on=True, S_on=True, C_on=True, L_on=True, R_on=True, Q_on=True):
                N, S, C, L, R, Q = i + 2, i + 1, i, i - 1, i - 2, i - 3
                if Q_on:
                    gate_exp(Q)
                    row_residual(Q)
                if C_on:
                    pvT_copy(C)
                if S_on:
                    kT_copy(S)
                if L_on:
                    cross_exp(L)
                if C_on:
                    ctx_k_copy(C)
                    x2_copy(C)
                    ctx_v_copy(C)
                if L_on:
                    pvx_copy(L)
                if C_on:
                    k_copy(C)
                if S_on:
                    v_copy(S)
                if C_on:
                    q_copy(C)
                if L_on:
                    enc_copy(L)
                if R_on:
                    x3_copy(R)
                if S_on:
                    squares(C + 1)
                    self_exp(S, 0)
                if R_on:
                    red_copy(R)
                if S_on:
                    self_exp(S, 1)
                if N_on:
                    x_copy(N)

            act.wait_ge(Z["ones_ready"], 1)
            x_copy(0)
            iteration(-1, C_on=False, L_on=False, R_on=False, Q_on=False)
            iteration(0, L_on=False, R_on=False, Q_on=False)
            iteration(1, R_on=False, Q_on=False)
            iteration(2, Q_on=False)
            iteration(3)
            with act.Fori(4, B - 2) as i:
                iteration(i)
            iteration(B - 2, N_on=False)
            iteration(B - 1, N_on=False, S_on=False)
            iteration(B, N_on=False, S_on=False, C_on=False)
            iteration(B + 1, N_on=False, S_on=False, C_on=False, L_on=False)
            iteration(B + 2, N_on=False, S_on=False, C_on=False, L_on=False, R_on=False)

            act.wait_ge(Z["pad_ready"], 1)
            act.wait_ge(Z["setup_dve"], 4)
            act.wait_ge(Z["g_base"], 1)
            with act.Fori(E // 2, E) as e:
                end = act.value_load(base_i[0:1, bass.ds(e, 1)], min_val=0, max_val=E * REGION - P)
                act.dma_start(sorted_x[bass.ds(end, P), :], pad[:]).then_inc(Z["pad_sent"], 16)

            def expert(j):
                return act.value_load(tile_e_i[0:1, bass.ds(j, 1)], min_val=0, max_val=E - 1)

            def tile_copy(j):
                act.wait_ge(Z["f_xT"], j + 1)
                if not (isinstance(j, int) and j == 0):
                    act.wait_ge(Z["f_h"], 2 * j)
                copy(xsT[:], xsT_ps).then_inc(Z["f_xsT"], 1)
                copy(w1_now[:, 1, :], w1[:, expert(j), 1, :]).then_inc(Z["f_w_act"], 1)

            def gelu(j, odd):
                e = expert(j)
                if not (isinstance(j, int) and j == 0):
                    act.wait_ge(Z["f_gelu"], 2 * j)
                copy(b1_now[:], b1[:, e, :]).then_inc(Z["f_b1"], 1)
                act.wait_ge(Z["f_b1"], j + 1)
                if not (isinstance(j, int) and j == 0):
                    act.wait_ge(Z["f_y"], j)
                for n in range(2):
                    act.wait_ge(Z["f_h"], 2 * j + n + 1)
                    for k in range(4 * n, 4 * n + 4):
                        g = act.activation(hidT[:, k, :], hT_ps[odd][:, k, :], ACT.Gelu, bias=b1_now[:, k:k + 1])
                    g.then_inc(Z["f_gelu"], 1)

            act.wait_ge(Z["g_table"], 1)
            act.wait_ge(Z["ld_late"], 32)
            act.wait_ge(Z["ld_early"], 16 * PIECES)
            act.wait_ge(Z["ld_bias"], 48)
            tile_copy(0)
            tile_copy(1)
            gelu(0, 0)
            with act.Fori(1, TILES - 2, 2) as j:
                tile_copy(j + 1)
                gelu(j, 1)
                tile_copy(j + 2)
                gelu(j + 1, 0)
            tile_copy(TILES - 1)
            gelu(TILES - 2, 1)
            gelu(TILES - 1, 0)

        @block.vector
        def _(dve):
            def norm_stats(b, n):
                bn, st = (("dve_bn1", "dve_st1"), ("dve_bn2", "dve_st2"), ("dve_bn3", "dve_st3"))[n]
                plain(dve)
                dve.bn_stats(stats[:, n, :], x[:, b, :]).then_inc(Z[bn], 1)
                dve.wait_ge(Z[bn], b + 1)
                plain(dve)
                dve.bn_aggr(mv[:, n, :], stats[:, n, :]).then_inc(Z[st], 1)

            def norm_apply(b, n, dst, done):
                dve.wait_ge(Z[("pool_r1", "pool_r2", "pool_r3")[n]], b + 1)
                dve.tensor_scalar(dst[:], x[:, b, :], mv[:, n, 0:1], rs[:, n, 1:2], ALU.subtract, ALU.mult)\
                   .then_inc(Z[done], 1)

            def stats1(b):
                dve.wait_ge(Z["ld_x"], 16 * (b + 1))
                norm_stats(b, 0)

            def apply1(b):
                dve.wait_ge(Z["pe_xT"], b)
                norm_apply(b, 0, xn, "dve_xn1")

            def stats2(b):
                dve.wait_ge(Z["dve_x1"], b + 1)
                norm_stats(b, 1)

            def apply2(b):
                dve.wait_ge(Z["pe_x2T"], b)
                norm_apply(b, 1, xn2, "dve_xn2")

            def stats3(b):
                dve.wait_ge(Z["dve_x2"], b + 1)
                norm_stats(b, 2)

            def apply3(b):
                dve.wait_ge(Z["pe_x3T"], b)
                norm_apply(b, 2, xn3, "dve_x3")
                dve.tensor_copy(mean_rstd3[:, b, 0:1], mv[:, 2, 0:1])
                dve.tensor_copy(mean_rstd3[:, b, 1:2], rs[:, 2, 1:2]).then_inc(Z["dve_keep3"], 1)

            def q_expand(b, c):
                dve.wait_ge(Z["act_kT"], b + 1)
                dve.wait_ge(Z["pe_sexp"], KC * b)
                dve.tensor_tensor(qexp[c], qk_ps[:, c, :].unsqueeze(1).to_broadcast([P, HC, T]),
                                  head_of.unsqueeze(2).to_broadcast([P, HC, T]), ALU.mult)\
                   .then_inc(Z["dve_qexp"], 1)

            def q_rope(b):
                dve.wait_ge(Z["pe_q"], b + 1)
                if not (isinstance(b, int) and b == 0):
                    dve.wait_ge(Z["pe_qT"], b)
                q4 = q_ps.rearrange("p (g d) -> p g d", g=G)
                a4 = ropea[:].rearrange("p (g d) -> p g d", g=G)
                r4 = ropeb[:].rearrange("p (g d) -> p g d", g=G)
                hf = GD // 2
                dve.tensor_tensor(a4, q4, ropeq[:, 0:GD].unsqueeze(1).to_broadcast([T, G, GD]), ALU.mult)\
                   .then_inc(Z["c_rope"], 1)
                dve.tensor_tensor(r4[:, :, 0:hf], q4[:, :, hf:GD],
                                  ropeq[:, GD:GD + hf].unsqueeze(1).to_broadcast([T, G, hf]), ALU.mult)\
                   .then_inc(Z["c_rope"], 1)
                dve.tensor_tensor(r4[:, :, hf:GD], q4[:, :, 0:hf],
                                  ropeq[:, GD + hf:2 * GD].unsqueeze(1).to_broadcast([T, G, hf]), ALU.mult)\
                   .then_inc(Z["c_rope"], 1)
                dve.wait_ge(Z["c_rope"], 3 * (b + 1))
                dve.tensor_tensor(qrot[:], ropea[:], ropeb[:], ALU.add).then_inc(Z["dve_rope"], 1)

            def self_max(b, c):
                dve.wait_ge(Z["pe_smax"], KC * b + c + 1)
                dve.wait_ge(Z["pool_D"], KC * b)
                dve.tensor_reduce(nm[:, HC * c:HC * c + HC].rearrange("p (a h) -> p a h", a=2),
                                  U[c][0:T, :, 0:4 * T].rearrange("p a (h t) -> p a h t", t=T), AX.X, ALU.max,
                                  negate=True).then_inc(Z["dve_smax"], 1)

            def cross_max(b):
                dve.wait_ge(Z["pool_Dx"], b)
                for u in range(2):
                    dve.wait_ge(Z["pe_xmax"], 2 * b + u + 1)
                    dve.tensor_reduce(nmx[:, 2 * u:2 * u + 2], U[u][0:T, :, 0:S], AX.X, ALU.max, negate=True)\
                       .then_inc(Z["dve_xmax"], 1)

            def self_out(b):
                dve.wait_ge(Z["pe_pvT"], b + 1)
                dve.reciprocal(den[:].unsqueeze(2), pv_ps[:, :, HD:HD + 1]).then_inc(Z["c_x1"], 1)
                dve.wait_ge(Z["c_x1"], 2 * b + 1)
                dve.tensor_tensor(tmp1[:].rearrange("p (h d) -> p h d", h=H), pv_ps[:, :, 0:HD],
                                  den[:].unsqueeze(2).to_broadcast([T, H, HD]), ALU.mult).then_inc(Z["c_x1"], 1)
                dve.wait_ge(Z["c_x1"], 2 * b + 2)
                dve.tensor_tensor(x[:, b, :], x[:, b, :], tmp1[:], ALU.add).then_inc(Z["dve_x1"], 1)

            def cross_enc(b):
                dve.wait_ge(Z["pe_pvx"], b + 1)
                dve.reciprocal(denx[:].unsqueeze(2), pvx_ps[:, :, GD:R]).then_inc(Z["c_enc"], 1)
                dve.wait_ge(Z["c_enc"], b + 1)
                dve.wait_ge(Z["pe_encT"], b)
                dve.tensor_tensor(enc[:].rearrange("p (g d) -> p g d", g=G), pvx_ps[:, :, 0:GD],
                                  denx[:].unsqueeze(2).to_broadcast([T, G, GD]), ALU.mult).then_inc(Z["dve_enc"], 1)

            def gate_max(b):
                dve.wait_ge(Z["pe_logit"], b + 1)
                dve.tensor_copy(logits[:], logit_ps).then_inc(Z["dve_logit"], 1)
                dve.wait_ge(Z["dve_logit"], b + 1)
                dve.tensor_reduce(gmax[:], logits[:], AX.X, ALU.max).then_inc(Z["gate_max"], 1)

            def gate_diff(b):
                dve.wait_ge(Z["gate_max"], b + 1)
                dve.tensor_scalar(gdiff[:], logits[:], gmax[:, 0:1], None, ALU.subtract).then_inc(Z["gate_diff"], 1)

            def gate_pick(b):
                dve.wait_ge(Z["gate_diff"], b + 1)
                dve.scalar_tensor_tensor(cand[:], gdiff[:], 0.0, misc[0:T, 8:16], ALU.is_ge, ALU.mult)\
                   .then_inc(Z["gate_cand"], 1)
                dve.wait_ge(Z["gate_cand"], b + 1)
                dve.tensor_reduce(best[:], cand[:], AX.X, ALU.min).then_inc(Z["gate_best"], 1)
                dve.wait_ge(Z["gate_best"], b + 1)
                dve.tensor_scalar(onehot[:], misc[0:T, 8:16], best[:, 0:1], None, ALU.is_equal)\
                   .then_inc(Z["gate_onehot"], 1)

            def gate_place(b):
                dve.wait_ge(Z["pe_count"], b + 1)
                if not isinstance(b, int) or b > 0:
                    dve.wait_ge(Z["dve_place"], b)
                dve.tensor_tensor(place[:], count_ps[:, 0, :], base[:], ALU.add).then_inc(Z["c_place"], 1)
                dve.tensor_tensor(base[:], count_ps[:, 1, :], base[:], ALU.add).then_inc(Z["dve_place"], 1)
                dve.wait_ge(Z["c_place"], 3 * b + 1)
                dve.tensor_tensor(place[:], place[:], onehot[:], ALU.mult).then_inc(Z["c_place"], 1)
                if not isinstance(b, int) or b > 0:
                    dve.wait_ge(Z["row_sent"], 16 * b)
                dve.tensor_scalar(row[:, 0:D], x[:, b, :], mean_rstd3[:, b, 0:1], mean_rstd3[:, b, 1:2],
                                  ALU.subtract, ALU.mult)
                dve.wait_ge(Z["c_place"], 3 * b + 2)
                dve.tensor_reduce(slot[:], place[:], AX.X, ALU.add).then_inc(Z["c_place"], 1)
                dve.wait_ge(Z["act_gate"], b + 1)
                dve.reciprocal(row[:, 2 * D:2 * D + 1], gsum[:])
                dve.tensor_copy(row[:, 2 * D + 1:ROW].bitcast(I32), token[0:T, bass.ds(b, 1)])
                dve.wait_ge(Z["c_place"], 3 * b + 3)
                dve.tensor_copy(slot_i[:], slot[:]).then_inc(Z["row_dve"], 1)

            def k_rope(b):
                dve.wait_ge(Z["act_kraw"], b + 1)
                hf = GD // 2
                dve.tensor_tensor(kra[:], kraw[:], ropek[:, :, 0:GD], ALU.mult).then_inc(Z["c_krope"], 1)
                dve.tensor_tensor(krb[:, :, 0:hf], kraw[:, :, hf:GD], ropek[:, :, GD:GD + hf], ALU.mult)\
                   .then_inc(Z["c_krope"], 1)
                dve.tensor_tensor(krb[:, :, hf:GD], kraw[:, :, 0:hf], ropek[:, :, GD + hf:2 * GD], ALU.mult)\
                   .then_inc(Z["c_krope"], 1)
                dve.wait_ge(Z["c_krope"], 3 * b + 3)
                dve.wait_ge(Z["pe_kT"], b)
                dve.tensor_tensor(krot[:], kra[:], krb[:], ALU.add).then_inc(Z["dve_krope"], 1)

            def cross_out(b):
                dve.wait_ge(Z["pe_out"], b + 1)
                dve.tensor_tensor(x[:, b, :], out_ps, x[:, b, :], ALU.add).then_inc(Z["dve_x2"], 1)

            def iteration(i, N_on=True, S_on=True, C_on=True, L_on=True, R_on=True, Q_on=True):
                N, S, C, L, R, Q = i + 2, i + 1, i, i - 1, i - 2, i - 3
                if L_on:
                    cross_max(L)
                if Q_on:
                    gate_place(Q)
                if N_on:
                    stats1(N)
                if C_on:
                    self_out(C)
                    stats2(C)
                if S_on:
                    q_expand(S, 0)
                if C_on:
                    apply2(C)
                if S_on:
                    q_expand(S, 1)
                if C_on:
                    k_rope(C)
                if S_on:
                    self_max(S, 0)
                if C_on:
                    q_rope(C)
                if L_on:
                    cross_enc(L)
                if S_on:
                    self_max(S, 1)
                if N_on:
                    apply1(N)
                if L_on:
                    cross_out(L)
                    stats3(L)
                if R_on:
                    gate_max(R)
                    gate_diff(R)
                    gate_pick(R)
                if L_on:
                    apply3(L)

            step = [0]

            def link(ins):
                step[0] += 1
                ins.then_inc(Z["c_setup"], 1)
                dve.wait_ge(Z["c_setup"], step[0])

            dve.memset(ones[:], 1.0)
            link(dve.memset(v1_flat, 0.0))
            for g in range(PG):
                heads = min(H - PH * g, PH)
                dve.memset(v_places(g, heads, HD + 1)[:, :, HD:HD + 1], 1.0)
            dve.memset(vx[:, :, GD:R], 1.0)
            dve.memset(neghalf[:], -0.5)
            dve.memset(ones_f[:], 1.0)
            dve.memset(qxT[GD:R, :], 1.0).then_inc(Z["ones_ready"], 1)
            dve.wait_ge(Z["ld_const"], 16 * 4)
            stats1(0)
            apply1(0)
            iteration(-1, C_on=False, L_on=False, R_on=False, Q_on=False)
            dve.wait_ge(Z["ld_w"], 16 * 9)
            link(dve.tensor_scalar(small[:, 2:4], small[:, 0:2], 1.0, None, ALU.add))
            for c in range(KC):
                dve.tensor_scalar(wxq[:, c, :], wxq[:, c, :], small[:, 2 + c:3 + c], None, ALU.mult)
                dve.tensor_scalar(wkv[:, c, :], wkv[:, c, :], small[:, 2 + c:3 + c], None, ALU.mult)
            link(dve.tensor_tensor(small[0:E, 48:64], small[0:E, 16:32], small[0:E, 16:32], ALU.mult))
            link(dve.tensor_reduce(small[0:E, 5:6], small[0:E, 48:64], AX.X, ALU.add))
            dve.tensor_copy(small[0:E, 6:7], small[0:E, 5:6]).then_inc(Z["setup_norm"], 1)
            dve.wait_ge(Z["setup_pool"], 1)
            link(dve.tensor_scalar(small[0:E, 8:9], small[0:E, 7:8], 0.0001, None, ALU.max))
            link(dve.reciprocal(small[0:E, 9:10], small[0:E, 8:9]))
            dve.tensor_scalar(small[0:E, 32:48], small[0:E, 16:32], small[0:E, 9:10], None, ALU.mult)\
               .then_inc(Z["weights_ready"], 1)
            dve.wait_ge(Z["setup_pe"], 1)
            dve.tensor_copy(wgT[:], b7[0:HD, 0:E]).then_inc(Z["setup_dve"], 1)
            dve.tensor_copy(tri[:], misc[0:T, 124:124 + T]).then_inc(Z["setup_dve"], 1)
            dve.tensor_copy(base[:], misc[0:T, 44:52]).then_inc(Z["setup_dve"], 1)
            dve.tensor_copy(pad[:, 2 * D + 1:ROW].bitcast(I32), token[:, B:B + 1]).then_inc(Z["setup_dve"], 1)

            def bias(n):
                dve.wait_ge(Z["ld_bias"], 48)
                if n > 0:
                    dve.wait_ge(Z["c_bias"], n)
                if n == 0:
                    done = dve.tensor_copy(b3[:, 0, :], braw2)
                elif n == 1:
                    done = dve.tensor_tensor(braw3, braw2, b3[:, 0, :], ALU.subtract)
                elif n == 2:
                    done = dve.tensor_copy(b3[:, 1, :], braw3)
                elif n == 3:
                    done = dve.tensor_tensor(braw2, braw3, b3[:, 1, :], ALU.subtract)
                else:
                    done = dve.tensor_copy(b3[:, 2, :], braw2)
                done.then_inc(Z["c_bias"], 1)

            iteration(0, L_on=False, R_on=False, Q_on=False)
            bias(0)
            bias(1)
            iteration(1, R_on=False, Q_on=False)
            bias(2)
            bias(3)
            iteration(2, Q_on=False)
            bias(4)
            dve.tensor_copy(pick[:].rearrange("p e n -> p (e n)"), pick_f).then_inc(Z["pick_ready"], 1)
            iteration(3)
            with dve.Fori(4, B - 2) as i:
                iteration(i)
            iteration(B - 2, N_on=False)
            iteration(B - 1, N_on=False, S_on=False)
            iteration(B, N_on=False, S_on=False, C_on=False)
            iteration(B + 1, N_on=False, S_on=False, C_on=False, L_on=False)
            iteration(B + 2, N_on=False, S_on=False, C_on=False, L_on=False, R_on=False)

            step[0] = 0

            def then(ins):
                step[0] += 1
                ins.then_inc(Z["c_table"], 1)
                dve.wait_ge(Z["c_table"], step[0])

            dve.wait_ge(Z["dve_place"], B)
            dve.tensor_copy(base_i[:], base[0:1, :]).then_inc(Z["g_base"], 1)
            then(dve.tensor_tensor(count[:], base[0:1, :], misc[0:1, 44:52], ALU.subtract))
            then(dve.tensor_tensor(over_t[:], count[:].unsqueeze(2).to_broadcast([1, E, 28]),
                                   misc[0:1, 16:44].unsqueeze(1).to_broadcast([1, E, 28]), ALU.is_gt))
            then(dve.tensor_reduce(tiles_e[:], over_t[:], AX.X, ALU.add))
            dve.tensor_tensor_scan(ends[:], ones_f[0:1, :], tiles_e[:], 0.0, ALU.mult, ALU.add)
            then(dve.tensor_scalar(skip[:], tiles_e[:], -float(P), float(REGION), ALU.mult, ALU.add))
            then(dve.tensor_tensor(past[:], misc[0:1, 52:88].unsqueeze(2).to_broadcast([1, 36, E]),
                                   ends[:].unsqueeze(1).to_broadcast([1, 36, E]), ALU.is_ge))
            then(dve.tensor_reduce(tile_e[:], past[:], AX.X, ALU.add))
            then(dve.tensor_tensor(past[:], past[:], skip[:].unsqueeze(1).to_broadcast([1, 36, E]), ALU.mult))
            then(dve.tensor_reduce(tile_row[:], past[:], AX.X, ALU.add))
            then(dve.tensor_tensor(tile_row[:], tile_row[:], misc[0:1, 88:124], ALU.add))
            dve.tensor_scalar(tile_e_i[:], tile_e[:], float(E - 1), None, ALU.min)
            dve.tensor_scalar(tile_row_i[:], tile_row[:], float(E * REGION), None, ALU.min)\
               .then_inc(Z["g_table"], 1)

            def w1_copy(j):
                e = dve.value_load(tile_e_i[0:1, bass.ds(j, 1)], min_val=0, max_val=E - 1)
                if not (isinstance(j, int) and j == 0):
                    dve.wait_ge(Z["f_h"], 2 * j)
                dve.tensor_copy(w1_now[:, 0, :], w1[:, e, 0, :]).then_inc(Z["f_w_dve"], 1)

            def finish(j):
                dve.wait_ge(Z["f_y"], j + 1)
                dve.wait_ge(Z["f_xr"], 16 * (j + 1))
                if not (isinstance(j, int) and j == 0):
                    dve.wait_ge(Z["f_sent"], 16 * j)
                dve.scalar_tensor_tensor(out_row[:], y_ps, xr[:, D:D + 1], xr[:, 0:D], ALU.mult, ALU.add)
                dve.tensor_copy(out_token[:], xr[:, D + 1:D + 2].bitcast(I32)).then_inc(Z["f_out"], 1)

            dve.wait_ge(Z["g_table"], 1)
            dve.wait_ge(Z["ld_late"], 32)
            dve.wait_ge(Z["ld_early"], 16 * PIECES)
            w1_copy(0)
            w1_copy(1)
            w1_copy(2)
            finish(0)
            with dve.Fori(1, TILES - 2) as j:
                w1_copy(j + 2)
                finish(j)
            finish(TILES - 2)
            finish(TILES - 1)

        @block.gpsimd
        def _(pool):
            pool.memset(pad[:, 0:2 * D + 1], 0.0).then_inc(Z["pad_ready"], 1)
            pool.memset(bias_rows[:], 0.0).then_inc(Z["zero_ready"], 1)

            def power(b, n, mult, add, v, r):
                pool.wait_ge(Z[("dve_st1", "dve_st2", "dve_st3")[n]], b + 1)
                pool.wait_ge(Z[("dve_xn1", "dve_xn2", "dve_keep3")[n]], b)
                plain(pool)
                pool.tensor_scalar(rs[:, n, 0:1], mv[:, n, 1:2], mult, add, ALU.mult, ALU.add).then_inc(Z[v], 1)
                pool.wait_ge(Z[v], b + 1)
                pool.tensor_tensor(rs[:, n, 1:2], rs[:, n, 0:1], neghalf[0:T, 0:1], ALU.pow).then_inc(Z[r], 1)

            def rstd1(b):
                power(b, 0, 1.0, 1e-5, "pool_v1", "pool_r1")

            def rstd2(b):
                power(b, 1, 1.0 + 1e-6, 1e-11, "pool_v2", "pool_r2")

            def rstd3(b):
                power(b, 2, 1.0, 1e-5, "pool_v3", "pool_r3")

            def rstd_ctx(b):
                pool.wait_ge(Z["act_sq"], KT * (b + 1))
                pool.wait_ge(Z["act_vx"], b)
                plain(pool)
                pool.tensor_scalar(ssm[:], ss[:], 1.0 / D, 1e-6, ALU.mult, ALU.add).then_inc(Z["pool_vc"], 1)
                pool.wait_ge(Z["pool_vc"], b + 1)
                pool.tensor_tensor(rc[:], ssm[:], neghalf[0:KP, 0:KT], ALU.pow).then_inc(Z["pool_rc"], 1)

            def diag(b):
                pool.wait_ge(Z["pe_sexp"], KC * b)
                for c in range(KC):
                    pool.wait_ge(Z["dve_smax"], KC * b + c + 1)
                    plain(pool)
                    pool.affine_select(neg_diag[:, HC * c:HC * c + HC, :],
                                       nm[:, HC * c:HC * c + HC].unsqueeze(2).to_broadcast([T, HC, T]),
                                       [[0, HC], [1, T]], ALU.is_equal, 0.0, base=0, channel_multiplier=-1)\
                        .then_inc(Z["pool_D"], 1)

            def diagx(b):
                pool.wait_ge(Z["pe_xexp"], KT * b)
                pool.wait_ge(Z["dve_xmax"], 2 * (b + 1))
                plain(pool)
                pool.affine_select(neg_diagx.rearrange("p (g t) -> p g t", g=G),
                                   nmx[:].unsqueeze(2).to_broadcast([T, G, T]),
                                   [[0, G], [1, T]], ALU.is_equal, 0.0, base=0, channel_multiplier=-1)\
                    .then_inc(Z["pool_Dx"], 1)

            def scatter(b):
                pool.wait_ge(Z["row_dve"], b + 1)
                pool.wait_ge(Z["row_act"], b + 1)
                plain(pool)
                pool.indirect_dma_start(out=sorted_x,
                                        out_offset=bass.IndirectOffsetOnAxis(ap=slot_i[:, 0:1], axis=0),
                                        in_=row[:], in_offset=None).then_inc(Z["row_sent"], 16)

            def iteration(i, N_on=True, S_on=True, C_on=True, L_on=True, Q_on=True):
                N, S, C, L, Q = i + 2, i + 1, i, i - 1, i - 3
                if L_on:
                    diagx(L)
                if Q_on:
                    scatter(Q)
                if N_on:
                    rstd1(N)
                if C_on:
                    rstd2(C)
                if S_on:
                    diag(S)
                    rstd_ctx(C + 1)
                if L_on:
                    rstd3(L)

            pool.wait_ge(Z["ones_ready"], 1)
            rstd1(0)
            iteration(-1, C_on=False, L_on=False, Q_on=False)
            pool.wait_ge(Z["setup_norm"], 1)
            pool.tensor_scalar(small[0:E, 10:11], neghalf[0:E, 0:1], -1.0, None, ALU.mult).then_inc(Z["c_pool"], 1)
            pool.wait_ge(Z["c_pool"], 1)
            pool.tensor_tensor(small[0:E, 7:8], small[0:E, 6:7], small[0:E, 10:11], ALU.pow)\
                .then_inc(Z["setup_pool"], 1)

            iteration(0, L_on=False, Q_on=False)
            iteration(1, Q_on=False)
            iteration(2, Q_on=False)
            pool.wait_ge(Z["c_bias"], 5)
            pool.wait_ge(Z["zero_ready"], 1)
            for part in range(3):
                pool.dma_start(bias_rows[part:3 * E:3, :], b3[:, part, :]).then_inc(Z["bias_sent"], 16)
            iteration(3)
            with pool.Fori(4, B - 2) as i:
                iteration(i)
            iteration(B - 2, N_on=False)
            iteration(B - 1, N_on=False, S_on=False)
            iteration(B, N_on=False, S_on=False, C_on=False)
            iteration(B + 1, N_on=False, S_on=False, C_on=False, L_on=False)
            iteration(B + 2, N_on=False, S_on=False, C_on=False, L_on=False)

            out_rows = out.rearrange("b t d -> (b t) d")

            def rest_load(j):
                at = pool.value_load(tile_row_i[0:1, bass.ds(j, 1)], min_val=0, max_val=E * REGION)
                pool.dma_start(xr[:], sorted_x[bass.ds(at, P), D:ROW]).then_inc(Z["f_xr"], 16)

            def send(j):
                pool.wait_ge(Z["f_out"], j + 1)
                plain(pool)
                pool.indirect_dma_start(out=out_rows,
                                        out_offset=bass.IndirectOffsetOnAxis(ap=out_token[:, 0:1], axis=0),
                                        in_=out_row[:], in_offset=None,
                                        bounds_check=B * T - 1, oob_is_err=False).then_inc(Z["f_sent"], 16)

            pool.wait_ge(Z["g_table"], 1)
            pool.wait_ge(Z["pad_sent"], 16 * (E + 1))
            pool.wait_ge(Z["row_sent"], 16 * B)
            rest_load(0)
            send(0)
            rest_load(1)
            with pool.Fori(1, TILES - 1) as j:
                send(j)
                rest_load(j + 1)
            send(TILES - 1)
            pool.wait_ge(Z["f_sent"], 16 * TILES)


def kernel(**inputs):
    import numpy as _np
    import concourse.bacc as _bacc
    from concourse import mybir as _mybir
    from concourse.bass_utils import run_bass_kernel_spmd as _run

    g = {k: _np.asarray(v) for k, v in inputs.items()}

    def chunks(w):
        return _np.ascontiguousarray(w.reshape(KC, P, -1).transpose(1, 0, 2))

    arrays = {
        "x": g["x"],
        "ctx": _np.ascontiguousarray(g["ctx_1024"].reshape(B, KT, KP, D).transpose(0, 2, 1, 3)),
        "ctxT": _np.ascontiguousarray(g["ctx_1024"].transpose(0, 2, 1).reshape(B, KC, P, S).transpose(0, 2, 1, 3)),
        "mask": g["mask_BxS2_bk0"].reshape(B, 1, S),
        "wqk": chunks(_np.concatenate([g["L0_attn_Wq"].T, g["L0_attn_Wk"].T], 1)),
        "wv": chunks(g["L0_attn_Wv"].T),
        "rms": _np.ascontiguousarray(g["L0_xattn_rms_scale"].reshape(KC, P).T),
        "wxq": chunks(g["L0_xattn_q_w"].transpose(1, 0, 2).reshape(D, G * GD)),
        "wkv": chunks(_np.concatenate([g["L0_xattn_kv_w"][0, 0], g["L0_xattn_kv_w"][1, 0]], 1)),
        "wo": chunks(g["L0_xattn_out_w"].reshape(G * GD, D)),
        "wred": chunks(g["L0_ffn_w_red"]),
        "wg": g["L0_ffn_wg"],
        "w": _np.ascontiguousarray(_np.concatenate(
            [g["L0_ffn_w1"].reshape(E, KC, P, F).transpose(2, 0, 1, 3).reshape(P, E, KC * F),
             g["L0_ffn_w2"].reshape(E, FC, P, D).transpose(2, 0, 1, 3).reshape(P, E, FC * D)], 2)).reshape(P, E * WE),
        "b1": _np.ascontiguousarray(g["L0_ffn_b1"].reshape(E, FC, P).transpose(2, 0, 1)),
        "b2": g["L0_ffn_b2"],
    }
    consts = constants()
    consts["pick"] = consts["pick"].reshape(P, E * P)
    arrays.update(consts)
    nc = _bacc.Bacc("TRN2", target_bir_lowering=False, num_devices=1)
    feed, aps = {}, {}
    for name, v in arrays.items():
        v = _np.ascontiguousarray(v)
        feed[f"in_{name}"] = v
        aps[name] = nc.dram_tensor(f"in_{name}", v.shape, _mybir.dt.from_np(v.dtype), kind="ExternalInput").ap()
    out = nc.dram_tensor("out_x", (B, T, D), F32, kind="ExternalOutput").ap()
    decoder(nc, aps, out)
    r = _run(nc, [feed], core_ids=[0])
    return r.results[0]["out_x"]
```
